# Optimizing a Trainium2 kernel written in Bass

```python
import numpy as np
import jax
import jax.numpy as jnp

def _softmax(x, axis=-1):
    return jax.nn.softmax(x, axis=axis)

def _gelu(x):
    return jax.nn.gelu(x, approximate=True)

def _silu(x):
    return jax.nn.silu(x)

def _sigmoid(x):
    return jax.nn.sigmoid(x)

def _layernorm(x, axis=-1, eps=1e-05):
    m = jnp.mean(x, axis=axis, keepdims=True)
    v = jnp.var(x, axis=axis, keepdims=True)
    return (x - m) / jnp.sqrt(v + eps)

def _scatter_add(tgt, idx, src, axis=0):
    return tgt.at[idx].add(src)

def _segment_sum(src, seg, n):
    return jax.ops.segment_sum(src, seg, n)
kernel_name = 'mk_prb_d2_jaxref_r8_865e07'

def setup_inputs(seed: int=0):
    np.random.seed(seed)
    _w = jnp.asarray

    def _L0_attn_setup():
        import jax, jax.numpy as jnp
        import numpy as np
        N_HEADS = 16
        EPS = 1e-06
        key = jax.random.key(seed)
        ks = jax.random.split(key, 5)
        B, N, D, H = (4, 256, 128, N_HEADS)
        x = jax.random.normal(ks[0], (B, N, D), dtype=jnp.float32)
        Wq = jax.random.normal(ks[1], (D, D), dtype=jnp.float32) * D ** (-0.5)
        Wk = jax.random.normal(ks[2], (D, D), dtype=jnp.float32) * D ** (-0.5)
        Wv = jax.random.normal(ks[3], (D, D), dtype=jnp.float32) * D ** (-0.5)
        Wo = jax.random.normal(ks[4], (D, D), dtype=jnp.float32) * D ** (-0.5)
        q_scale = jnp.ones((H,), dtype=jnp.float32)
        k_scale = jnp.ones((H,), dtype=jnp.float32)
        return {'x': x, 'Wq': Wq, 'Wk': Wk, 'Wv': Wv, 'Wo': Wo, 'q_scale': q_scale, 'k_scale': k_scale}
    _L0_attn_in = _L0_attn_setup()

    def _L0_ffn_setup():
        import jax, jax.numpy as jnp
        import numpy as np
        NEG_INF = -1e+30

        def _moe_forward(x, router_w, router_b, w1, b1, w2, b2, top_k=2):
            B, S, D = x.shape
            E = router_w.shape[1]
            logits = jnp.einsum('bsd,de->bse', x, router_w) + router_b
            top_vals, top_idx = jax.lax.top_k(logits, top_k)
            keep = jax.nn.one_hot(top_idx, E, dtype=logits.dtype).sum(-2) > 0
            sparse_logits = jnp.where(keep, logits, NEG_INF)
            gating = jax.nn.softmax(sparse_logits, axis=-1)
            xf = x.reshape(-1, D)
            gf = gating.reshape(-1, E)
            h = jax.nn.relu(jnp.einsum('td,edh->eth', xf, w1) + b1[:, None, :])
            y = jnp.einsum('eth,ehd->etd', h, w2) + b2[:, None, :]
            out = jnp.einsum('etd,te->td', y, gf)
            return out.reshape(B, S, D)
        key = jax.random.key(seed)
        ks = jax.random.split(key, 5)
        B, S, D, E, H = (2, 256, 128, 8, 512)
        scale = 0.02
        return {'x': jax.random.normal(ks[0], (B, S, D), dtype=jnp.float32), 'router_w': jax.random.normal(ks[1], (D, E), dtype=jnp.float32) * scale, 'router_b': jnp.zeros((E,), dtype=jnp.float32), 'w1': jax.random.normal(ks[2], (E, D, H), dtype=jnp.float32) * scale, 'b1': jnp.zeros((E, H), dtype=jnp.float32), 'w2': jax.random.normal(ks[3], (E, H, D), dtype=jnp.float32) * scale, 'b2': jnp.zeros((E, D), dtype=jnp.float32)}
    _L0_ffn_in = _L0_ffn_setup()

    def _L1_attn_setup():
        import jax, jax.numpy as jnp
        import numpy as np
        D = 128
        E = 2 * D
        S = 128
        LN_EPS = 1e-05
        key = jax.random.key(seed)
        ks = jax.random.split(key, 4)
        bs, seq_len = (4, 256)
        x = jax.random.normal(ks[0], (bs, seq_len, D), dtype=jnp.float32)
        W_in = jax.random.normal(ks[1], (D, 2 * E + S), dtype=jnp.float32) / np.sqrt(D)
        b_in = jnp.zeros((2 * E + S,), dtype=jnp.float32)
        W_out = jax.random.normal(ks[2], (E, D), dtype=jnp.float32) / np.sqrt(E)
        b_out = jnp.zeros((D,), dtype=jnp.float32)
        ln_g = jnp.ones((D,), dtype=jnp.float32)
        ln_b = jnp.zeros((D,), dtype=jnp.float32)
        gamma_q = jnp.ones((S,), dtype=jnp.float32)
        beta_q = jnp.zeros((S,), dtype=jnp.float32)
        gamma_k = jnp.ones((S,), dtype=jnp.float32)
        beta_k = jnp.zeros((S,), dtype=jnp.float32)
        return {'x': x, 'ln_g': ln_g, 'ln_b': ln_b, 'W_in': W_in, 'b_in': b_in, 'W_out': W_out, 'b_out': b_out, 'gamma_q': gamma_q, 'beta_q': beta_q, 'gamma_k': gamma_k, 'beta_k': beta_k}
    _L1_attn_in = _L1_attn_setup()

    def _L1_ffn_setup():
        import jax, jax.numpy as jnp
        import numpy as np
        B, M, D = (4, 256, 128)
        N, P = (64, 32)
        key = jax.random.key(seed)
        k1, k2, k3, k4 = jax.random.split(key, 4)
        x = jax.random.normal(k1, (B, M, D), dtype=jnp.float32)
        phi = jax.random.normal(k2, (D, N, P), dtype=jnp.float32) * (1.0 / np.sqrt(D))
        W = jax.random.normal(k3, (N, D, D), dtype=jnp.float32) * (1.0 / np.sqrt(D))
        b = jax.random.normal(k4, (N, D), dtype=jnp.float32) * 0.01
        return {'x': x, 'phi': phi, 'W': W, 'b': b}
    _L1_ffn_in = _L1_ffn_setup()
    _d = {'L0_attn_x': _L0_attn_in['x'], 'L0_attn_Wq': _L0_attn_in['Wq'], 'L0_attn_Wk': _L0_attn_in['Wk'], 'L0_attn_Wv': _L0_attn_in['Wv'], 'L0_attn_Wo': _L0_attn_in['Wo'], 'L0_attn_q_scale': _L0_attn_in['q_scale'], 'L0_attn_k_scale': _L0_attn_in['k_scale'], 'L0_ffn_router_w': _L0_ffn_in['router_w'], 'L0_ffn_router_b': _L0_ffn_in['router_b'], 'L0_ffn_w1': _L0_ffn_in['w1'], 'L0_ffn_b1': _L0_ffn_in['b1'], 'L0_ffn_w2': _L0_ffn_in['w2'], 'L0_ffn_b2': _L0_ffn_in['b2'], 'L1_attn_ln_g': _L1_attn_in['ln_g'], 'L1_attn_ln_b': _L1_attn_in['ln_b'], 'L1_attn_W_in': _L1_attn_in['W_in'], 'L1_attn_b_in': _L1_attn_in['b_in'], 'L1_attn_W_out': _L1_attn_in['W_out'], 'L1_attn_b_out': _L1_attn_in['b_out'], 'L1_attn_gamma_q': _L1_attn_in['gamma_q'], 'L1_attn_beta_q': _L1_attn_in['beta_q'], 'L1_attn_gamma_k': _L1_attn_in['gamma_k'], 'L1_attn_beta_k': _L1_attn_in['beta_k'], 'L1_ffn_phi': _L1_ffn_in['phi'], 'L1_ffn_W': _L1_ffn_in['W'], 'L1_ffn_b': _L1_ffn_in['b']}
    _x0 = _d['L0_attn_x']
    _d['L0_attn_x'] = jax.random.normal(jax.random.fold_in(jax.random.key(seed), 1), (4, 1024, 128), dtype=_x0.dtype)
    del _x0
    return _d

def reference(L0_attn_x, L0_attn_Wq, L0_attn_Wk, L0_attn_Wv, L0_attn_Wo, L0_attn_q_scale, L0_attn_k_scale, L0_ffn_router_w, L0_ffn_router_b, L0_ffn_w1, L0_ffn_b1, L0_ffn_w2, L0_ffn_b2, L1_attn_ln_g, L1_attn_ln_b, L1_attn_W_in, L1_attn_b_in, L1_attn_W_out, L1_attn_b_out, L1_attn_gamma_q, L1_attn_beta_q, L1_attn_gamma_k, L1_attn_beta_k, L1_ffn_phi, L1_ffn_W, L1_ffn_b):

    def _L0_attn_ref(x, Wq, Wk, Wv, Wo, q_scale, k_scale):
        import jax, jax.numpy as jnp
        import numpy as np
        N_HEADS = 16
        EPS = 1e-06
        B, N, D = x.shape
        H = N_HEADS
        hd = D // H
        q = jax.nn.silu(x @ Wq.T)
        k = jax.nn.silu(x @ Wk.T)
        v = jax.nn.silu(x @ Wv.T)
        q = q.reshape(B, N, H, hd).transpose(0, 2, 1, 3)
        k = k.reshape(B, N, H, hd).transpose(0, 2, 1, 3)
        v = v.reshape(B, N, H, hd).transpose(0, 2, 1, 3)
        r_q = jnp.linalg.norm(q, axis=-1, keepdims=True)
        r_k = jnp.linalg.norm(k, axis=-1, keepdims=True)
        q_dir = q / (r_q + EPS)
        k_dir = k / (r_k + EPS)
        scores = jnp.einsum('bhnd,bhmd->bhnm', q_dir, k_dir)
        sq = q_scale[None, :, None, None]
        sk = k_scale[None, :, None, None]
        scores = scores * (r_q * sq) * (jnp.swapaxes(r_k, -2, -1) * sk)
        mask = jnp.tril(jnp.ones((N, N), dtype=bool))
        scores = jnp.where(mask, scores, -jnp.inf)
        probs = jax.nn.softmax(scores, axis=-1)
        out = jnp.einsum('bhnm,bhmd->bhnd', probs, v)
        out = out.transpose(0, 2, 1, 3).reshape(B, N, D)
        return out @ Wo.T

    def _L0_ffn_ref(x, router_w, router_b, w1, b1, w2, b2):
        import jax, jax.numpy as jnp
        import numpy as np
        NEG_INF = -1e+30

        def _moe_forward(x, router_w, router_b, w1, b1, w2, b2, top_k=2):
            B, S, D = x.shape
            E = router_w.shape[1]
            logits = jnp.einsum('bsd,de->bse', x, router_w) + router_b
            top_vals, top_idx = jax.lax.top_k(logits, top_k)
            keep = jax.nn.one_hot(top_idx, E, dtype=logits.dtype).sum(-2) > 0
            sparse_logits = jnp.where(keep, logits, NEG_INF)
            gating = jax.nn.softmax(sparse_logits, axis=-1)
            xf = x.reshape(-1, D)
            gf = gating.reshape(-1, E)
            h = jax.nn.relu(jnp.einsum('td,edh->eth', xf, w1) + b1[:, None, :])
            y = jnp.einsum('eth,ehd->etd', h, w2) + b2[:, None, :]
            out = jnp.einsum('etd,te->td', y, gf)
            return out.reshape(B, S, D)
        return _moe_forward(x, router_w, router_b, w1, b1, w2, b2, top_k=2)

    def _L1_attn_ref(x, ln_g, ln_b, W_in, b_in, W_out, b_out, gamma_q, beta_q, gamma_k, beta_k):
        import jax, jax.numpy as jnp
        import numpy as np
        D = 128
        E = 2 * D
        S = 128
        LN_EPS = 1e-05
        seq_len = x.shape[1]
        mu = jnp.mean(x, axis=-1, keepdims=True)
        var = jnp.mean(jnp.square(x - mu), axis=-1, keepdims=True)
        xn = (x - mu) * jax.lax.rsqrt(var + LN_EPS) * ln_g + ln_b
        uvz = jax.nn.silu(jnp.einsum('bld,df->blf', xn, W_in) + b_in)
        u, v, z = (uvz[..., :E], uvz[..., E:2 * E], uvz[..., 2 * E:])
        q = z * gamma_q + beta_q
        k = z * gamma_k + beta_k
        attn = jnp.einsum('bqs,bks->bqk', q, k) / seq_len
        attn = jnp.square(jax.nn.relu(attn))
        out = u * jnp.einsum('bqk,bke->bqe', attn, v)
        return x + jnp.einsum('ble,ed->bld', out, W_out) + b_out

    def _L1_ffn_ref(x, phi, W, b):
        import jax, jax.numpy as jnp
        import numpy as np
        B, M, D = (4, 256, 128)
        N, P = (64, 32)
        logits = jnp.einsum('bmd,dnp->bmnp', x, phi)
        dispatch = jax.nn.softmax(logits, axis=0)
        bsz, m, n, p = logits.shape
        combine = jax.nn.softmax(logits.reshape(bsz, m, n * p), axis=-1).reshape(bsz, m, n, p)
        slots = jnp.einsum('bmd,bmnp->bnpd', x, dispatch)
        y = jnp.einsum('bnpd,nde->bnpe', slots, W) + b[None, :, None, :]
        out = jnp.einsum('bnpd,bmnp->bmd', y, combine)
        return out
    x = L0_attn_x
    xn = _layernorm(x, axis=-1)
    x = x + _L0_attn_ref(xn, L0_attn_Wq, L0_attn_Wk, L0_attn_Wv, L0_attn_Wo, L0_attn_q_scale, L0_attn_k_scale) + _L0_ffn_ref(xn, L0_ffn_router_w, L0_ffn_router_b, L0_ffn_w1, L0_ffn_b1, L0_ffn_w2, L0_ffn_b2)
    xn = _layernorm(x, axis=-1)
    x = x + _L1_attn_ref(xn, L1_attn_ln_g, L1_attn_ln_b, L1_attn_W_in, L1_attn_b_in, L1_attn_W_out, L1_attn_b_out, L1_attn_gamma_q, L1_attn_beta_q, L1_attn_gamma_k, L1_attn_beta_k) + _L1_ffn_ref(xn, L1_ffn_phi, L1_ffn_W, L1_ffn_b)
    return x

_drawn_inputs = setup_inputs


def setup_inputs(seed=0):
    import zlib

    import numpy as np

    out = dict(_drawn_inputs(seed))
    spreads = {'L0_attn_q_scale': (1.0, 0.2),
     'L0_attn_k_scale': (1.0, 0.2),
     'L0_ffn_router_b': (0.0, 0.1),
     'L0_ffn_b1': (0.0, 0.1),
     'L0_ffn_b2': (0.0, 0.1),
     'L1_attn_ln_g': (1.0, 0.2),
     'L1_attn_ln_b': (0.0, 0.1),
     'L1_attn_b_in': (0.0, 0.1),
     'L1_attn_b_out': (0.0, 0.1),
     'L1_attn_gamma_q': (1.0, 0.2),
     'L1_attn_beta_q': (0.0, 0.1),
     'L1_attn_gamma_k': (1.0, 0.2),
     'L1_attn_beta_k': (0.0, 0.1)}
    factors = {}
    for name, (base, spread) in spreads.items():
        noise = np.random.default_rng([zlib.crc32(name.encode()), seed]).standard_normal(out[name].shape)
        drawn = base * np.exp(spread * noise) if base else spread * noise
        out[name] = jnp.asarray(drawn.astype(out[name].dtype))
    for name, factor in factors.items():
        out[name] = (out[name] * factor).astype(out[name].dtype)
    return out
```

```python
from contextlib import ExitStack

import concourse.bass as bass
from concourse import mybir

fp32 = mybir.dt.float32
f32r = mybir.dt.float32r
bf16 = mybir.dt.bfloat16
ALU = mybir.AluOpType
ACT = mybir.ActivationFunctionType
AX = mybir.AxisListType

P = 128
B, N, D = 4, 1024, 128
TB = N // P
TILES = B * TB
H, HD = 16, 8
HG = 4
G = H // HG
U = B * G
E, HID = 8, 512
HC = HID // P
NE, NP_ = 64, 32
SLOTS = NE * NP_
S1, E1 = 128, 256
EPS_LN, EPS_DIR = 1e-5, 1e-6
MASKED = -1e30


class Own:

    def __init__(self, eng, sem, per=0, turn=0):
        self.eng, self.sem, self.per, self.turn, self.n = eng, sem, per, turn, 0

    def mark(self, ins):
        self.n += 1
        ins.then_inc(self.sem, 1)
        return ins

    def wait(self):
        self.eng.wait_ge(self.sem, self.turn * self.per + self.n)

    def step(self, ins):
        self.mark(ins)
        self.wait()

    def end(self):
        assert self.n == self.per, self.n


def hold(eng, m):
    eng.sem_inc(m.held, 1)


def prime(eng, *semaphores):
    for s in semaphores:
        eng.sem_inc(s, 1)


def bc(ap, shape):
    return ap.to_broadcast(shape)


def normalise(nc, own, eng_wait_square, src, xc, sq, st, out, eps, squared, centred, var_sum, rstd):
    v = nc.vector
    own.step(v.tensor_reduce(st[:, 0, :], src, AX.X, ALU.add))
    own.step(v.tensor_scalar(st[:, 1, :], st[:, 0, :], -1.0 / D, None, ALU.mult))
    v.tensor_tensor(xc, src, bc(st[:, 1, :].unsqueeze(2), [P, TB, D]), ALU.add).then_inc(centred, 1)
    eng_wait_square()
    v.tensor_reduce(st[:, 2, :], sq, AX.X, ALU.add).then_inc(var_sum, 1)


def setup(nc, m, d):
    with ExitStack() as ctx:
        zeroed = ctx.enter_context(nc.semaphore("zeroed"))
        block = ctx.enter_context(nc.Block())

        @block.sync
        def _(sp):
            sp.dma_start(m.X[:, :, :], d.x.rearrange("b (t p) d -> p (b t) d", p=P)).then_inc(m.loaded, 16)
            sp.dma_start(m.Wqkv[:, :], d.wqkv).then_inc(m.loaded, 16)
            sp.dma_start(m.Wr[:, :], d.router_w).then_inc(m.loaded, 16)
            sp.dma_start(m.router_b[:, :], d.router_b.partition_broadcast(P)).then_inc(m.loaded, 16)
            sp.dma_start(m.qk_scale[:, 0:H], d.q_scale.partition_broadcast(P)).then_inc(m.loaded, 16)
            sp.dma_start(m.qk_scale[:, H:2 * H], d.k_scale.partition_broadcast(P)).then_inc(m.loaded, 16)
            sp.wait_ge(m.loaded, 6 * 16)

        @block.gpsimd
        def _(pool):
            pool.memset(m.ident[:, :], 0.0).then_inc(zeroed, 1)
            pool.memset(m.ident_bf[:, :], 0.0).then_inc(zeroed, 1)
            pool.memset(m.mask_qk[:, :], 0.0).then_inc(zeroed, 1)
            pool.memset(m.mask_kq[:, :], 0.0).then_inc(zeroed, 1)
            pool.memset(m.lower[:, :, :], 0.0).then_inc(zeroed, 1)
            pool.memset(m.half[:, :], -0.5).then_inc(zeroed, 1)
            pool.wait_ge(zeroed, 6)
            for t in (m.ident, m.ident_bf):
                pool.affine_select(out=t[:, :], in_=t[:, :], compare_op=ALU.not_equal, fill=1.0, base=0,
                                   pattern=[[-1, P]], channel_multiplier=1).then_inc(zeroed, 1)
            pool.affine_select(out=m.mask_qk[:, :], in_=m.mask_qk[:, :], compare_op=ALU.is_ge, fill=MASKED,
                               base=0, pattern=[[-1, P]], channel_multiplier=1).then_inc(zeroed, 1)
            pool.affine_select(out=m.mask_kq[:, :], in_=m.mask_kq[:, :], compare_op=ALU.is_ge, fill=MASKED,
                               base=0, pattern=[[1, P]], channel_multiplier=-1).then_inc(zeroed, 1)
            pool.affine_select(out=m.lower[:, :, :], in_=m.lower[:, :, :], compare_op=ALU.is_ge, fill=1.0,
                               base=0, pattern=[[-1, E], [1, E]], channel_multiplier=0).then_inc(zeroed, 1)
            pool.wait_ge(zeroed, 11)


def project(nc, m):
    with ExitStack() as ctx:
        def sem(name):
            return ctx.enter_context(nc.semaphore("pj_" + name))

        def sb(name, shape, dt=fp32):
            return ctx.enter_context(nc.sbuf_tensor("pj_" + name, shape, dt))

        centred, squared, var_sum, rstd_ready = sem("centred"), sem("squared"), sem("var_sum"), sem("rstd")
        xn_ready, xt_psum, xt_ready = sem("xn_ready"), sem("xt_psum"), sem("xt_ready")
        copied = sem("copied")
        qkv_psum, silu_done, logits_psum = sem("qkv_psum"), sem("silu_done"), sem("logits_psum")
        n2_ready, r_ready, qk_scaled = sem("n2_ready"), sem("r_ready"), sem("qk_scaled")
        vec, pl = sem("vec"), sem("pool")
        XC, SQ = sb("xc", [P, TB, D]), sb("sq", [P, TB, D])
        XN, XT = sb("xn", [P, TB, D]), sb("xt", [P, N])
        ST = sb("st", [P, 4, TB])
        SQK, SQ2 = sb("sqk", [P, TB, 2 * D]), sb("sq2", [P, TB, 2 * D])
        N2, R, F = sb("n2", [P, TB, 2 * H]), sb("r", [P, TB, 2 * H]), sb("f", [P, TB, 2 * H])
        ps = m.ps
        block = ctx.enter_context(nc.Block())

        @block.vector
        def _(v):
            prime(v, qk_scaled)
            with v.Fori(0, B) as b:
                own = Own(v, vec, 8, b)
                xb = m.X[:, bass.ds(b * TB, TB), :]

                def square_wait():
                    v.wait_ge(squared, b + 1)

                normalise(nc, own, square_wait, xb, XC[:, :, :], SQ[:, :, :], ST, XN, EPS_LN,
                          squared, centred, var_sum, None)
                v.wait_ge(rstd_ready, b + 1)
                v.wait_ge(xt_psum, 2 * b + 1)
                v.tensor_tensor(XN[:, :, :], XC[:, :, :], bc(ST[:, 3, :].unsqueeze(2), [P, TB, D]),
                                ALU.mult).then_inc(xn_ready, 1)
                v.wait_ge(logits_psum, b + 1)
                v.tensor_tensor(m.LG[:, bass.ds(b * TB, TB), :],
                                ps[:, 6, 0:TB * E].rearrange("p (t e) -> p t e", e=E),
                                bc(m.router_b[:, :].unsqueeze(1), [P, TB, E]), ALU.add)
                v.wait_ge(silu_done, TB * (b + 1))
                own.step(v.tensor_tensor(SQ2[:, :, :], SQK[:, :, :], SQK[:, :, :], ALU.mult))
                v.tensor_reduce(N2[:, :, :], SQ2[:, :, :].rearrange("p t (h i) -> p t h i", i=HD), AX.X,
                                ALU.add).then_inc(n2_ready, 1)
                v.wait_ge(r_ready, b + 1)
                own.step(v.tensor_scalar(F[:, :, :], R[:, :, :], EPS_DIR, None, ALU.add))
                own.step(v.reciprocal(N2[:, :, :], F[:, :, :]))
                own.step(v.tensor_tensor(F[:, :, :], R[:, :, :], N2[:, :, :], ALU.mult))
                own.step(v.tensor_tensor(N2[:, :, :], F[:, :, :],
                                         bc(m.qk_scale[:, :].unsqueeze(1), [P, TB, 2 * H]), ALU.mult))
                for s, dst in ((0, m.QU), (1, m.KU)):
                    for g in range(G):
                        last = v.tensor_tensor(
                            dst[:, bass.ds(b * G + g, 1), :, :].rearrange("p o t (j i) -> p (o t) j i", i=HD),
                            SQK[:, :, s * D + g * 32:s * D + g * 32 + 32].rearrange("p t (j i) -> p t j i", i=HD),
                            bc(N2[:, :, s * H + g * HG:s * H + g * HG + HG].unsqueeze(3), [P, TB, HG, HD]),
                            ALU.mult)
                last.then_inc(qk_scaled, 1)
                own.mark(v.tensor_copy(ST[:, 1, 0:1], ST[:, 0, 0:1]))
                own.wait()
                own.end()

        @block.gpsimd
        def _(pool):
            prime(pool, copied)
            with pool.Fori(0, B) as b:
                own = Own(pool, pl, 1, b)
                pool.wait_ge(var_sum, b + 1)
                hold(pool, m)
                own.step(pool.tensor_scalar(ST[:, 2, :], ST[:, 2, :], 1.0 / D, EPS_LN, ALU.mult, ALU.add))
                pool.tensor_tensor(ST[:, 3, :], ST[:, 2, :], m.half[:, 0:TB], ALU.pow).then_inc(rstd_ready, 1)
                own.end()
                pool.wait_ge(xt_ready, 2 * b + 2)
                pool.tensor_copy(m.XNT[:, bass.ds(b * N, N)], XT[:, :]).then_inc(copied, 1)

        @block.scalar
        def _(act):
            with act.Fori(0, B) as b:
                act.wait_ge(centred, b + 1)
                act.activation(SQ[:, :, :], XC[:, :, :], ACT.Square).then_inc(squared, 1)
                act.wait_ge(copied, b + 1)
                for f in range(2):
                    act.wait_ge(xt_psum, 2 * b + f + 1 + 1)
                    act.activation(XT[:, f * 512:f * 512 + 512], ps[:, f, :], ACT.Copy).then_inc(xt_ready, 1)
                act.wait_ge(qk_scaled, b + 1)
                for t in range(TB):
                    act.wait_ge(qkv_psum, TB * b + t + 1)
                    act.activation(SQK[:, t, :], ps[:, 2 + t % 4, 0:2 * D], ACT.Silu)
                    act.activation(m.VU[:, bass.ds(b * G, G), t, :],
                                   ps[:, 2 + t % 4, 2 * D:3 * D].rearrange("p (g c) -> p g c", g=G),
                                   ACT.Silu).then_inc(silu_done, 1)
                act.wait_ge(n2_ready, b + 1)
                act.activation(R[:, :, :], N2[:, :, :], ACT.Sqrt).then_inc(r_ready, 1)

        @block.tensor
        def _(pe):
            prime(pe, xt_psum)
            with pe.Fori(0, B) as b:
                pe.wait_ge(xn_ready, b + 1)
                for t in range(TB):
                    ins = pe.transpose(ps[:, t // 4, (t % 4) * P:(t % 4 + 1) * P], XN[:, t, :], m.ident[:, :])
                    if t % 4 == 3:
                        ins.then_inc(xt_psum, 1)
                pe.wait_ge(xt_ready, 2 * b + 2)
                for t in range(TB):
                    last = pe.matmul(ps[:, 6, t * E:t * E + E], XT[:, t * P:(t + 1) * P], m.Wr[:, :],
                                     start=True, stop=True)
                last.then_inc(logits_psum, 1)
                for t in range(TB):
                    if t >= 4:
                        pe.wait_ge(silu_done, TB * b + t - 3)
                    pe.matmul(ps[:, 2 + t % 4, 0:3 * D], XT[:, t * P:(t + 1) * P], m.Wqkv[:, :],
                              start=True, stop=True).then_inc(qkv_psum, 1)


def gates(nc, m):
    with ExitStack() as ctx:
        vec, top, expd = (ctx.enter_context(nc.semaphore("gt_" + n)) for n in ("vec", "top", "exp"))
        cmp_ = ctx.enter_context(nc.sbuf_tensor("gt_cmp", [P, TILES, E, E], fp32))
        rank, tie = (ctx.enter_context(nc.sbuf_tensor("gt_" + n, [P, TILES, E], fp32)) for n in ("rank", "tie"))
        mx = ctx.enter_context(nc.sbuf_tensor("gt_mx", [P, TILES], fp32))
        block = ctx.enter_context(nc.Block())
        full = [P, TILES, E, E]

        @block.vector
        def _(v):
            own = Own(v, vec)
            LG = m.LG[:, :, :]
            other, this = bc(LG.unsqueeze(2), full), bc(LG.unsqueeze(3), full)
            own.step(v.tensor_tensor(cmp_[:, :, :, :], other, this, ALU.is_gt))
            own.step(v.tensor_reduce(rank[:, :, :], cmp_[:, :, :, :], AX.X, ALU.add))
            own.step(v.tensor_tensor(cmp_[:, :, :, :], other, this, ALU.is_equal))
            own.step(v.tensor_tensor(cmp_[:, :, :, :], cmp_[:, :, :, :],
                                     bc(m.lower[:, :, :].unsqueeze(1), full), ALU.mult))
            own.step(v.tensor_reduce(tie[:, :, :], cmp_[:, :, :, :], AX.X, ALU.add))
            own.step(v.tensor_tensor(rank[:, :, :], rank[:, :, :], tie[:, :, :], ALU.add))
            own.step(v.tensor_scalar(rank[:, :, :], rank[:, :, :], 1.5, None, ALU.is_lt))
            own.step(v.tensor_reduce(mx[:, :], LG, AX.X, ALU.max))
            v.tensor_tensor(tie[:, :, :], LG, bc(mx[:, :].unsqueeze(2), [P, TILES, E]),
                            ALU.subtract).then_inc(top, 1)
            v.wait_ge(expd, 1)
            own.step(v.tensor_tensor(tie[:, :, :], m.GT[:, :, :], rank[:, :, :], ALU.mult))
            own.step(v.tensor_reduce(mx[:, :], tie[:, :, :], AX.X, ALU.add))
            own.step(v.reciprocal(mx[:, :], mx[:, :]))
            own.step(v.tensor_tensor(m.GT[:, :, :], tie[:, :, :], bc(mx[:, :].unsqueeze(2), [P, TILES, E]),
                                     ALU.mult))

        @block.scalar
        def _(act):
            act.wait_ge(top, 1)
            act.activation(m.GT[:, :, :], tie[:, :, :], ACT.Exp).then_inc(expd, 1)


P2_UNITS = [(k, c) for half in (0, 1) for k in range(TB) for c in (2 * half, 2 * half + 1) if c >= k // 2]
P1_UNITS = [(i, c, j) for i in range(TB) for c in range(i // 4 + 1) for j in range(HG)]
N2U, N1U = len(P2_UNITS), len(P1_UNITS)
HALF2 = sum(c < 2 for _, c in P2_UNITS)
HALF1 = sum(i < 4 for i, _, _ in P1_UNITS)
P1_FROM = N2U - N1U // 3
OB1, Q2B, OB0, Q2A, K0, K1, Q0, Q1 = range(8)
FILL_AT = {2: OB1, 3: Q2B, 9: OB0, 12: Q2A, 14: K0, 15: K1, 16: Q0, 17: Q1}
PRO_FILLS = 9


def attention(nc, m):
    with ExitStack() as ctx:
        def sem(name):
            return ctx.enter_context(nc.semaphore("at_" + name))

        def sb(name, shape, dt=fp32):
            return ctx.enter_context(nc.sbuf_tensor("at_" + name, shape, dt))

        kq_staged, v_staged, ktx_loaded = sem("kq_staged"), sem("v_staged"), sem("ktx_loaded")
        filled, emptied = sem("filled"), sem("emptied")
        p1_psum, max_done, max_staged = sem("p1_psum"), sem("max_done"), sem("max_staged")
        s2_psum, exp_done, pv_done = sem("s2_psum"), sem("exp_done"), sem("pv_done")
        o_copied, norm_done = sem("o_copied"), sem("norm_done")
        vec, pl, zeroed = sem("vec"), sem("pool"), sem("zeroed")
        KP, QP = sb("kp", [P, TB, HG, 32]), sb("qp", [P, 2, TB, HG, 32])
        VW = sb("vw", [P, 2, TB, HG, 32])
        KT = sb("kt", [P, N], f32r)
        KTX = sb("ktx", [P, 2, HG, N], f32r)
        QT1, QT2 = sb("qt1", [P, 2, N], f32r), sb("qt2", [P, 2, N], f32r)
        PT = sb("pt", [P, 4, HG, 256])
        OT = sb("ot", [P, 512])
        MX, NM = sb("mx", [P, TB, 2, HG]), sb("nm", [P, TB, HG])
        DEN = sb("den", [P, 4, HG])
        ps = m.ps
        P2B = [ps[:, 2 * s:2 * s + 2, :].rearrange("p b (h n) -> p (b h) n", h=2) for s in range(2)]
        P1B = [ps[:, 4 + s, :] for s in range(2)]
        OB, TR = ps[:, 6, :], ps[:, 7, :]
        block = ctx.enter_context(nc.Block())

        def fills(u, at, left_out=0):
            return u * 8 + (at + PRO_FILLS - left_out)

        def steps(eng, step, before, after):
            before()
            step(0, 0)
            step(1, 1)
            with eng.Fori(0, (U - 4) // 2) as i:
                step(i * 2 + 2, 0)
                step(i * 2 + 3, 1)
            step(U - 2, 0)
            step(U - 1, 1)
            after()

        def is_(u, n):
            return isinstance(u, int) and u == n

        def has(u, d):
            return not isinstance(u, int) or u + d < U

        @block.sync
        def _(sp):
            def load(v, par):
                for j in range(HG):
                    sp.dma_start(KTX[32 * j:32 * j + 32, par, j, :].bitcast(fp32),
                                 KT[32 * j:32 * j + 32, :].bitcast(fp32))\
                      .then_inc(ktx_loaded, 16)

            def before():
                sp.wait_ge(zeroed, 1)
                sp.wait_ge(emptied, 2)
                load(0, 0)
                sp.wait_ge(emptied, 6)
                load(1, 1)

            def step(u, par):
                if has(u, 2):
                    sp.wait_ge(emptied, fills(u, K1))
                    sp.wait_ge(s2_psum, u * N2U + N2U)
                    load(u + 2, par)

            steps(sp, step, before, lambda: None)

        @block.gpsimd
        def _(pool):
            def round_split(own, src, hi, hi2, lo):
                own.mark(pool.tensor_copy(hi.bitcast(f32r), src))
                pool.tensor_copy(hi2.bitcast(f32r), src)
                own.wait()
                hold(pool, m)
                return pool.tensor_tensor(lo.bitcast(f32r), src, hi, ALU.subtract)

            def unit_of(t, v):
                return t[:, bass.ds(v, 1), :, :].rearrange("p o t (j i) -> p (o t) j i", i=HD)

            def stage_kq(v, par, count):
                own = Own(pool, pl, 2, count)
                q = QP[:, par, :, :, :]
                round_split(own, unit_of(m.KU, v), KP[:, :, :, 0:8], KP[:, :, :, 8:16], KP[:, :, :, 16:24])
                round_split(own, unit_of(m.QU, v), q[:, :, :, 0:8], q[:, :, :, 16:24], q[:, :, :, 8:16])
                pool.memset(q[:, :, :, 24:26], 0.0).then_inc(kq_staged, 1)

            def stage_v(v, par):
                pool.tensor_copy(VW[:, par, :, :, 0:8], unit_of(m.VU, v)).then_inc(v_staged, 1)

            def before():
                for t in (KP[:, :, :, :], QP[:, :, :, :, :], VW[:, :, :, :, :], KTX[:, :, :, :].bitcast(fp32)):
                    last = pool.memset(t, 0.0)
                last.then_inc(zeroed, 1)
                pool.wait_ge(zeroed, 1)
                pool.memset(KP[:, :, :, 24:26], 1.0)
                pool.memset(VW[:, :, :, :, 8:9], 1.0)
                stage_kq(0, 0, 0)
                stage_v(0, 0)
                pool.wait_ge(filled, 4)
                stage_kq(1, 1, 1)

            def step(u, par):
                if has(u, 1):
                    pool.wait_ge(pv_done, u * N2U)
                    stage_v(u + 1, 1 - par)
                if has(u, 2):
                    pool.wait_ge(filled, fills(u, Q2B))
                    stage_kq(u + 2, par, u + 2)

            steps(pool, step, before, lambda: None)

        @block.scalar
        def _(act):
            def copy_out(dst, count):
                act.wait_ge(filled, count)
                act.activation(dst, TR, ACT.Copy).then_inc(emptied, 1)

            def before():
                for v in (0, 1):
                    if v == 1:
                        act.wait_ge(ktx_loaded, HG * 16)
                    for f in range(2):
                        copy_out(KT[:, f * 512:f * 512 + 512], 4 * v + f + 1)
                    for f in range(2):
                        copy_out(QT1[:, v, f * 512:f * 512 + 512], 4 * v + f + 3)
                copy_out(QT2[:, 0, 0:512], 9)

            def step(u, par):
                less = 4 if is_(u, U - 1) else 0
                for q, (k, c) in enumerate(P2_UNITS):
                    act.wait_ge(s2_psum, u * N2U + q + 1)
                    if q >= 4 or not is_(u, 0):
                        act.wait_ge(pv_done, u * N2U + (q - 3))
                    lo = 128 if k % 2 and c == k // 2 else 0
                    act.activation(PT[:, q % 4, :, lo:256] if lo else PT[:, q % 4, :, :],
                                   P2B[q % 2][:, :, lo:256] if lo else P2B[q % 2], ACT.Exp)\
                       .then_inc(exp_done, 1)
                    f = FILL_AT.get(q)
                    if f == Q2B:
                        copy_out(QT2[:, par, 512:1024], fills(u, Q2B, less))
                    if f == Q2A and has(u, 1):
                        copy_out(QT2[:, 1 - par, 0:512], fills(u, Q2A))
                    if f in (K0, K1) and has(u, 2):
                        copy_out(KT[:, (f - K0) * 512:(f - K0) * 512 + 512], fills(u, f))
                    if f in (Q0, Q1) and has(u, 2):
                        copy_out(QT1[:, par, (f - Q0) * 512:(f - Q0) * 512 + 512], fills(u, f))

            steps(act, step, before, lambda: None)

        @block.vector
        def _(v):
            def reduce(un, n):
                i, c, j = P1_UNITS[n]
                w = min(512, (i + 1) * P - c * 512)
                v.wait_ge(p1_psum, un * N1U + n + 1)
                v.tensor_reduce(MX[:, i, c, j:j + 1], P1B[n % 2][:, 0:w], AX.X, ALU.max).then_inc(max_done, 1)

            def stage_max(own, un, par, half):
                rows = slice(4 * half, 4 * half + 4)
                v.wait_ge(max_done, un * N1U + (N1U if half else HALF1))
                src = MX[:, rows, 0, :]
                if half:
                    own.step(v.tensor_tensor(MX[:, rows, 0, :], src, MX[:, rows, 1, :], ALU.max))
                own.step(v.tensor_scalar(NM[:, rows, :], src, -1.0, None, ALU.mult))
                hi, lo = (QP[:, par, rows, :, c:c + 1].rearrange("p t j o -> p t (j o)") for c in (24, 25))
                own.step(v.tensor_scalar(hi.bitcast(f32r), NM[:, rows, :], 1.0, None, ALU.mult))
                v.tensor_tensor(lo.bitcast(f32r), NM[:, rows, :], hi, ALU.subtract).then_inc(max_staged, 1)

            def copy_o(u, half):
                v.wait_ge(pv_done, u * N2U + (N2U if half else HALF2))
                v.tensor_copy(OT[:, :], OB).then_inc(o_copied, 1)

            def divide(own, u, half, count):
                v.wait_ge(filled, count)
                t4 = TR.rearrange("p (t j c) -> p t j c", t=4, j=HG)
                own.step(v.reciprocal(DEN[:, :, :], t4[:, :, :, 8:9].rearrange("p t j o -> p t (j o)")))
                v.tensor_tensor(
                    m.QU[:, bass.ds(u, 1), 4 * half:4 * half + 4, :].rearrange("p o t (j i) -> p (o t) j i", i=HD),
                    t4[:, :, :, 0:8], bc(DEN[:, :, :].unsqueeze(3), [P, 4, HG, HD]), ALU.mult)\
                 .then_inc(emptied, 1)

            PER = 7

            def before():
                own = Own(v, vec)
                for n in range(N1U):
                    reduce(0, n)
                    if n == HALF1 - 1:
                        stage_max(own, 0, 0, 0)
                stage_max(own, 0, 0, 1)
                assert own.n == 5

            def step(u, par):
                less = 4 if is_(u, U - 1) else 0
                own = Own(v, vec, 1, u * PER + 5 - (0 if is_(u, 0) else 1))
                if not is_(u, 0):
                    copy_o(u - 1, 1)
                    divide(own, u - 1, 1, fills(u, OB1, less))
                for n in range(N1U):
                    if n == 9:
                        copy_o(u, 0)
                    if n == HALF1 and has(u, 1):
                        stage_max(own, u + 1, 1 - par, 0)
                    if n == HALF1 + 2:
                        divide(own, u, 0, fills(u, OB0, less))
                    if has(u, 1):
                        reduce(u + 1, n)
                if has(u, 1):
                    stage_max(own, u + 1, 1 - par, 1)

            def after():
                own = Own(v, vec, 1, (U - 1) * PER + 5 - 1 + 2)
                copy_o(U - 1, 1)
                divide(own, U - 1, 1, fills(U, OB1, 9))

            steps(v, step, before, after)

        @block.tensor
        def _(pe):
            def fill(what, in_of, count):
                if count > 1:
                    pe.wait_ge(emptied, count - 1)
                for t in range(4):
                    ins = pe.transpose(TR[:, t * P:(t + 1) * P], in_of(t), m.ident[:, :])
                ins.then_inc(filled, 1)

            def staged(tile, half):
                return lambda t: tile[:, 4 * half + t, :, :].rearrange("p j c -> p (j c)")

            def pass1(un, par, n):
                i, c, j = P1_UNITS[n]
                w = max(256, min(512, (i + 1) * P - c * 512))
                if not (is_(un, 0) and n < 2):
                    pe.wait_ge(max_done, un * N1U + (n - 1))
                diag = c == i // 4
                ins = pe.matmul(P1B[n % 2][:, 0:w], QT1[:, par, i * P:(i + 1) * P],
                                KTX[:, par, j, c * 512:c * 512 + w], start=True, stop=not diag)
                if diag:
                    at = (i % 4) * P
                    ins = pe.matmul(P1B[n % 2][:, at:at + P], m.ident_bf[:, :], m.mask_qk[:, :],
                                    start=False, stop=True)
                ins.then_inc(p1_psum, 1)

            def scores2(u, par, q):
                k, c = P2_UNITS[q]
                if not (is_(u, 0) and q < 2):
                    pe.wait_ge(exp_done, u * N2U + (q - 1))
                diag = c == k // 2
                for j in range(HG):
                    out = P2B[q % 2][:, j, :]
                    ins = pe.matmul(out, KTX[:, par, j, k * P:(k + 1) * P],
                                    QT2[:, par, c * 256:c * 256 + 256], start=True, stop=not diag)
                    if diag:
                        at = (k % 2) * P
                        ins = pe.matmul(out[:, at:at + P], m.ident_bf[:, :], m.mask_kq[:, :],
                                        start=False, stop=True)
                ins.then_inc(s2_psum, 1)

            def values(u, par, q):
                k, c = P2_UNITS[q]
                pe.wait_ge(exp_done, u * N2U + q + 1)
                if q == 0:
                    pe.wait_ge(v_staged, u + 1)
                if q in (0, HALF2) and not (is_(u, 0) and q == 0):
                    pe.wait_ge(o_copied, u * 2 + (1 if q else 0))
                lo = 128 if k % 2 and c == k // 2 else 0
                at = (c % 2) * 256 + lo
                for j in range(HG):
                    ins = pe.matmul(OB[32 * j:32 * j + 32, at:at + 256 - lo], VW[:, par, k, j, :],
                                    PT[:, q % 4, j, lo:256], start=q in (0, HALF2),
                                    stop=q in (HALF2 - 1, N2U - 1), skip_group_check=True)
                ins.then_inc(pv_done, 1)

            def before():
                for v in (0, 1):
                    pe.wait_ge(kq_staged, v + 1)
                    for f in range(2):
                        fill("k", staged(KP, f), 4 * v + f + 1)
                    for f in range(2):
                        fill("q", staged(QP[:, v, :, :, :], f), 4 * v + f + 3)
                pe.wait_ge(emptied, 4)
                pe.wait_ge(ktx_loaded, HG * 16)
                for n in range(N1U):
                    pass1(0, 0, n)
                    if n == HALF1 + 8:
                        pe.wait_ge(max_staged, 1)
                        fill("q2", staged(QP[:, 0, :, :, :], 0), 9)

            def step(u, par):
                less = 4 if is_(u, U - 1) else 0
                n = 0
                for q in range(N2U):
                    if q == 0:
                        pe.wait_ge(emptied, 9 if is_(u, 0) else fills(u - 1, Q2A))
                    if q == HALF2:
                        pe.wait_ge(emptied, fills(u, Q2B, less))
                    scores2(u, par, q)
                    if q >= P1_FROM and has(u, 1):
                        if n == 0:
                            pe.wait_ge(ktx_loaded, (u + 2) * (HG * 16))
                            if not is_(u, 0):
                                pe.wait_ge(emptied, fills(u - 1, Q1))
                        for _ in range(3):
                            pass1(u + 1, 1 - par, n)
                            n += 1
                    f = FILL_AT.get(q)
                    if f == OB1 and not is_(u, 0):
                        pe.wait_ge(o_copied, u * 2)
                        fill("o", lambda t: OT[:, t * P:(t + 1) * P], fills(u, OB1, less))
                    if f == Q2B:
                        pe.wait_ge(max_staged, u * 2 + 2)
                        fill("q2", staged(QP[:, par, :, :, :], 1), fills(u, Q2B, less))
                    if f == OB0:
                        pe.wait_ge(o_copied, u * 2 + 1)
                        fill("o", lambda t: OT[:, t * P:(t + 1) * P], fills(u, OB0, less))
                    if f == Q2A and has(u, 1):
                        pe.wait_ge(max_staged, u * 2 + 3)
                        fill("q2", staged(QP[:, 1 - par, :, :, :], 0), fills(u, Q2A))
                    if f in (K0, K1, Q0, Q1) and has(u, 2):
                        if f == K0:
                            pe.wait_ge(kq_staged, u + 3)
                        tile = KP if f in (K0, K1) else QP[:, par, :, :, :]
                        fill("kq", staged(tile, f % 2), fills(u, f))
                    if q:
                        values(u, par, q - 1)
                    elif not is_(u, 0):
                        values(u - 1, 1 - par, N2U - 1)

            def after():
                values(U - 1, 1, N2U - 1)
                pe.wait_ge(o_copied, 2 * U)
                fill("o", lambda t: OT[:, t * P:(t + 1) * P], fills(U, OB1, 9))

            steps(pe, step, before, after)


def mix_heads(nc, m):
    with ExitStack() as ctx:
        def sem(name):
            return ctx.enter_context(nc.semaphore("mh_" + name))

        copied, gathered, turned, out_ready, added = (sem(n) for n in ("copied", "gathered", "turned", "out", "added"))
        AW = ctx.enter_context(nc.sbuf_tensor("mh_aw", [P, TB, G, 32], fp32))
        AT = ctx.enter_context(nc.sbuf_tensor("mh_at", [P, N], fp32))
        GW = ctx.enter_context(nc.sbuf_tensor("mh_gw", [P, TB, E], fp32))
        GTT = ctx.enter_context(nc.sbuf_tensor("mh_gt", [E, N], fp32))
        ps = m.ps
        block = ctx.enter_context(nc.Block())

        @block.vector
        def _(v):
            prime(v, added)
            with v.Fori(0, B) as b:
                v.wait_ge(gathered, 4 * b + 1)
                v.tensor_copy(AW[:, :, :, :].rearrange("p t g c -> p g t c"), m.QU[:, bass.ds(b * G, G), :, :])
                v.tensor_copy(GW[:, :, :], m.GT[:, bass.ds(b * TB, TB), :]).then_inc(copied, 1)
                for f in range(2):
                    v.wait_ge(out_ready, 2 * b + f + 1)
                    xs = m.X[:, bass.ds(b * TB + 4 * f, 4), :]
                    v.tensor_tensor(xs, xs, ps[:, 4 + f, :].rearrange("p (t d) -> p t d", t=4), ALU.add)\
                     .then_inc(added, 1)

        @block.scalar
        def _(act):
            with act.Fori(0, B) as b:
                for f in range(2):
                    act.wait_ge(gathered, 4 * b + f + 1 + 1)
                    act.activation(AT[:, f * 512:f * 512 + 512], ps[:, f, :], ACT.Copy).then_inc(turned, 1)
                for f in range(2):
                    act.wait_ge(gathered, 4 * b + f + 3 + 1)
                    act.activation(GTT[:, f * 512:f * 512 + 512], ps[0:E, 2 + f, :], ACT.Copy).then_inc(turned, 1)

        @block.tensor
        def _(pe):
            prime(pe, gathered)
            with pe.Fori(0, B) as b:
                pe.wait_ge(copied, b + 1)
                for t in range(TB):
                    ins = pe.transpose(ps[:, t // 4, (t % 4) * P:(t % 4 + 1) * P], AW[:, t, :, :].rearrange("p g c -> p (g c)"), m.ident[:, :])
                    if t % 4 == 3:
                        ins.then_inc(gathered, 1)
                for t in range(TB):
                    ins = pe.transpose(ps[0:E, 2 + t // 4, (t % 4) * P:(t % 4 + 1) * P], GW[:, t, :], m.ident[:, :])
                    if t % 4 == 3:
                        ins.then_inc(gathered, 1)
                pe.wait_ge(turned, 4 * b + 4)
                for t in range(TB):
                    if t % 4 == 0:
                        pe.wait_ge(added, 2 * b + 1)
                    out = ps[:, 4 + t // 4, (t % 4) * P:(t % 4 + 1) * P]
                    pe.matmul(out, AT[:, t * P:(t + 1) * P], m.Wo[:, :], start=True, stop=False)
                    ins = pe.matmul(out, GTT[:, t * P:(t + 1) * P], m.b2[:, :], start=False, stop=True)
                    if t % 4 == 3:
                        ins.then_inc(out_ready, 1)


def experts(nc, m, d):
    CH = B * N // 512
    with ExitStack() as ctx:
        def sem(name):
            return ctx.enter_context(nc.semaphore("ex_" + name))

        loaded = [sem("loaded0"), sem("loaded1")]
        h_psum, h_ready, y_psum, added = (sem(n) for n in ("h_psum", "h_ready", "y_psum", "added"))
        W1 = ctx.enter_context(nc.sbuf_tensor("ex_w1", [P, 2, HID], fp32))
        W2 = ctx.enter_context(nc.sbuf_tensor("ex_w2", [P, 2, HC, D], fp32))
        HT = ctx.enter_context(nc.sbuf_tensor("ex_ht", [P, 2, HC, 512], fp32))
        ps = m.ps
        block = ctx.enter_context(nc.Block())

        @block.sync
        def _(sp):
            def load(s, e):
                sp.dma_start(W1[:, s, :], d.w1[e, :, :]).then_inc(loaded[s], 16)
                sp.dma_start(W2[:, s, :, :], d.w2[e, :, :].rearrange("(c p) d -> p c d", p=P))\
                  .then_inc(loaded[s], 16)

            with sp.Fori(0, E // 2) as ep:
                load(0, ep * 2)
                sp.wait_ge(y_psum, ep * (2 * CH) + 1)
                load(1, ep * 2 + 1)
                sp.wait_ge(y_psum, ep * (2 * CH) + CH + 1)
                hold(sp, m)

        @block.scalar
        def _(act):
            with act.Fori(0, E) as e:
                with act.Fori(0, CH // 2) as cp:
                    for s in range(2):
                        n = e * CH + cp * 2 + s
                        for hc in range(HC):
                            act.wait_ge(h_psum, n * HC + hc + 1)
                            hold(act, m)
                            act.activation(HT[:, s, hc, :], ps[:, hc, :], ACT.Relu,
                                           bias=m.b1[:, bass.ds(e, 1), hc]).then_inc(h_ready, 1)

        @block.vector
        def _(v):
            prime(v, added)
            with v.Fori(0, E) as e:
                with v.Fori(0, CH // 2) as cp:
                    for s in range(2):
                        n = e * CH + cp * 2 + s
                        v.wait_ge(y_psum, n + 1 + 1)
                        for t in range(4):
                            tile = m.X[:, bass.ds(cp * 8 + (4 * s + t), 1), :].rearrange("p o d -> p (o d)")
                            last = v.scalar_tensor_tensor(
                                tile, ps[:, 4 + s, t * P:(t + 1) * P],
                                m.GT[:, bass.ds(cp * 8 + (4 * s + t), 1), bass.ds(e, 1)]
                                 .rearrange("p a b -> p (a b)"), tile, ALU.mult, ALU.add)
                        last.then_inc(added, 1)

        @block.tensor
        def _(pe):
            prime(pe, y_psum)
            with pe.Fori(0, E // 2) as ep:
                for w in range(2):
                    pe.wait_ge(loaded[w], ep * 32 + 32)
                    hold(pe, m)
                    with pe.Fori(0, CH // 2) as cp:
                        n = ep * (2 * CH) + w * CH + cp * 2
                        for s in range(2):
                            for hc in range(HC):
                                if s == 1:
                                    pe.wait_ge(h_ready, n * HC + hc + 1)
                                pe.matmul(ps[:, hc, :], W1[:, w, hc * P:(hc + 1) * P],
                                          m.XNT[:, bass.ds((cp * 2 + s) * 512, 512)],
                                          start=True, stop=True).then_inc(h_psum, 1)
                        for s in range(2):
                            pe.wait_ge(h_ready, (n + s + 1) * HC)
                            pe.wait_ge(added, n + 1)
                            for t in range(4):
                                for hc in range(HC):
                                    ins = pe.matmul(ps[:, 4 + s, t * P:(t + 1) * P],
                                                    HT[:, s, hc, t * P:(t + 1) * P], W2[:, w, hc, :],
                                                    start=hc == 0, stop=hc == HC - 1)
                            ins.then_inc(y_psum, 1)


def load_late(nc, m, d):
    with ExitStack() as ctx:
        block = ctx.enter_context(nc.Block())

        @block.sync
        def _(sp):
            sp.dma_start(m.Wo[:, :], d.wo).then_inc(m.loaded, 16)
            sp.dma_start(m.b2[:, :], d.b2).then_inc(m.loaded, 16)
            sp.dma_start(m.b1[:, :, :], d.b1).then_inc(m.loaded, 16)
            sp.wait_ge(m.loaded, 9 * 16)


def gated_attention(nc, m, d):
    with ExitStack() as ctx:
        def sem(name):
            return ctx.enter_context(nc.semaphore("ga_" + name))

        def sb(name, shape, dt=fp32):
            return ctx.enter_context(nc.sbuf_tensor("ga_" + name, shape, dt))

        ps = m.ps
        loaded = sem("loaded")
        centred, squared, var_sum, rstd = sem("centred"), sem("squared"), sem("var_sum"), sem("rstd")
        xn_ready, turned_psum, turned = sem("xn_ready"), sem("turned_psum"), sem("turned")
        xnn_ready, kept, residual = sem("xnn_ready"), sem("kept"), sem("residual")
        z_psum, z_ready, qk_ready = sem("z_psum"), sem("z_ready"), sem("qk_ready")
        uv_psum, uv_ready = sem("uv_psum"), sem("uv_ready")
        s_psum, relu_done, a_ready, av_psum, o_ready = sem("s_psum"), sem("relu"), sem("a"), sem("av"), sem("o")
        out_psum, out_added = sem("out_psum"), sem("out_added")
        vec, pl = sem("vec"), sem("pool")
        WIN, BIN = sb("win", [P, 5 * P]), sb("bin", [P, 5])
        BV, ONE = sb("bv", [1, E1]), sb("one", [1, P])
        WOUT, BOUT = sb("wout", [P, 2, D]), sb("bout", [P, D])
        COL = sb("col", [P, 6])
        XC, SQ, XN, XNN = (sb(n, [P, TB, D]) for n in ("xc", "sq", "xn", "xnn"))
        ST = sb("st", [P, 2, 4, TB])
        XT = sb("xt", [P, N])
        Z, Q, K = (sb(n, [P, N]) for n in ("z", "q", "k"))
        UT, V = sb("ut", [P, 2, N]), sb("v", [P, TB, E1])
        RL, A = sb("rl", [P, 2, 512]), sb("a", [P, 2, 512])
        OG = sb("og", [P, 2, 512])
        block = ctx.enter_context(nc.Block())

        @block.sync
        def _(sp):
            for dst, src in ((WIN[:, :], d.w_in), (BIN[:, :], d.b_in),
                             (BV[:, :], d.b_v.unsqueeze(0)),
                             (WOUT[:, :, :], d.w_out.rearrange("(c p) d -> p c d", p=P)),
                             (BOUT[:, :], d.b_out.partition_broadcast(P)),
                             (COL[:, :], d.columns)):
                sp.dma_start(dst, src).then_inc(loaded, 16)

        LOADS = 6 * 16

        @block.vector
        def _(v):
            v.memset(ONE[:, :], 1.0)
            v.wait_ge(loaded, LOADS)
            with v.Fori(0, B) as b:
                own = Own(v, vec, 4, b)
                xb = m.X[:, bass.ds(b * TB, TB), :]
                for k, (src, out, ready) in enumerate(((xb, XN, xn_ready), (XN[:, :, :], XNN, xnn_ready))):
                    st = ST[:, k, :, :]

                    def square_wait():
                        v.wait_ge(squared, 2 * b + k + 1)

                    if k == 1:
                        v.wait_ge(xn_ready, b + 1)
                    normalise(nc, own, square_wait, src, XC[:, :, :], SQ[:, :, :], st, out, EPS_LN,
                              squared, centred, var_sum, rstd)
                    v.wait_ge(rstd, 2 * b + k + 1)
                    if k == 0:
                        v.wait_ge(kept, b + 1)
                        v.wait_ge(turned_psum, 4 * b + 1)
                    v.tensor_tensor(out[:, :, :], XC[:, :, :], bc(st[:, 3, :].unsqueeze(2), [P, TB, D]),
                                    ALU.mult).then_inc(ready, 1)
                own.end()
                for f in range(2):
                    v.wait_ge(turned_psum, 4 * b + f + 3 + 1)
                    v.tensor_scalar(XT[:, f * 512:f * 512 + 512], ps[:, 2 + f, :], COL[:, 0:1], COL[:, 1:2],
                                    ALU.mult, ALU.add).then_inc(turned, 1)
                v.wait_ge(z_ready, 2 * b + 2)
                v.tensor_scalar(Q[:, :], Z[:, :], COL[:, 2:3], COL[:, 3:4], ALU.mult, ALU.add)
                v.tensor_scalar(K[:, :], Z[:, :], COL[:, 4:5], COL[:, 5:6], ALU.mult, ALU.add).then_inc(qk_ready, 1)
                for c in range(2):
                    for kk in range(TB):
                        n = 2 * TB * b + (c * TB + kk)
                        v.wait_ge(relu_done, n + 1)
                        if kk >= 2:
                            v.wait_ge(av_psum, n - 1)
                        v.tensor_tensor(A[:, kk % 2, :], RL[:, kk % 2, :], RL[:, kk % 2, :], ALU.mult)\
                         .then_inc(a_ready, 1)
                    v.wait_ge(av_psum, 2 * TB * b + (c + 1) * TB)
                    for e in range(2):
                        ins = v.tensor_tensor(OG[:, e, :], ps[:, 4 + e, :], UT[:, e, c * 512:c * 512 + 512], ALU.mult)
                    ins.then_inc(o_ready, 1)
                    v.wait_ge(out_psum, 2 * b + c + 1)
                    v.wait_ge(residual, b + 1)
                    xs = m.X[:, bass.ds(b * TB + 4 * c, 4), :]
                    v.tensor_tensor(xs, xs, ps[:, 6, :].rearrange("p (t d) -> p t d", t=4), ALU.add)\
                     .then_inc(out_added, 1)

        @block.gpsimd
        def _(pool):
            prime(pool, kept)
            pool.wait_ge(loaded, LOADS)
            with pool.Fori(0, B) as b:
                own = Own(pool, pl, 3, b)
                for k in range(2):
                    pool.wait_ge(var_sum, 2 * b + k + 1)
                    hold(pool, m)
                    own.step(pool.tensor_scalar(ST[:, k, 2, :], ST[:, k, 2, :], 1.0 / D, EPS_LN, ALU.mult, ALU.add))
                    pool.tensor_tensor(ST[:, k, 3, :], ST[:, k, 2, :], m.half[:, 0:TB], ALU.pow).then_inc(rstd, 1)
                xb = m.X[:, bass.ds(b * TB, TB), :]
                pool.wait_ge(xnn_ready, b + 1)
                own.step(pool.tensor_tensor(xb, xb, XN[:, :, :], ALU.add))
                hold(pool, m)
                pool.tensor_tensor(xb, xb, bc(BOUT[:, :].unsqueeze(1), [P, TB, D]), ALU.add).then_inc(residual, 1)
                pool.tensor_copy(m.XN2[:, bass.ds(b * TB, TB), :], XN[:, :, :]).then_inc(kept, 1)
                own.end()

        @block.scalar
        def _(act):
            act.wait_ge(loaded, LOADS)
            with act.Fori(0, B) as b:
                act.wait_ge(centred, 2 * b + 1)
                act.activation(SQ[:, :, :], XC[:, :, :], ACT.Square).then_inc(squared, 1)
                act.wait_ge(centred, 2 * b + 2)
                act.activation(SQ[:, :, :], XC[:, :, :], ACT.Square).then_inc(squared, 1)
                for f in range(2):
                    act.wait_ge(turned_psum, 4 * b + f + 1 + 1)
                    act.activation(m.XNT[:, bass.ds(b * N + f * 512, 512)], ps[:, f, :], ACT.Copy)\
                       .then_inc(turned, 1)
                for f in range(2):
                    act.wait_ge(z_psum, 2 * b + f + 1)
                    act.activation(Z[:, f * 512:f * 512 + 512], ps[:, f, :], ACT.Silu, bias=BIN[:, 4:5])\
                       .then_inc(z_ready, 1)
                for n in range(4):
                    act.wait_ge(uv_psum, 12 * b + n + 1)
                    act.activation(UT[:, n // 2, (n % 2) * 512:(n % 2) * 512 + 512], ps[:, 2 + n % 2, :], ACT.Silu,
                                   bias=BIN[:, n // 2:n // 2 + 1]).then_inc(uv_ready, 1)
                for t in range(TB):
                    act.wait_ge(uv_psum, 12 * b + t + 5)
                    act.activation(V[:, t, :], ps[:, 4 + t % 2, 0:E1], ACT.Silu).then_inc(uv_ready, 1)
                for n in range(2 * TB):
                    act.wait_ge(s_psum, 2 * TB * b + n + 1)
                    if n >= 2:
                        act.wait_ge(a_ready, 2 * TB * b + n - 1)
                    act.activation(RL[:, n % 2, :], ps[:, n % 4, :], ACT.Relu, scale=1.0 / N).then_inc(relu_done, 1)

        @block.tensor
        def _(pe):
            prime(pe, turned_psum)
            pe.wait_ge(loaded, LOADS)
            with pe.Fori(0, B) as b:
                for k, (src, ready) in enumerate(((XN, xn_ready), (XNN, xnn_ready))):
                    pe.wait_ge(ready, b + 1)
                    for t in range(TB):
                        ins = pe.transpose(ps[:, 2 * k + t // 4, (t % 4) * P:(t % 4 + 1) * P], src[:, t, :],
                                           m.ident[:, :])
                        if t % 4 == 3:
                            ins.then_inc(turned_psum, 1)
                pe.wait_ge(turned, 4 * b + 4)
                for f in range(2):
                    pe.matmul(ps[:, f, :], WIN[:, 4 * P:5 * P], XT[:, f * 512:f * 512 + 512],
                              start=True, stop=True).then_inc(z_psum, 1)
                for n in range(4):
                    if n >= 2:
                        pe.wait_ge(uv_ready, 12 * b + n - 1)
                    pe.matmul(ps[:, 2 + n % 2, :], WIN[:, (n // 2) * P:(n // 2 + 1) * P],
                              XT[:, (n % 2) * 512:(n % 2) * 512 + 512], start=True, stop=True).then_inc(uv_psum, 1)
                for t in range(TB):
                    if t >= 2:
                        pe.wait_ge(uv_ready, 12 * b + t + 3)
                    out = ps[:, 4 + t % 2, 0:E1]
                    pe.matmul(out, XT[:, t * P:(t + 1) * P], WIN[:, E1:2 * E1], start=True, stop=False)
                    pe.matmul(out, ONE[:, :], BV[:, :], start=False, stop=True).then_inc(uv_psum, 1)
                pe.wait_ge(qk_ready, b + 1)
                pe.wait_ge(uv_ready, 12 * b + 12)

                def scores(n):
                    if n >= 4:
                        pe.wait_ge(relu_done, 2 * TB * b + n - 3)
                    pe.matmul(ps[:, n % 4, :], K[:, (n % TB) * P:(n % TB + 1) * P],
                              Q[:, (n // TB) * 512:(n // TB) * 512 + 512], start=True, stop=True).then_inc(s_psum, 1)

                scores(0)
                scores(1)
                for n in range(2 * TB):
                    c, kk = n // TB, n % TB
                    if n + 2 < 2 * TB:
                        scores(n + 2)
                    pe.wait_ge(a_ready, 2 * TB * b + n + 1)
                    if kk == 0 and c == 1:
                        pe.wait_ge(o_ready, 2 * b + 1)
                    for e in range(2):
                        ins = pe.matmul(ps[:, 4 + e, :], V[:, kk, e * P:(e + 1) * P], A[:, kk % 2, :],
                                        start=kk == 0, stop=kk == TB - 1)
                    ins.then_inc(av_psum, 1)
                    if kk == TB - 1:
                        pe.wait_ge(o_ready, 2 * b + c + 1)
                        if c == 1:
                            pe.wait_ge(out_added, 2 * b + 1)
                        for t in range(4):
                            for e in range(2):
                                ins = pe.matmul(ps[:, 6, t * P:(t + 1) * P], OG[:, e, t * P:(t + 1) * P],
                                                WOUT[:, e, :], start=e == 0, stop=e == 1)
                        ins.then_inc(out_psum, 1)


CW = 256
CHUNKS = SLOTS // CW
EC = CW // NP_
GROUPS = SLOTS // P
YW = D + 2


def soft_experts(nc, m, d):
    with ExitStack() as ctx:
        def sem(name):
            return ctx.enter_context(nc.semaphore("se_" + name))

        def sb(name, shape, dt=fp32):
            return ctx.enter_context(nc.sbuf_tensor("se_" + name, shape, dt))

        ps = m.ps
        loaded, w_loaded, filled = sem("loaded"), sem("w_loaded"), sem("filled")
        l_psum, shifted, exp_done, sum_done, inv_done = sem("l_psum"), sem("shifted"), sem("exp"), sem("sum"), sem("inv")
        disp_ready, slots_psum, slots_ready = sem("disp"), sem("slots_psum"), sem("slots_ready")
        y_psum, y_ready = sem("y_psum"), sem("y_ready")
        vec, pl, row_ready, row_psum = sem("vec"), sem("pool"), sem("row_ready"), sem("row_psum")
        row_copied, row_stored, row_spread = sem("row_copied"), sem("row_stored"), sem("row_spread")
        PHI = sb("phi", [P, SLOTS])
        W = sb("w", [P, EC, D])
        BIAS = sb("bias", [P, GROUPS, D])
        Y = sb("y", [P, GROUPS, B, YW])
        M = sb("m", [P, 2, CW])
        EX, SU = sb("ex", [P, 4, B, CW]), sb("su", [P, 2, 2, CW])
        SL = sb("sl", [P, B, CW])
        RM, RT = sb("rm", [P, B, TB]), sb("rt", [P, 2, B])
        RR = sb("rr", [B * TB, P])
        RB = sb("rb", [P, B * N])
        row_dram = nc.dram_tensor("row_max", (B * TB, P), fp32).ap()

        def logits_of(s):
            return ps[:, 2 * s:2 * s + 2, :].rearrange("p k (h c) -> p (k h) c", h=2)

        slots_bank = ps[:, 4:6, :].rearrange("p k (h c) -> p (k h) c", h=2)
        part1 = nc.Block()
        block = part1.__enter__()

        @block.sync
        def _(sp):
            sp.dma_start(PHI[:, :], d.phi).then_inc(loaded, 16)
            for q in range(4):
                sp.dma_start(BIAS[32 * q:32 * q + 32, :, :],
                             d.b.rearrange("(g q) e -> q g e", q=4)[q, :, :].partition_broadcast(32))\
                  .then_inc(loaded, 16)
            with sp.Fori(0, CHUNKS) as c:
                sp.wait_ge(y_psum, 2 * c + 1)
                sp.dma_start(W[:, :, :], d.w[bass.ds(c * EC, EC), :, :].rearrange("n d e -> d n e"))\
                  .then_inc(w_loaded, 16)
            sp.wait_ge(row_copied, 1)
            sp.dma_start(row_dram, RR[:, :]).then_inc(row_stored, 16)
            sp.wait_ge(row_stored, 16)
            sp.dma_start(RB[:, :], row_dram.rearrange("a p -> (a p)").partition_broadcast(P)).then_inc(row_spread, 16)
            sp.wait_ge(row_spread, 16)

        @block.vector
        def _(v):
            prime(v, y_ready)
            v.memset(RM[:, :, :], -3.0e38)
            v.memset(Y[:, :, :, D:YW], 1.0).then_inc(filled, 1)
            v.wait_ge(filled, 1)
            v.wait_ge(loaded, 5 * 16)
            with v.Fori(0, CHUNKS) as c:
                own = Own(v, vec, 2 * TB, c)

                def invert(t):
                    v.wait_ge(sum_done, TB * c + t + 1)
                    v.reciprocal(SU[:, 1, t % 2, :], SU[:, 0, t % 2, :]).then_inc(inv_done, 1)

                for t in range(TB):
                    s = t % 2
                    v.wait_ge(l_psum, TB * c + t + 1)
                    L = logits_of(s)
                    own.mark(v.tensor_reduce(M[:, s, :], L.rearrange("p b c -> p c b"), AX.X, ALU.max))
                    own.mark(v.tensor_reduce(RT[:, s, :], L, AX.X, ALU.max))
                    own.wait()
                    if t >= 4:
                        v.wait_ge(slots_psum, TB * c + t - 3)
                    v.tensor_tensor(EX[:, t % 4, :, :], L, bc(M[:, s, :].unsqueeze(1), [P, B, CW]), ALU.subtract)\
                     .then_inc(shifted, 1)
                    v.tensor_tensor(RM[:, :, t], RM[:, :, t], RT[:, s, :], ALU.max).then_inc(row_ready, 1)
                    if t:
                        invert(t - 1)
                invert(TB - 1)
                own.end()
                v.wait_ge(row_ready, TB * c + TB)
                for h in range(2):
                    v.wait_ge(y_psum, 2 * c + h + 1 + 1)
                    v.tensor_tensor(Y[:, bass.ds(2 * c + h, 1), :, 0:D].rearrange("p o b e -> p (o b) e"),
                                    ps[:, 6 + h, :].rearrange("p (b e) -> p b e", b=B),
                                    bc(BIAS[:, bass.ds(2 * c + h, 1), :], [P, B, D]), ALU.add).then_inc(y_ready, 1)

        @block.scalar
        def _(act):
            prime(act, slots_ready)
            with act.Fori(0, CHUNKS) as c:
                def exponentials(t):
                    act.wait_ge(shifted, TB * c + t + 1)
                    act.activation(EX[:, t % 4, :, :], EX[:, t % 4, :, :], ACT.Exp).then_inc(exp_done, 1)

                for t in range(TB):
                    exponentials(t)
                act.wait_ge(slots_psum, TB * c + TB)
                act.activation(SL[:, :, :], slots_bank, ACT.Copy).then_inc(slots_ready, 1)
            act.wait_ge(row_psum, 1)
            act.activation(RR[:, :], ps[0:B * TB, 0, 0:P], ACT.Copy).then_inc(row_copied, 1)

        @block.gpsimd
        def _(pool):
            with pool.Fori(0, CHUNKS) as c:
                own = Own(pool, pl, 2 * TB, c)
                def add_up(t):
                    s, e = t % 2, EX[:, t % 4, :, :]
                    pool.wait_ge(exp_done, TB * c + t + 1)
                    own.step(pool.tensor_tensor(SU[:, 0, s, :], e[:, 0, :], e[:, 1, :], ALU.add))
                    own.step(pool.tensor_tensor(SU[:, 0, s, :], SU[:, 0, s, :], e[:, 2, :], ALU.add))
                    pool.tensor_tensor(SU[:, 0, s, :], SU[:, 0, s, :], e[:, 3, :], ALU.add).then_inc(sum_done, 1)

                add_up(0)
                for t in range(TB):
                    if t + 1 < TB:
                        add_up(t + 1)
                    pool.wait_ge(inv_done, TB * c + t + 1)
                    e = EX[:, t % 4, :, :]
                    pool.tensor_tensor(e, e, bc(SU[:, 1, t % 2, :].unsqueeze(1), [P, B, CW]), ALU.mult)\
                        .then_inc(disp_ready, 1)
                own.end()

        @block.tensor
        def _(pe):
            prime(pe, y_psum)
            pe.wait_ge(loaded, 5 * 16)
            with pe.Fori(0, CHUNKS) as c:
                def logits(t):
                    if t >= 2:
                        pe.wait_ge(shifted, TB * c + t - 1)
                    for b in range(B):
                        at = b * N + t * P
                        ins = pe.matmul(logits_of(t % 2)[:, b, :], m.XNT[:, at:at + P],
                                        PHI[:, bass.ds(c * CW, CW)], start=True, stop=True)
                    ins.then_inc(l_psum, 1)

                logits(0)
                logits(1)
                pe.wait_ge(slots_ready, c + 1)
                for t in range(TB):
                    if t + 2 < TB:
                        logits(t + 2)
                    pe.wait_ge(disp_ready, TB * c + t + 1)
                    for b in range(B):
                        ins = pe.matmul(slots_bank[:, b, :], m.XN2[:, b * TB + t, :], EX[:, t % 4, b, :],
                                        start=t == 0 and b % 2 == 0, stop=t == TB - 1, skip_group_check=True)
                    ins.then_inc(slots_psum, 1)
                pe.wait_ge(slots_ready, c + 1 + 1)
                pe.wait_ge(w_loaded, 16 * c + 16)
                pe.wait_ge(y_ready, 2 * c + 1)
                for h in range(2):
                    for b in range(B):
                        for q in range(4):
                            n = 4 * h + q
                            ins = pe.matmul(ps[32 * q:32 * q + 32, 6 + h, b * D:(b + 1) * D],
                                            SL[:, b, n * NP_:(n + 1) * NP_], W[:, n, :], start=True, stop=True)
                    ins.then_inc(y_psum, 1)
            pe.wait_ge(row_ready, TB * CHUNKS)
            pe.wait_ge(y_ready, 2 * CHUNKS + 1)
            pe.transpose(ps[0:B * TB, 0, 0:P], RM[:, :, :].rearrange("p b t -> p (b t)"), m.ident[:, :])\
              .then_inc(row_psum, 1)
        part1.__exit__(None, None, None)

        MC = B * N // 512
        l2_psum, shifted2, exp2_done = sem("l2_psum"), sem("shifted2"), sem("exp2")
        acc_psum, out_ready, stored = sem("acc_psum"), sem("out_ready"), sem("stored")
        SH, CT = sb("sh", [P, 2, 512]), sb("ct", [P, 4, 512])
        DEN = sb("den", [P, 2, 4])
        block = ctx.enter_context(nc.Block())

        def acc(s, t):
            return ps[:, 4 + 2 * s + t // 2, (t % 2) * YW:(t % 2) * YW + YW]

        @block.sync
        def _(sp):
            with sp.Fori(0, MC) as c:
                sp.wait_ge(out_ready, c + 1 + 1)
                sp.dma_start(d.out[:, bass.ds(c * 4, 4), :], m.X[:, bass.ds(c * 4, 4), :]).then_inc(stored, 16)
            sp.wait_ge(stored, 16 * MC)

        @block.vector
        def _(v):
            prime(v, out_ready)
            with v.Fori(0, MC // 2) as cp:
                own = Own(v, vec, 8, cp + CHUNKS * 2)
                for s in range(2):
                    c = cp * 2 + s
                    for n in range(GROUPS):
                        v.wait_ge(l2_psum, c * GROUPS + n + 1)
                        if n >= 2:
                            v.wait_ge(exp2_done, c * GROUPS + n - 1)
                        v.tensor_tensor(SH[:, n % 2, :], ps[:, n % 4, :], RB[:, bass.ds(c * 512, 512)],
                                        ALU.subtract).then_inc(shifted2, 1)
                    v.wait_ge(acc_psum, (c + 1) * GROUPS)
                    for t in range(4):
                        own.mark(v.reciprocal(DEN[:, s, t:t + 1], acc(s, t)[:, D:D + 1]))
                    own.wait()
                    for t in range(4):
                        tile = m.X[:, bass.ds(c * 4 + t, 1), :].rearrange("p o d -> p (o d)")
                        ins = v.scalar_tensor_tensor(tile, acc(s, t)[:, 0:D], DEN[:, s, t:t + 1], tile,
                                                     ALU.mult, ALU.add)
                    ins.then_inc(out_ready, 1)
                own.end()

        @block.scalar
        def _(act):
            with act.Fori(0, MC) as c:
                for n in range(GROUPS):
                    act.wait_ge(shifted2, c * GROUPS + n + 1)
                    if n >= 4:
                        act.wait_ge(acc_psum, c * GROUPS + n - 3)
                    act.activation(CT[:, n % 4, :], SH[:, n % 2, :], ACT.Exp).then_inc(exp2_done, 1)

        @block.tensor
        def _(pe):
            with pe.Fori(0, MC // 2) as cp:
                for s in range(2):
                    c = cp * 2 + s

                    def logits2(n):
                        if n >= 4:
                            pe.wait_ge(shifted2, c * GROUPS + n - 3)
                        pe.matmul(ps[:, n % 4, :], PHI[:, n * P:(n + 1) * P], m.XNT[:, bass.ds(c * 512, 512)],
                                  start=True, stop=True).then_inc(l2_psum, 1)

                    for n in range(3):
                        logits2(n)
                    pe.wait_ge(out_ready, cp * 2 + 1)
                    for n in range(GROUPS):
                        pe.wait_ge(exp2_done, c * GROUPS + n + 1)
                        for t in range(4):
                            ins = pe.matmul(acc(s, t), CT[:, n % 4, t * P:(t + 1) * P],
                                            Y[:, n, bass.ds(cp, 1), :]
                                            .rearrange("p o e -> p (o e)"),
                                            start=n == 0 and t % 2 == 0, stop=n == GROUPS - 1, skip_group_check=True)
                        ins.then_inc(acc_psum, 1)
                        if n + 3 < GROUPS:
                            logits2(n + 3)


class Names:
    pass


def memory(nc, ctx):
    m = Names()

    def sb(name, shape, dt=fp32):
        return ctx.enter_context(nc.sbuf_tensor(name, shape, dt))

    m.X = sb("X", [P, TILES, D])
    m.ident, m.ident_bf = sb("ident", [P, P]), sb("ident_bf", [P, P], bf16)
    m.mask_qk, m.mask_kq = sb("mask_qk", [P, P], bf16), sb("mask_kq", [P, P], bf16)
    m.lower, m.half = sb("lower", [P, E, E]), sb("half", [P, TILES])
    m.Wqkv, m.Wr = sb("Wqkv", [P, 3 * D]), sb("Wr", [P, E])
    m.router_b, m.qk_scale = sb("router_b", [P, E]), sb("qk_scale", [P, 2 * H])
    m.XNT = sb("XNT", [P, B * N])
    m.QU, m.KU, m.VU = (sb(n, [P, U, TB, 32]) for n in ("QU", "KU", "VU"))
    m.LG, m.GT = sb("LG", [P, TILES, E]), sb("GT", [P, TILES, E])
    m.XN2 = m.KU[:, :, :, :].rearrange("p u t c -> p (u t c)").rearrange("p (a d) -> p a d", d=D)
    m.Wo, m.b2, m.b1 = sb("Wo", [P, D]), sb("b2", [E, D]), sb("b1", [P, E, HC])
    m.ps = ctx.enter_context(nc.psum_tensor("ps", [P, 8, 512], fp32))
    m.held = ctx.enter_context(nc.semaphore("held"))
    m.loaded = ctx.enter_context(nc.semaphore("loaded"))
    return m


def declare(nc, inputs):
    import numpy as np
    arr = {}
    d = Names()

    def give(name, a):
        arr["in_" + name] = np.ascontiguousarray(a)
        return nc.dram_tensor("in_" + name, a.shape, mybir.dt.from_np(a.dtype), kind="ExternalInput").ap()

    d.x = give("x", inputs["L0_attn_x"])
    d.wqkv = give("wqkv", np.concatenate([inputs["L0_attn_W" + c].T for c in "qkv"], axis=1))
    d.router_w = give("router_w", inputs["L0_ffn_router_w"])
    d.router_b = give("router_b", inputs["L0_ffn_router_b"])
    d.q_scale = give("q_scale", inputs["L0_attn_q_scale"])
    d.k_scale = give("k_scale", inputs["L0_attn_k_scale"])
    d.wo = give("wo", inputs["L0_attn_Wo"].T)
    d.w1, d.b1 = give("w1", inputs["L0_ffn_w1"]), give("b1", inputs["L0_ffn_b1"].reshape(E, HC, P).transpose(2, 0, 1))
    d.w2, d.b2 = give("w2", inputs["L0_ffn_w2"]), give("b2", inputs["L0_ffn_b2"])
    d.columns = give("columns", np.stack([inputs["L1_attn_" + name] for name in (
        "ln_g", "ln_b", "gamma_q", "beta_q", "gamma_k", "beta_k")], axis=1))
    d.w_in, d.b_out = give("w_in", inputs["L1_attn_W_in"]), give("b_out", inputs["L1_attn_b_out"])
    d.b_in = give("b_in", inputs["L1_attn_b_in"].reshape(5, P).T)
    d.b_v = give("b_v", inputs["L1_attn_b_in"][E1:2 * E1])
    d.w_out = give("w_out", inputs["L1_attn_W_out"])
    d.phi = give("phi", inputs["L1_ffn_phi"].reshape(D, SLOTS))
    d.w, d.b = give("w", inputs["L1_ffn_W"]), give("b", inputs["L1_ffn_b"])
    d.out = nc.dram_tensor("out", (B, N, D), fp32, kind="ExternalOutput").ap()\
        .rearrange("b (t p) d -> p (b t) d", p=P)
    return arr, d


def build(nc, d):
    with ExitStack() as ctx:
        m = memory(nc, ctx)
        setup(nc, m, d)
        project(nc, m)
        gates(nc, m)
        load_late(nc, m, d)
        attention(nc, m)
        mix_heads(nc, m)
        experts(nc, m, d)
        gated_attention(nc, m, d)
        soft_experts(nc, m, d)


def kernel(**inputs):
    import numpy as np
    import concourse.bacc as bacc
    from concourse.bass_utils import run_bass_kernel_spmd

    nc = bacc.Bacc("TRN2", target_bir_lowering=False, num_devices=1)
    arrays, d = declare(nc, {name: np.asarray(a) for name, a in inputs.items()})
    build(nc, d)
    return run_bass_kernel_spmd(nc, [arrays], core_ids=[0]).results[0]["out"]
```

```python
from contextlib import ExitStack

import concourse.bass as bass
from concourse import mybir

fp32 = mybir.dt.float32
f32r = mybir.dt.float32r
bf16 = mybir.dt.bfloat16
ALU = mybir.AluOpType
ACT = mybir.ActivationFunctionType
AX = mybir.AxisListType

P = 128
B, N, D = 4, 1024, 128
TB = N // P
TILES = B * TB
H, HD = 16, 8
HG = 4
G = H // HG
U = B * G
E, HID = 8, 512
HC = HID // P
NE, NP_ = 64, 32
SLOTS = NE * NP_
S1, E1 = 128, 256
EPS_LN, EPS_DIR = 1e-5, 1e-6
MASKED = -1e30


class Own:

    def __init__(self, eng, sem, per=0, turn=0):
        self.eng, self.sem, self.per, self.turn, self.n = eng, sem, per, turn, 0

    def mark(self, ins):
        self.n += 1
        ins.then_inc(self.sem, 1)
        return ins

    def wait(self):
        self.eng.wait_ge(self.sem, self.turn * self.per + self.n)

    def step(self, ins):
        self.mark(ins)
        self.wait()

    def end(self):
        assert self.n == self.per, self.n


def hold(eng, m):
    eng.sem_inc(m.held, 1)


def prime(eng, *semaphores):
    for s in semaphores:
        eng.sem_inc(s, 1)


def bc(ap, shape):
    return ap.to_broadcast(shape)


def normalise(nc, own, eng_wait_square, src, xc, sq, st, out, eps, squared, centred, var_sum, rstd):
    v = nc.vector
    own.step(v.tensor_reduce(st[:, 0, :], src, AX.X, ALU.add))
    own.step(v.tensor_scalar(st[:, 1, :], st[:, 0, :], -1.0 / D, None, ALU.mult))
    v.tensor_tensor(xc, src, bc(st[:, 1, :].unsqueeze(2), [P, TB, D]), ALU.add).then_inc(centred, 1)
    eng_wait_square()
    v.tensor_reduce(st[:, 2, :], sq, AX.X, ALU.add).then_inc(var_sum, 1)


def setup(nc, m, d):
    with ExitStack() as ctx:
        zeroed = ctx.enter_context(nc.semaphore("zeroed"))
        block = ctx.enter_context(nc.Block())

        @block.sync
        def _(sp):
            sp.dma_start(m.X[:, :, :], d.x.rearrange("b (t p) d -> p (b t) d", p=P)).then_inc(m.loaded, 16)
            sp.dma_start(m.Wqkv[:, :], d.wqkv).then_inc(m.loaded, 16)
            sp.dma_start(m.Wr[:, :], d.router_w).then_inc(m.loaded, 16)
            sp.dma_start(m.router_b[:, :], d.router_b.partition_broadcast(P)).then_inc(m.loaded, 16)
            sp.dma_start(m.qk_scale[:, 0:H], d.q_scale.partition_broadcast(P)).then_inc(m.loaded, 16)
            sp.dma_start(m.qk_scale[:, H:2 * H], d.k_scale.partition_broadcast(P)).then_inc(m.loaded, 16)
            sp.wait_ge(m.loaded, 6 * 16)

        @block.gpsimd
        def _(pool):
            pool.memset(m.ident[:, :], 0.0).then_inc(zeroed, 1)
            pool.memset(m.mask_q[:, :], 0.0).then_inc(zeroed, 1)
            pool.memset(m.lower[:, :, :], 0.0).then_inc(zeroed, 1)
            pool.memset(m.half[:, :], -0.5).then_inc(zeroed, 1)
            pool.wait_ge(zeroed, 4)
            for t in (m.ident,):
                pool.affine_select(out=t[:, :], in_=t[:, :], compare_op=ALU.not_equal, fill=1.0, base=0,
                                   pattern=[[-1, P]], channel_multiplier=1).then_inc(zeroed, 1)
            pool.affine_select(out=m.mask_q[:, 512 - P:512], in_=m.mask_q[:, 512 - P:512], compare_op=ALU.is_ge, fill=MASKED,
                               base=0, pattern=[[-1, P]], channel_multiplier=1).then_inc(zeroed, 1)
            pool.affine_select(out=m.lower[:, :, :], in_=m.lower[:, :, :], compare_op=ALU.is_ge, fill=1.0,
                               base=0, pattern=[[-1, E], [1, E]], channel_multiplier=0).then_inc(zeroed, 1)
            pool.wait_ge(zeroed, 7)


def project(nc, m):
    with ExitStack() as ctx:
        def sem(name):
            return ctx.enter_context(nc.semaphore("pj_" + name))

        def sb(name, shape, dt=fp32):
            return ctx.enter_context(nc.sbuf_tensor("pj_" + name, shape, dt))

        centred, squared, var_sum, rstd_ready = sem("centred"), sem("squared"), sem("var_sum"), sem("rstd")
        xn_ready, xt_psum, xt_ready = sem("xn_ready"), sem("xt_psum"), sem("xt_ready")
        copied = sem("copied")
        qkv_psum, silu_done, logits_psum = sem("qkv_psum"), sem("silu_done"), sem("logits_psum")
        n2_ready, r_ready, qk_scaled = sem("n2_ready"), sem("r_ready"), sem("qk_scaled")
        vec, pl = sem("vec"), sem("pool")
        XC, SQ = sb("xc", [P, TB, D]), sb("sq", [P, TB, D])
        XN, XT = sb("xn", [P, TB, D]), sb("xt", [P, N])
        ST = sb("st", [P, 4, TB])
        SQK, SQ2 = sb("sqk", [P, TB, 2 * D]), sb("sq2", [P, TB, 2 * D])
        N2, R, F = sb("n2", [P, TB, 2 * H]), sb("r", [P, TB, 2 * H]), sb("f", [P, TB, 2 * H])
        ps = m.ps
        block = ctx.enter_context(nc.Block())

        @block.vector
        def _(v):
            prime(v, qk_scaled)
            with v.Fori(0, B) as b:
                own = Own(v, vec, 8, b)
                xb = m.X[:, bass.ds(b * TB, TB), :]

                def square_wait():
                    v.wait_ge(squared, b + 1)

                normalise(nc, own, square_wait, xb, XC[:, :, :], SQ[:, :, :], ST, XN, EPS_LN,
                          squared, centred, var_sum, None)
                v.wait_ge(rstd_ready, b + 1)
                v.wait_ge(xt_psum, 2 * b + 1)
                v.tensor_tensor(XN[:, :, :], XC[:, :, :], bc(ST[:, 3, :].unsqueeze(2), [P, TB, D]),
                                ALU.mult).then_inc(xn_ready, 1)
                v.wait_ge(logits_psum, b + 1)
                v.tensor_tensor(m.LG[:, bass.ds(b * TB, TB), :],
                                ps[:, 6, 0:TB * E].rearrange("p (t e) -> p t e", e=E),
                                bc(m.router_b[:, :].unsqueeze(1), [P, TB, E]), ALU.add)
                v.wait_ge(silu_done, TB * (b + 1))
                own.step(v.tensor_tensor(SQ2[:, :, :], SQK[:, :, :], SQK[:, :, :], ALU.mult))
                v.tensor_reduce(N2[:, :, :], SQ2[:, :, :].rearrange("p t (h i) -> p t h i", i=HD), AX.X,
                                ALU.add).then_inc(n2_ready, 1)
                v.wait_ge(r_ready, b + 1)
                own.step(v.tensor_scalar(F[:, :, :], R[:, :, :], EPS_DIR, None, ALU.add))
                own.step(v.reciprocal(N2[:, :, :], F[:, :, :]))
                own.step(v.tensor_tensor(F[:, :, :], R[:, :, :], N2[:, :, :], ALU.mult))
                own.step(v.tensor_tensor(N2[:, :, :], F[:, :, :],
                                         bc(m.qk_scale[:, :].unsqueeze(1), [P, TB, 2 * H]), ALU.mult))
                for s, dst in ((0, m.QU), (1, m.KU)):
                    for g in range(G):
                        last = v.tensor_tensor(
                            dst[:, bass.ds(b * G + g, 1), :, :].rearrange("p o t (j i) -> p (o t) j i", i=HD),
                            SQK[:, :, s * D + g * 32:s * D + g * 32 + 32].rearrange("p t (j i) -> p t j i", i=HD),
                            bc(N2[:, :, s * H + g * HG:s * H + g * HG + HG].unsqueeze(3), [P, TB, HG, HD]),
                            ALU.mult)
                last.then_inc(qk_scaled, 1)
                own.mark(v.tensor_copy(ST[:, 1, 0:1], ST[:, 0, 0:1]))
                own.wait()
                own.end()

        @block.gpsimd
        def _(pool):
            prime(pool, copied)
            with pool.Fori(0, B) as b:
                own = Own(pool, pl, 1, b)
                pool.wait_ge(var_sum, b + 1)
                hold(pool, m)
                own.step(pool.tensor_scalar(ST[:, 2, :], ST[:, 2, :], 1.0 / D, EPS_LN, ALU.mult, ALU.add))
                pool.tensor_tensor(ST[:, 3, :], ST[:, 2, :], m.half[:, 0:TB], ALU.pow).then_inc(rstd_ready, 1)
                own.end()
                pool.wait_ge(xt_ready, 2 * b + 2)
                pool.tensor_copy(m.XNT[:, bass.ds(b * N, N)], XT[:, :]).then_inc(copied, 1)

        @block.scalar
        def _(act):
            with act.Fori(0, B) as b:
                act.wait_ge(centred, b + 1)
                act.activation(SQ[:, :, :], XC[:, :, :], ACT.Square).then_inc(squared, 1)
                act.wait_ge(copied, b + 1)
                for f in range(2):
                    act.wait_ge(xt_psum, 2 * b + f + 1 + 1)
                    act.activation(XT[:, f * 512:f * 512 + 512], ps[:, f, :], ACT.Copy).then_inc(xt_ready, 1)
                act.wait_ge(qk_scaled, b + 1)
                for t in range(TB):
                    act.wait_ge(qkv_psum, TB * b + t + 1)
                    act.activation(SQK[:, t, :], ps[:, 2 + t % 4, 0:2 * D], ACT.Silu)
                    act.activation(m.VU[:, bass.ds(b * G, G), t, :],
                                   ps[:, 2 + t % 4, 2 * D:3 * D].rearrange("p (g c) -> p g c", g=G),
                                   ACT.Silu).then_inc(silu_done, 1)
                act.wait_ge(n2_ready, b + 1)
                act.activation(R[:, :, :], N2[:, :, :], ACT.Sqrt).then_inc(r_ready, 1)

        @block.tensor
        def _(pe):
            prime(pe, xt_psum)
            with pe.Fori(0, B) as b:
                pe.wait_ge(xn_ready, b + 1)
                for t in range(TB):
                    ins = pe.transpose(ps[:, t // 4, (t % 4) * P:(t % 4 + 1) * P], XN[:, t, :], m.ident[:, :])
                    if t % 4 == 3:
                        ins.then_inc(xt_psum, 1)
                pe.wait_ge(xt_ready, 2 * b + 2)
                for t in range(TB):
                    last = pe.matmul(ps[:, 6, t * E:t * E + E], XT[:, t * P:(t + 1) * P], m.Wr[:, :],
                                     start=True, stop=True)
                last.then_inc(logits_psum, 1)
                for t in range(TB):
                    if t >= 4:
                        pe.wait_ge(silu_done, TB * b + t - 3)
                    pe.matmul(ps[:, 2 + t % 4, 0:3 * D], XT[:, t * P:(t + 1) * P], m.Wqkv[:, :],
                              start=True, stop=True).then_inc(qkv_psum, 1)


def gates(nc, m):
    with ExitStack() as ctx:
        vec, top, expd = (ctx.enter_context(nc.semaphore("gt_" + n)) for n in ("vec", "top", "exp"))
        cmp_ = ctx.enter_context(nc.sbuf_tensor("gt_cmp", [P, TILES, E, E], fp32))
        rank, tie = (ctx.enter_context(nc.sbuf_tensor("gt_" + n, [P, TILES, E], fp32)) for n in ("rank", "tie"))
        mx = ctx.enter_context(nc.sbuf_tensor("gt_mx", [P, TILES], fp32))
        block = ctx.enter_context(nc.Block())
        full = [P, TILES, E, E]

        @block.vector
        def _(v):
            own = Own(v, vec)
            LG = m.LG[:, :, :]
            other, this = bc(LG.unsqueeze(2), full), bc(LG.unsqueeze(3), full)
            own.step(v.tensor_tensor(cmp_[:, :, :, :], other, this, ALU.is_gt))
            own.step(v.tensor_reduce(rank[:, :, :], cmp_[:, :, :, :], AX.X, ALU.add))
            own.step(v.tensor_tensor(cmp_[:, :, :, :], other, this, ALU.is_equal))
            own.step(v.tensor_tensor(cmp_[:, :, :, :], cmp_[:, :, :, :],
                                     bc(m.lower[:, :, :].unsqueeze(1), full), ALU.mult))
            own.step(v.tensor_reduce(tie[:, :, :], cmp_[:, :, :, :], AX.X, ALU.add))
            own.step(v.tensor_tensor(rank[:, :, :], rank[:, :, :], tie[:, :, :], ALU.add))
            own.step(v.tensor_scalar(rank[:, :, :], rank[:, :, :], 1.5, None, ALU.is_lt))
            own.step(v.tensor_reduce(mx[:, :], LG, AX.X, ALU.max))
            v.tensor_tensor(tie[:, :, :], LG, bc(mx[:, :].unsqueeze(2), [P, TILES, E]),
                            ALU.subtract).then_inc(top, 1)
            v.wait_ge(expd, 1)
            own.step(v.tensor_tensor(tie[:, :, :], m.GT[:, :, :], rank[:, :, :], ALU.mult))
            own.step(v.tensor_reduce(mx[:, :], tie[:, :, :], AX.X, ALU.add))
            own.step(v.reciprocal(mx[:, :], mx[:, :]))
            own.step(v.tensor_tensor(m.GT[:, :, :], tie[:, :, :], bc(mx[:, :].unsqueeze(2), [P, TILES, E]),
                                     ALU.mult))

        @block.scalar
        def _(act):
            act.wait_ge(top, 1)
            act.activation(m.GT[:, :, :], tie[:, :, :], ACT.Exp).then_inc(expd, 1)


P2_UNITS = [(k, c) for half in (0, 1) for k in range(TB) for c in (2 * half, 2 * half + 1) if c >= k // 2]
P1_UNITS = ([(i, 0, j) for j in range(HG) for i in (0, 3, 1, 2)]
            + [(i, c, j) for i in range(4, TB) for j in range(HG) for c in (0, 1)])
N2U, N1U = len(P2_UNITS), len(P1_UNITS)
HALF2 = sum(c < 2 for _, c in P2_UNITS)
HALF1 = sum(i < 4 for i, _, _ in P1_UNITS)
DIAGONAL = [q for q, (k, c) in enumerate(P2_UNITS) if c == k // 2]
PV_LAG = 2
FREE_A = 1 + max(q for q, (k, _) in enumerate(P2_UNITS) if k < 4)
OB1, Q2B, OB0, Q2A, K0, K1, Q0, Q1 = range(8)
FILL_AT = {3: OB1, 4: Q2B, 9: OB0, 10: Q2A, 12: K0, 13: K1, 15: Q0, 17: Q1}
AT_FILL = {f: q for q, f in FILL_AT.items()}


def p1_upto(q):
    return (N1U * (q + 1) + N2U // 2) // N2U


def p1_before_fill(q):
    return p1_upto(q) - 1


PRO_FILLS = 9


def attention(nc, m):
    with ExitStack() as ctx:
        def sem(name):
            return ctx.enter_context(nc.semaphore("at_" + name))

        def sb(name, shape, dt=fp32):
            return ctx.enter_context(nc.sbuf_tensor("at_" + name, shape, dt))

        kq_staged, v_staged = sem("kq_staged"), sem("v_staged")
        ktx_loaded = [sem("ktx_loaded_a"), sem("ktx_loaded_b")]
        filled, emptied = sem("filled"), sem("emptied")
        p1_psum, max_done, max_staged = sem("p1_psum"), sem("max_done"), sem("max_staged")
        masked = sem("masked_pt")
        s2_psum, exp_done, pv_done = sem("s2_psum"), sem("exp_done"), sem("pv_done")
        o_copied, norm_done = sem("o_copied"), sem("norm_done")
        vec, pl, zeroed = sem("vec"), sem("pool"), sem("zeroed")
        KP, QP = sb("kp", [P, TB, HG, 32]), sb("qp", [P, 2, TB, HG, 32])
        VW = sb("vw", [P, 2, TB, HG, 32])
        KT = sb("kt", [P, N], f32r)
        KTX = sb("ktx", [P, 2, HG, N], f32r)
        QT1, QT2 = sb("qt1", [P, 2, N], f32r), sb("qt2", [P, 2, N], f32r)
        PT = sb("pt", [P, 4, HG, 256])
        OT = sb("ot", [P, 512])
        MX, NM = sb("mx", [P, TB, 2, HG]), sb("nm", [P, TB, HG])
        DEN = sb("den", [P, 4, HG])
        MASKED_S = sb("masked", [P, 2, 512], bf16)
        ps = m.ps
        P2B = [ps[:, 2 * s:2 * s + 2, :].rearrange("p b (h n) -> p (b h) n", h=2) for s in range(2)]
        P1B = [ps[:, 4 + s, :] for s in range(2)]
        OB, TR = ps[:, 6, :], ps[:, 7, :]
        block = ctx.enter_context(nc.Block())

        def fills(u, at, left_out=0):
            return u * 8 + (at + PRO_FILLS - left_out)

        def steps(eng, step, before, after):
            before()
            step(0, 0)
            step(1, 1)
            with eng.Fori(0, (U - 4) // 2) as i:
                step(i * 2 + 2, 0)
                step(i * 2 + 3, 1)
            step(U - 2, 0)
            step(U - 1, 1)
            after()

        def is_(u, n):
            return isinstance(u, int) and u == n

        def has(u, d):
            return not isinstance(u, int) or u + d < U

        @block.sync
        def _(sp):
            def load(half, par):
                cols = slice(512 * half, 512 * half + 512)
                for j in range(HG):
                    sp.dma_start(KTX[32 * j:32 * j + 32, par, j, cols].bitcast(fp32),
                                 KT[32 * j:32 * j + 32, cols].bitcast(fp32)).then_inc(ktx_loaded[half], 16)

            def before():
                sp.wait_ge(zeroed, 1)
                for v in (0, 1):
                    for half in (0, 1):
                        sp.wait_ge(emptied, 4 * v + half + 1)
                        load(half, v)

            def step(u, par):
                if has(u, 2):
                    sp.wait_ge(emptied, fills(u, K0))
                    hold(sp, m)
                    sp.wait_ge(s2_psum, u * N2U + FREE_A)
                    hold(sp, m)
                    load(0, par)
                    sp.wait_ge(emptied, fills(u, K1))
                    hold(sp, m)
                    sp.wait_ge(s2_psum, u * N2U + N2U)
                    hold(sp, m)
                    load(1, par)

            steps(sp, step, before, lambda: None)

        @block.gpsimd
        def _(pool):
            def round_split(own, src, hi, hi2, lo):
                own.mark(pool.tensor_copy(hi.bitcast(f32r), src))
                pool.tensor_copy(hi2.bitcast(f32r), src)
                own.wait()
                hold(pool, m)
                return pool.tensor_tensor(lo.bitcast(f32r), src, hi, ALU.subtract)

            def unit_of(t, v):
                return t[:, bass.ds(v, 1), :, :].rearrange("p o t (j i) -> p (o t) j i", i=HD)

            def stage_kq(v, par, count):
                own = Own(pool, pl, 2, count)
                q = QP[:, par, :, :, :]
                round_split(own, unit_of(m.KU, v), KP[:, :, :, 0:8], KP[:, :, :, 8:16], KP[:, :, :, 16:24])
                round_split(own, unit_of(m.QU, v), q[:, :, :, 0:8], q[:, :, :, 16:24], q[:, :, :, 8:16])
                pool.memset(q[:, :, :, 24:26], 0.0).then_inc(kq_staged, 1)

            def stage_v(v, par):
                pool.tensor_copy(VW[:, par, :, :, 0:8], unit_of(m.VU, v)).then_inc(v_staged, 1)

            def before():
                for t in (KP[:, :, :, :], QP[:, :, :, :, :], VW[:, :, :, :, :], KTX[:, :, :, :].bitcast(fp32)):
                    last = pool.memset(t, 0.0)
                last.then_inc(zeroed, 1)
                pool.wait_ge(zeroed, 1)
                pool.memset(KP[:, :, :, 24:26], 1.0)
                pool.memset(VW[:, :, :, :, 8:9], 1.0)
                stage_kq(0, 0, 0)
                stage_v(0, 0)
                pool.wait_ge(filled, 4)
                stage_kq(1, 1, 1)

            def mask(u, q):
                k, _ = P2_UNITS[q]
                pool.wait_ge(exp_done, u * N2U + q + 1)
                hold(pool, m)
                tile = PT[:, q % 4, :, (k % 2) * P:(k % 2 + 1) * P]
                pool.affine_select(out=tile, in_=tile, compare_op=ALU.is_ge, fill=0.0, base=0,
                                   pattern=[[0, HG], [1, P]], channel_multiplier=-1).then_inc(masked, 1)

            def step(u, par):
                for q in DIAGONAL:
                    if q == DIAGONAL[4]:
                        if has(u, 2):
                            pool.wait_ge(filled, fills(u, Q2B))
                            stage_kq(u + 2, par, u + 2)
                        if has(u, 1):
                            pool.wait_ge(pv_done, u * N2U + 1)
                            stage_v(u + 1, 1 - par)
                    mask(u, q)

            steps(pool, step, before, lambda: None)

        @block.scalar
        def _(act):
            def copy_out(dst, count):
                act.wait_ge(filled, count)
                act.activation(dst, TR, ACT.Copy).then_inc(emptied, 1)

            def before():
                for v in (0, 1):
                    for f in range(2):
                        if v == 1:
                            act.wait_ge(ktx_loaded[f], HG * 16)
                        copy_out(KT[:, f * 512:f * 512 + 512], 4 * v + f + 1)
                    for f in range(2):
                        copy_out(QT1[:, v, f * 512:f * 512 + 512], 4 * v + f + 3)
                copy_out(QT2[:, 0, 0:512], 9)

            def copy_o(u, half):
                act.wait_ge(pv_done, u * N2U + (N2U if half else HALF2))
                act.activation(OT[:, :], OB, ACT.Copy).then_inc(o_copied, 1)

            def step(u, par):
                less = 4 if is_(u, U - 1) else 0
                for q, (k, c) in enumerate(P2_UNITS):
                    if q == PV_LAG and not is_(u, 0):
                        copy_o(u - 1, 1)
                    if q == HALF2 + PV_LAG:
                        copy_o(u, 0)
                    act.wait_ge(s2_psum, u * N2U + q + 1)
                    if q >= 4 or not is_(u, 0):
                        act.wait_ge(pv_done, u * N2U + (q - 3))
                    lo = 128 if k % 2 and c == k // 2 else 0
                    act.activation(PT[:, q % 4, :, lo:256] if lo else PT[:, q % 4, :, :],
                                   P2B[q % 2][:, :, lo:256] if lo else P2B[q % 2], ACT.Exp)\
                       .then_inc(exp_done, 1)
                    f = FILL_AT.get(q)
                    if f == Q2B:
                        copy_out(QT2[:, par, 512:1024], fills(u, Q2B, less))
                    if f == Q2A and has(u, 1):
                        copy_out(QT2[:, 1 - par, 0:512], fills(u, Q2A))
                    if f in (K0, K1) and has(u, 2):
                        copy_out(KT[:, (f - K0) * 512:(f - K0) * 512 + 512], fills(u, f))
                    if f in (Q0, Q1) and has(u, 2):
                        copy_out(QT1[:, par, (f - Q0) * 512:(f - Q0) * 512 + 512], fills(u, f))

            steps(act, step, before, lambda: copy_o(U - 1, 1))

        @block.vector
        def _(v):
            def reduce(un, n):
                i, c, j = P1_UNITS[n]
                w = min(512, (i + 1) * P - c * 512)
                v.wait_ge(p1_psum, un * N1U + n + 1)
                if c == i // 4:
                    hold(v, m)
                if c == i // 4:
                    v.tensor_tensor_reduce(out=MASKED_S[:, n % 2, 0:w], in0=P1B[n % 2][:, 0:w], in1=m.mask_q[:, 512 - w:512],
                                           scale=1.0, scalar=-3e38, op0=ALU.add, op1=ALU.max,
                                           accum_out=MX[:, i, c, j:j + 1]).then_inc(max_done, 1)
                else:
                    v.tensor_reduce(MX[:, i, c, j:j + 1], P1B[n % 2][:, 0:w], AX.X, ALU.max).then_inc(max_done, 1)

            def stage_max(own, un, par, half):
                rows = slice(4 * half, 4 * half + 4)
                v.wait_ge(max_done, un * N1U + (N1U if half else HALF1))
                src = MX[:, rows, 0, :]
                if half:
                    own.step(v.tensor_tensor(MX[:, rows, 0, :], src, MX[:, rows, 1, :], ALU.max))
                own.step(v.tensor_scalar(NM[:, rows, :], src, -1.0, None, ALU.mult))
                hi, lo = (QP[:, par, rows, :, c:c + 1].rearrange("p t j o -> p t (j o)") for c in (24, 25))
                own.step(v.tensor_scalar(hi.bitcast(f32r), NM[:, rows, :], 1.0, None, ALU.mult))
                v.tensor_tensor(lo.bitcast(f32r), NM[:, rows, :], hi, ALU.subtract).then_inc(max_staged, 1)

            def divide(own, u, half, count):
                v.wait_ge(filled, count)
                t4 = TR.rearrange("p (t j c) -> p t j c", t=4, j=HG)
                own.step(v.reciprocal(DEN[:, :, :], t4[:, :, :, 8:9].rearrange("p t j o -> p t (j o)")))
                v.tensor_tensor(
                    m.QU[:, bass.ds(u, 1), 4 * half:4 * half + 4, :].rearrange("p o t (j i) -> p (o t) j i", i=HD),
                    t4[:, :, :, 0:8], bc(DEN[:, :, :].unsqueeze(3), [P, 4, HG, HD]), ALU.mult)\
                 .then_inc(emptied, 1)

            PER = 7

            def before():
                own = Own(v, vec)
                for n in range(N1U):
                    reduce(0, n)
                    if n == HALF1 - 1:
                        stage_max(own, 0, 0, 0)
                stage_max(own, 0, 0, 1)
                assert own.n == 5

            def step(u, par):
                less = 4 if is_(u, U - 1) else 0
                own = Own(v, vec, 1, u * PER + 5 - (0 if is_(u, 0) else 1))
                for n in range(N1U):
                    if n == p1_before_fill(AT_FILL[OB1]) and not is_(u, 0):
                        divide(own, u - 1, 1, fills(u, OB1, less))
                    if n == HALF1 and has(u, 1):
                        stage_max(own, u + 1, 1 - par, 0)
                    if n == p1_before_fill(AT_FILL[OB0]):
                        divide(own, u, 0, fills(u, OB0, less))
                    if has(u, 1):
                        reduce(u + 1, n)
                if has(u, 1):
                    stage_max(own, u + 1, 1 - par, 1)

            def after():
                own = Own(v, vec, 1, (U - 1) * PER + 5 - 1 + 2)
                divide(own, U - 1, 1, fills(U, OB1, 9))

            steps(v, step, before, after)

        @block.tensor
        def _(pe):
            def fill(what, in_of, count):
                if count > 1:
                    pe.wait_ge(emptied, count - 1)
                for t in range(4):
                    ins = pe.transpose(TR[:, t * P:(t + 1) * P], in_of(t), m.ident[:, :])
                ins.then_inc(filled, 1)

            def staged(tile, half):
                return lambda t: tile[:, 4 * half + t, :, :].rearrange("p j c -> p (j c)")

            def pass1(un, par, n):
                i, c, j = P1_UNITS[n]
                w = max(256, min(512, (i + 1) * P - c * 512))
                if not (is_(un, 0) and n < 2):
                    pe.wait_ge(max_done, un * N1U + (n - 1))
                pe.matmul(P1B[n % 2][:, 0:w], QT1[:, par, i * P:(i + 1) * P],
                          KTX[:, par, j, c * 512:c * 512 + w], start=True, stop=True).then_inc(p1_psum, 1)

            def scores2(u, par, q, pass1_steps):
                k, c = P2_UNITS[q]
                if not (is_(u, 0) and q < 2):
                    pe.wait_ge(exp_done, u * N2U + (q - 1))
                for j in range(HG):
                    if j == 2:
                        pass1_steps()
                    ins = pe.matmul(P2B[q % 2][:, j, :], KTX[:, par, j, k * P:(k + 1) * P],
                                    QT2[:, par, c * 256:c * 256 + 256], start=True, stop=True)
                ins.then_inc(s2_psum, 1)

            def values(u, par, q):
                k, c = P2_UNITS[q]
                if q in DIAGONAL:
                    pe.wait_ge(masked, u * len(DIAGONAL) + DIAGONAL.index(q) + 1)
                else:
                    pe.wait_ge(exp_done, u * N2U + q + 1)
                if q == 0:
                    pe.wait_ge(v_staged, u + 1)
                if q in (0, HALF2) and not (is_(u, 0) and q == 0):
                    pe.wait_ge(o_copied, u * 2 + (1 if q else 0))
                lo = 128 if k % 2 and c == k // 2 else 0
                at = (c % 2) * 256 + lo
                for j in range(HG):
                    ins = pe.matmul(OB[32 * j:32 * j + 32, at:at + 256 - lo], VW[:, par, k, j, :],
                                    PT[:, q % 4, j, lo:256], start=q in (0, HALF2),
                                    stop=q in (HALF2 - 1, N2U - 1), skip_group_check=True)
                ins.then_inc(pv_done, 1)

            def before():
                for v in (0, 1):
                    pe.wait_ge(kq_staged, v + 1)
                    for f in range(2):
                        fill("k", staged(KP, f), 4 * v + f + 1)
                    for f in range(2):
                        fill("q", staged(QP[:, v, :, :, :], f), 4 * v + f + 3)
                pe.wait_ge(emptied, 4)
                for n in range(N1U):
                    if n in (0, HALF1):
                        pe.wait_ge(ktx_loaded[n // HALF1], HG * 16)
                    pass1(0, 0, n)
                    if n == HALF1 + 8:
                        pe.wait_ge(max_staged, 1)
                        fill("q2", staged(QP[:, 0, :, :, :], 0), 9)

            def step(u, par):
                less = 4 if is_(u, U - 1) else 0
                issued = 0

                def pass1_steps(upto):
                    nonlocal issued
                    while has(u, 1) and issued < upto:
                        if issued in (0, HALF1):
                            pe.wait_ge(ktx_loaded[issued // HALF1], (u + 2) * (HG * 16))
                            if not is_(u, 0):
                                pe.wait_ge(emptied, fills(u - 1, Q1 if issued else Q0))
                        pass1(u + 1, 1 - par, issued)
                        issued += 1

                for q in range(N2U):
                    if q == 0:
                        pe.wait_ge(emptied, 9 if is_(u, 0) else fills(u - 1, Q2A))
                    if q == HALF2:
                        pe.wait_ge(emptied, fills(u, Q2B, less))
                    scores2(u, par, q, lambda: pass1_steps(p1_upto(q) - 2))
                    pass1_steps(p1_before_fill(q))
                    f = FILL_AT.get(q)
                    if f == OB1 and not is_(u, 0):
                        pe.wait_ge(o_copied, u * 2)
                        fill("o", lambda t: OT[:, t * P:(t + 1) * P], fills(u, OB1, less))
                    if f == Q2B:
                        pe.wait_ge(max_staged, u * 2 + 2)
                        fill("q2", staged(QP[:, par, :, :, :], 1), fills(u, Q2B, less))
                    if f == OB0:
                        pe.wait_ge(o_copied, u * 2 + 1)
                        fill("o", lambda t: OT[:, t * P:(t + 1) * P], fills(u, OB0, less))
                    if f == Q2A and has(u, 1):
                        pe.wait_ge(max_staged, u * 2 + 3)
                        fill("q2", staged(QP[:, 1 - par, :, :, :], 0), fills(u, Q2A))
                    if f in (K0, K1, Q0, Q1) and has(u, 2):
                        if f == K0:
                            pe.wait_ge(kq_staged, u + 3)
                        tile = KP if f in (K0, K1) else QP[:, par, :, :, :]
                        fill("kq", staged(tile, f % 2), fills(u, f))
                    if q >= PV_LAG:
                        values(u, par, q - PV_LAG)
                    elif not is_(u, 0):
                        values(u - 1, 1 - par, N2U + q - PV_LAG)
                    pass1_steps(p1_upto(q))

            def after():
                for q in range(N2U - PV_LAG, N2U):
                    values(U - 1, 1, q)
                pe.wait_ge(o_copied, 2 * U)
                fill("o", lambda t: OT[:, t * P:(t + 1) * P], fills(U, OB1, 9))

            steps(pe, step, before, after)


def mix_heads(nc, m):
    with ExitStack() as ctx:
        def sem(name):
            return ctx.enter_context(nc.semaphore("mh_" + name))

        copied, gathered, turned, out_ready, added = (sem(n) for n in ("copied", "gathered", "turned", "out", "added"))
        AW = ctx.enter_context(nc.sbuf_tensor("mh_aw", [P, TB, G, 32], fp32))
        AT = ctx.enter_context(nc.sbuf_tensor("mh_at", [P, N], fp32))
        GW = ctx.enter_context(nc.sbuf_tensor("mh_gw", [P, TB, E], fp32))
        GTT = ctx.enter_context(nc.sbuf_tensor("mh_gt", [E, N], fp32))
        ps = m.ps
        block = ctx.enter_context(nc.Block())

        @block.vector
        def _(v):
            prime(v, added)
            with v.Fori(0, B) as b:
                v.wait_ge(gathered, 4 * b + 1)
                v.tensor_copy(AW[:, :, :, :].rearrange("p t g c -> p g t c"), m.QU[:, bass.ds(b * G, G), :, :])
                v.tensor_copy(GW[:, :, :], m.GT[:, bass.ds(b * TB, TB), :]).then_inc(copied, 1)
                for f in range(2):
                    v.wait_ge(out_ready, 2 * b + f + 1)
                    xs = m.X[:, bass.ds(b * TB + 4 * f, 4), :]
                    v.tensor_tensor(xs, xs, ps[:, 4 + f, :].rearrange("p (t d) -> p t d", t=4), ALU.add)\
                     .then_inc(added, 1)

        @block.scalar
        def _(act):
            with act.Fori(0, B) as b:
                for f in range(2):
                    act.wait_ge(gathered, 4 * b + f + 1 + 1)
                    act.activation(AT[:, f * 512:f * 512 + 512], ps[:, f, :], ACT.Copy).then_inc(turned, 1)
                for f in range(2):
                    act.wait_ge(gathered, 4 * b + f + 3 + 1)
                    act.activation(GTT[:, f * 512:f * 512 + 512], ps[0:E, 2 + f, :], ACT.Copy).then_inc(turned, 1)

        @block.tensor
        def _(pe):
            prime(pe, gathered)
            with pe.Fori(0, B) as b:
                pe.wait_ge(copied, b + 1)
                for t in range(TB):
                    ins = pe.transpose(ps[:, t // 4, (t % 4) * P:(t % 4 + 1) * P], AW[:, t, :, :].rearrange("p g c -> p (g c)"), m.ident[:, :])
                    if t % 4 == 3:
                        ins.then_inc(gathered, 1)
                for t in range(TB):
                    ins = pe.transpose(ps[0:E, 2 + t // 4, (t % 4) * P:(t % 4 + 1) * P], GW[:, t, :], m.ident[:, :])
                    if t % 4 == 3:
                        ins.then_inc(gathered, 1)
                pe.wait_ge(turned, 4 * b + 4)
                for t in range(TB):
                    if t % 4 == 0:
                        pe.wait_ge(added, 2 * b + 1)
                    out = ps[:, 4 + t // 4, (t % 4) * P:(t % 4 + 1) * P]
                    pe.matmul(out, AT[:, t * P:(t + 1) * P], m.Wo[:, :], start=True, stop=False)
                    ins = pe.matmul(out, GTT[:, t * P:(t + 1) * P], m.b2[:, :], start=False, stop=True)
                    if t % 4 == 3:
                        ins.then_inc(out_ready, 1)


def experts(nc, m, d):
    CH = B * N // 512
    with ExitStack() as ctx:
        def sem(name):
            return ctx.enter_context(nc.semaphore("ex_" + name))

        loaded = [sem("loaded0"), sem("loaded1")]
        h_psum, h_ready, y_psum, added = (sem(n) for n in ("h_psum", "h_ready", "y_psum", "added"))
        W1 = ctx.enter_context(nc.sbuf_tensor("ex_w1", [P, 2, HID], fp32))
        W2 = ctx.enter_context(nc.sbuf_tensor("ex_w2", [P, 2, HC, D], fp32))
        HT = ctx.enter_context(nc.sbuf_tensor("ex_ht", [P, 2, HC, 512], fp32))
        ps = m.ps
        block = ctx.enter_context(nc.Block())

        @block.sync
        def _(sp):
            def load(s, e):
                sp.dma_start(W1[:, s, :], d.w1[e, :, :]).then_inc(loaded[s], 16)
                sp.dma_start(W2[:, s, :, :], d.w2[e, :, :].rearrange("(c p) d -> p c d", p=P))\
                  .then_inc(loaded[s], 16)

            with sp.Fori(0, E // 2) as ep:
                load(0, ep * 2)
                sp.wait_ge(y_psum, ep * (2 * CH) + 1)
                load(1, ep * 2 + 1)
                sp.wait_ge(y_psum, ep * (2 * CH) + CH + 1)
                hold(sp, m)

        @block.scalar
        def _(act):
            with act.Fori(0, E) as e:
                with act.Fori(0, CH // 2) as cp:
                    for s in range(2):
                        n = e * CH + cp * 2 + s
                        for hc in range(HC):
                            act.wait_ge(h_psum, n * HC + hc + 1)
                            hold(act, m)
                            act.activation(HT[:, s, hc, :], ps[:, hc, :], ACT.Relu,
                                           bias=m.b1[:, bass.ds(e, 1), hc]).then_inc(h_ready, 1)

        @block.vector
        def _(v):
            prime(v, added)
            with v.Fori(0, E) as e:
                with v.Fori(0, CH // 2) as cp:
                    for s in range(2):
                        n = e * CH + cp * 2 + s
                        v.wait_ge(y_psum, n + 1 + 1)
                        for t in range(4):
                            tile = m.X[:, bass.ds(cp * 8 + (4 * s + t), 1), :].rearrange("p o d -> p (o d)")
                            last = v.scalar_tensor_tensor(
                                tile, ps[:, 4 + s, t * P:(t + 1) * P],
                                m.GT[:, bass.ds(cp * 8 + (4 * s + t), 1), bass.ds(e, 1)]
                                 .rearrange("p a b -> p (a b)"), tile, ALU.mult, ALU.add)
                        last.then_inc(added, 1)

        @block.tensor
        def _(pe):
            prime(pe, y_psum)
            with pe.Fori(0, E // 2) as ep:
                for w in range(2):
                    pe.wait_ge(loaded[w], ep * 32 + 32)
                    hold(pe, m)
                    with pe.Fori(0, CH // 2) as cp:
                        n = ep * (2 * CH) + w * CH + cp * 2
                        for s in range(2):
                            for hc in range(HC):
                                if s == 1:
                                    pe.wait_ge(h_ready, n * HC + hc + 1)
                                pe.matmul(ps[:, hc, :], W1[:, w, hc * P:(hc + 1) * P],
                                          m.XNT[:, bass.ds((cp * 2 + s) * 512, 512)],
                                          start=True, stop=True).then_inc(h_psum, 1)
                        for s in range(2):
                            pe.wait_ge(h_ready, (n + s + 1) * HC)
                            pe.wait_ge(added, n + 1)
                            for t in range(4):
                                for hc in range(HC):
                                    ins = pe.matmul(ps[:, 4 + s, t * P:(t + 1) * P],
                                                    HT[:, s, hc, t * P:(t + 1) * P], W2[:, w, hc, :],
                                                    start=hc == 0, stop=hc == HC - 1)
                            ins.then_inc(y_psum, 1)


def load_late(nc, m, d):
    with ExitStack() as ctx:
        block = ctx.enter_context(nc.Block())

        @block.sync
        def _(sp):
            sp.dma_start(m.Wo[:, :], d.wo).then_inc(m.loaded, 16)
            sp.dma_start(m.b2[:, :], d.b2).then_inc(m.loaded, 16)
            sp.dma_start(m.b1[:, :, :], d.b1).then_inc(m.loaded, 16)
            sp.wait_ge(m.loaded, 9 * 16)


def gated_attention(nc, m, d):
    with ExitStack() as ctx:
        def sem(name):
            return ctx.enter_context(nc.semaphore("ga_" + name))

        def sb(name, shape, dt=fp32):
            return ctx.enter_context(nc.sbuf_tensor("ga_" + name, shape, dt))

        ps = m.ps
        loaded = sem("loaded")
        centred, squared, var_sum, rstd = sem("centred"), sem("squared"), sem("var_sum"), sem("rstd")
        xn_ready, turned_psum, turned = sem("xn_ready"), sem("turned_psum"), sem("turned")
        xnn_ready, kept, residual = sem("xnn_ready"), sem("kept"), sem("residual")
        z_psum, z_ready, qk_ready = sem("z_psum"), sem("z_ready"), sem("qk_ready")
        uv_psum, uv_ready = sem("uv_psum"), sem("uv_ready")
        s_psum, relu_done, a_ready, av_psum, o_ready = sem("s_psum"), sem("relu"), sem("a"), sem("av"), sem("o")
        out_psum, out_added = sem("out_psum"), sem("out_added")
        vec, pl = sem("vec"), sem("pool")
        WIN, BIN = sb("win", [P, 5 * P]), sb("bin", [P, 5])
        BV, ONE = sb("bv", [1, E1]), sb("one", [1, P])
        WOUT, BOUT = sb("wout", [P, 2, D]), sb("bout", [P, D])
        COL = sb("col", [P, 6])
        XC, SQ, XN, XNN = (sb(n, [P, TB, D]) for n in ("xc", "sq", "xn", "xnn"))
        ST = sb("st", [P, 2, 4, TB])
        XT = sb("xt", [P, N])
        Z, Q, K = (sb(n, [P, N]) for n in ("z", "q", "k"))
        UT, V = sb("ut", [P, 2, N]), sb("v", [P, TB, E1])
        RL, A = sb("rl", [P, 2, 512]), sb("a", [P, 2, 512])
        OG = sb("og", [P, 2, 512])
        block = ctx.enter_context(nc.Block())

        @block.sync
        def _(sp):
            for dst, src in ((WIN[:, :], d.w_in), (BIN[:, :], d.b_in),
                             (BV[:, :], d.b_v.unsqueeze(0)),
                             (WOUT[:, :, :], d.w_out.rearrange("(c p) d -> p c d", p=P)),
                             (BOUT[:, :], d.b_out.partition_broadcast(P)),
                             (COL[:, :], d.columns)):
                sp.dma_start(dst, src).then_inc(loaded, 16)

        LOADS = 6 * 16

        @block.vector
        def _(v):
            v.memset(ONE[:, :], 1.0)
            v.wait_ge(loaded, LOADS)
            with v.Fori(0, B) as b:
                own = Own(v, vec, 4, b)
                xb = m.X[:, bass.ds(b * TB, TB), :]
                for k, (src, out, ready) in enumerate(((xb, XN, xn_ready), (XN[:, :, :], XNN, xnn_ready))):
                    st = ST[:, k, :, :]

                    def square_wait():
                        v.wait_ge(squared, 2 * b + k + 1)

                    if k == 1:
                        v.wait_ge(xn_ready, b + 1)
                    normalise(nc, own, square_wait, src, XC[:, :, :], SQ[:, :, :], st, out, EPS_LN,
                              squared, centred, var_sum, rstd)
                    v.wait_ge(rstd, 2 * b + k + 1)
                    if k == 0:
                        v.wait_ge(kept, b + 1)
                        v.wait_ge(turned_psum, 4 * b + 1)
                    v.tensor_tensor(out[:, :, :], XC[:, :, :], bc(st[:, 3, :].unsqueeze(2), [P, TB, D]),
                                    ALU.mult).then_inc(ready, 1)
                own.end()
                for f in range(2):
                    v.wait_ge(turned_psum, 4 * b + f + 3 + 1)
                    v.tensor_scalar(XT[:, f * 512:f * 512 + 512], ps[:, 2 + f, :], COL[:, 0:1], COL[:, 1:2],
                                    ALU.mult, ALU.add).then_inc(turned, 1)
                v.wait_ge(z_ready, 2 * b + 2)
                v.tensor_scalar(Q[:, :], Z[:, :], COL[:, 2:3], COL[:, 3:4], ALU.mult, ALU.add)
                v.tensor_scalar(K[:, :], Z[:, :], COL[:, 4:5], COL[:, 5:6], ALU.mult, ALU.add).then_inc(qk_ready, 1)
                for c in range(2):
                    for kk in range(TB):
                        n = 2 * TB * b + (c * TB + kk)
                        v.wait_ge(relu_done, n + 1)
                        if kk >= 2:
                            v.wait_ge(av_psum, n - 1)
                        v.tensor_tensor(A[:, kk % 2, :], RL[:, kk % 2, :], RL[:, kk % 2, :], ALU.mult)\
                         .then_inc(a_ready, 1)
                    v.wait_ge(av_psum, 2 * TB * b + (c + 1) * TB)
                    for e in range(2):
                        ins = v.tensor_tensor(OG[:, e, :], ps[:, 4 + e, :], UT[:, e, c * 512:c * 512 + 512], ALU.mult)
                    ins.then_inc(o_ready, 1)
                    v.wait_ge(out_psum, 2 * b + c + 1)
                    v.wait_ge(residual, b + 1)
                    xs = m.X[:, bass.ds(b * TB + 4 * c, 4), :]
                    v.tensor_tensor(xs, xs, ps[:, 6, :].rearrange("p (t d) -> p t d", t=4), ALU.add)\
                     .then_inc(out_added, 1)

        @block.gpsimd
        def _(pool):
            prime(pool, kept)
            pool.wait_ge(loaded, LOADS)
            with pool.Fori(0, B) as b:
                own = Own(pool, pl, 3, b)
                for k in range(2):
                    pool.wait_ge(var_sum, 2 * b + k + 1)
                    hold(pool, m)
                    own.step(pool.tensor_scalar(ST[:, k, 2, :], ST[:, k, 2, :], 1.0 / D, EPS_LN, ALU.mult, ALU.add))
                    pool.tensor_tensor(ST[:, k, 3, :], ST[:, k, 2, :], m.half[:, 0:TB], ALU.pow).then_inc(rstd, 1)
                xb = m.X[:, bass.ds(b * TB, TB), :]
                pool.wait_ge(xnn_ready, b + 1)
                own.step(pool.tensor_tensor(xb, xb, XN[:, :, :], ALU.add))
                hold(pool, m)
                pool.tensor_tensor(xb, xb, bc(BOUT[:, :].unsqueeze(1), [P, TB, D]), ALU.add).then_inc(residual, 1)
                pool.tensor_copy(m.XN2[:, bass.ds(b * TB, TB), :], XN[:, :, :]).then_inc(kept, 1)
                own.end()

        @block.scalar
        def _(act):
            act.wait_ge(loaded, LOADS)
            with act.Fori(0, B) as b:
                act.wait_ge(centred, 2 * b + 1)
                act.activation(SQ[:, :, :], XC[:, :, :], ACT.Square).then_inc(squared, 1)
                act.wait_ge(centred, 2 * b + 2)
                act.activation(SQ[:, :, :], XC[:, :, :], ACT.Square).then_inc(squared, 1)
                for f in range(2):
                    act.wait_ge(turned_psum, 4 * b + f + 1 + 1)
                    act.activation(m.XNT[:, bass.ds(b * N + f * 512, 512)], ps[:, f, :], ACT.Copy)\
                       .then_inc(turned, 1)
                for f in range(2):
                    act.wait_ge(z_psum, 2 * b + f + 1)
                    act.activation(Z[:, f * 512:f * 512 + 512], ps[:, f, :], ACT.Silu, bias=BIN[:, 4:5])\
                       .then_inc(z_ready, 1)
                for n in range(4):
                    act.wait_ge(uv_psum, 12 * b + n + 1)
                    act.activation(UT[:, n // 2, (n % 2) * 512:(n % 2) * 512 + 512], ps[:, 2 + n % 2, :], ACT.Silu,
                                   bias=BIN[:, n // 2:n // 2 + 1]).then_inc(uv_ready, 1)
                for t in range(TB):
                    act.wait_ge(uv_psum, 12 * b + t + 5)
                    act.activation(V[:, t, :], ps[:, 4 + t % 2, 0:E1], ACT.Silu).then_inc(uv_ready, 1)
                for n in range(2 * TB):
                    act.wait_ge(s_psum, 2 * TB * b + n + 1)
                    if n >= 2:
                        act.wait_ge(a_ready, 2 * TB * b + n - 1)
                    act.activation(RL[:, n % 2, :], ps[:, n % 4, :], ACT.Relu, scale=1.0 / N).then_inc(relu_done, 1)

        @block.tensor
        def _(pe):
            prime(pe, turned_psum)
            pe.wait_ge(loaded, LOADS)
            with pe.Fori(0, B) as b:
                for k, (src, ready) in enumerate(((XN, xn_ready), (XNN, xnn_ready))):
                    pe.wait_ge(ready, b + 1)
                    for t in range(TB):
                        ins = pe.transpose(ps[:, 2 * k + t // 4, (t % 4) * P:(t % 4 + 1) * P], src[:, t, :],
                                           m.ident[:, :])
                        if t % 4 == 3:
                            ins.then_inc(turned_psum, 1)
                pe.wait_ge(turned, 4 * b + 4)
                for f in range(2):
                    pe.matmul(ps[:, f, :], WIN[:, 4 * P:5 * P], XT[:, f * 512:f * 512 + 512],
                              start=True, stop=True).then_inc(z_psum, 1)
                for n in range(4):
                    if n >= 2:
                        pe.wait_ge(uv_ready, 12 * b + n - 1)
                    pe.matmul(ps[:, 2 + n % 2, :], WIN[:, (n // 2) * P:(n // 2 + 1) * P],
                              XT[:, (n % 2) * 512:(n % 2) * 512 + 512], start=True, stop=True).then_inc(uv_psum, 1)
                for t in range(TB):
                    if t >= 2:
                        pe.wait_ge(uv_ready, 12 * b + t + 3)
                    out = ps[:, 4 + t % 2, 0:E1]
                    pe.matmul(out, XT[:, t * P:(t + 1) * P], WIN[:, E1:2 * E1], start=True, stop=False)
                    pe.matmul(out, ONE[:, :], BV[:, :], start=False, stop=True).then_inc(uv_psum, 1)
                pe.wait_ge(qk_ready, b + 1)
                pe.wait_ge(uv_ready, 12 * b + 12)

                def scores(n):
                    if n >= 4:
                        pe.wait_ge(relu_done, 2 * TB * b + n - 3)
                    pe.matmul(ps[:, n % 4, :], K[:, (n % TB) * P:(n % TB + 1) * P],
                              Q[:, (n // TB) * 512:(n // TB) * 512 + 512], start=True, stop=True).then_inc(s_psum, 1)

                scores(0)
                scores(1)
                for n in range(2 * TB):
                    c, kk = n // TB, n % TB
                    if n + 2 < 2 * TB:
                        scores(n + 2)
                    pe.wait_ge(a_ready, 2 * TB * b + n + 1)
                    if kk == 0 and c == 1:
                        pe.wait_ge(o_ready, 2 * b + 1)
                    for e in range(2):
                        ins = pe.matmul(ps[:, 4 + e, :], V[:, kk, e * P:(e + 1) * P], A[:, kk % 2, :],
                                        start=kk == 0, stop=kk == TB - 1)
                    ins.then_inc(av_psum, 1)
                    if kk == TB - 1:
                        pe.wait_ge(o_ready, 2 * b + c + 1)
                        if c == 1:
                            pe.wait_ge(out_added, 2 * b + 1)
                        for t in range(4):
                            for e in range(2):
                                ins = pe.matmul(ps[:, 6, t * P:(t + 1) * P], OG[:, e, t * P:(t + 1) * P],
                                                WOUT[:, e, :], start=e == 0, stop=e == 1)
                        ins.then_inc(out_psum, 1)


CW = 256
CHUNKS = SLOTS // CW
EC = CW // NP_
GROUPS = SLOTS // P
AHEAD = 4
YW = D + 2


def soft_experts(nc, m, d):
    with ExitStack() as ctx:
        def sem(name):
            return ctx.enter_context(nc.semaphore("se_" + name))

        def sb(name, shape, dt=fp32):
            return ctx.enter_context(nc.sbuf_tensor("se_" + name, shape, dt))

        ps = m.ps
        loaded, w_loaded, filled = sem("loaded"), sem("w_loaded"), sem("filled")
        l_psum, shifted, exp_done, sum_done, inv_done = sem("l_psum"), sem("shifted"), sem("exp"), sem("sum"), sem("inv")
        disp_ready, slots_psum, slots_ready = sem("disp"), sem("slots_psum"), sem("slots_ready")
        y_psum, y_ready = sem("y_psum"), sem("y_ready")
        vec, pl, row_ready, row_psum = sem("vec"), sem("pool"), sem("row_ready"), sem("row_psum")
        row_copied, row_stored, row_spread = sem("row_copied"), sem("row_stored"), sem("row_spread")
        PHI = sb("phi", [P, SLOTS])
        W = sb("w", [P, EC, D])
        BIAS = sb("bias", [P, GROUPS, D])
        Y = sb("y", [P, GROUPS, B, YW])
        M = sb("m", [P, 2, CW])
        SU = sb("su", [P, 2, 4, CW])
        SL = sb("sl", [P, B, CW])
        RM, RT = sb("rm", [P, B, TB]), sb("rt", [P, 2, B])
        RR = sb("rr", [B * TB, P])
        RB = sb("rb", [P, B * N])
        row_dram = nc.dram_tensor("row_max", (B * TB, P), fp32).ap()

        def logits_of(s):
            return ps[:, 2 * s:2 * s + 2, :].rearrange("p k (h c) -> p (k h) c", h=2)

        EXH = [t[:, :, :, :].rearrange("p u t c -> p (u t c)").rearrange("p (s b c) -> p s b c", s=4, b=B)
               for t in (m.QU, m.VU)]

        def ex(t):
            return EXH[t % TB // 4][:, t % 4, :, :]

        slots_bank = ps[:, 4:6, :].rearrange("p k (h c) -> p (k h) c", h=2)
        def over_chunks(eng, chunk):
            chunk(0, True, False)
            with eng.Fori(0, CHUNKS - 2) as i:
                chunk(i + 1, False, False)
            chunk(CHUNKS - 1, False, True)

        part1 = nc.Block()
        block = part1.__enter__()

        @block.sync
        def _(sp):
            sp.dma_start(PHI[:, :], d.phi).then_inc(loaded, 16)
            for q in range(4):
                sp.dma_start(BIAS[32 * q:32 * q + 32, :, :],
                             d.b.rearrange("(g q) e -> q g e", q=4)[q, :, :].partition_broadcast(32))\
                  .then_inc(loaded, 16)
            with sp.Fori(0, CHUNKS) as c:
                sp.wait_ge(y_psum, 2 * c + 1)
                sp.dma_start(W[:, :, :], d.w[bass.ds(c * EC, EC), :, :].rearrange("n d e -> d n e"))\
                  .then_inc(w_loaded, 16)
            sp.wait_ge(row_copied, 1)
            sp.dma_start(row_dram, RR[:, :]).then_inc(row_stored, 16)
            sp.wait_ge(row_stored, 16)
            sp.dma_start(RB[:, :], row_dram.rearrange("a p -> (a p)").partition_broadcast(P)).then_inc(row_spread, 16)
            sp.wait_ge(row_spread, 16)

        @block.vector
        def _(v):
            prime(v, y_ready)
            v.memset(RM[:, :, :], -3.0e38)
            v.memset(Y[:, :, :, D:YW], 1.0).then_inc(filled, 1)
            v.wait_ge(filled, 1)
            v.wait_ge(loaded, 5 * 16)

            def invert(c, t):
                v.wait_ge(sum_done, TB * c + t + 1)
                v.reciprocal(SU[:, 1, t % 4, :], SU[:, 0, t % 4, :]).then_inc(inv_done, 1)

            def add_bias(c, h):
                v.wait_ge(y_psum, 2 * c + h + 1 + 1)
                v.tensor_tensor(Y[:, bass.ds(2 * c + h, 1), :, 0:D].rearrange("p o b e -> p (o b) e"),
                                ps[:, 6 + h, :].rearrange("p (b e) -> p b e", b=B),
                                bc(BIAS[:, bass.ds(2 * c + h, 1), :], [P, B, D]), ALU.add).then_inc(y_ready, 1)

            def chunk(c, first, last):
                own = Own(v, vec, 2 * TB, c)
                for t in range(TB):
                    s = t % 2
                    v.wait_ge(l_psum, TB * c + t + 1)
                    L = logits_of(s)
                    own.mark(v.tensor_reduce(M[:, s, :], L.rearrange("p b c -> p c b"), AX.X, ALU.max))
                    own.mark(v.tensor_reduce(RT[:, s, :], L, AX.X, ALU.max))
                    if t >= 2 or not first:
                        invert(c, t - 2)
                    own.wait()
                    if not first:
                        v.wait_ge(slots_psum, TB * c + t - 7)
                    v.tensor_tensor(ex(t), L, bc(M[:, s, :].unsqueeze(1), [P, B, CW]), ALU.subtract)\
                     .then_inc(shifted, 1)
                    if not first:
                        v.wait_ge(row_ready, TB * c + t - 7)
                    v.tensor_tensor(RM[:, :, t], RM[:, :, t], RT[:, s, :], ALU.max).then_inc(row_ready, 1)
                    if t >= TB - 2 and not first:
                        add_bias(c - 1, t - (TB - 2))
                if last:
                    invert(c, TB - 2)
                    invert(c, TB - 1)
                    add_bias(c, 0)
                    add_bias(c, 1)

            over_chunks(v, chunk)

        @block.scalar
        def _(act):
            prime(act, slots_ready)

            def copy_slots(c):
                act.wait_ge(slots_psum, TB * c + TB)
                act.activation(SL[:, :, :], slots_bank, ACT.Copy).then_inc(slots_ready, 1)

            def chunk(c, first, last):
                for t in range(TB):
                    if t == 3 and not first:
                        act.wait_ge(y_psum, 2 * c - 2 + 1)
                        copy_slots(c - 1)
                    act.wait_ge(shifted, TB * c + t + 1)
                    act.activation(ex(t), ex(t), ACT.Exp).then_inc(exp_done, 1)
                if last:
                    act.wait_ge(y_psum, 2 * c + 1)
                    copy_slots(c)

            over_chunks(act, chunk)
            act.wait_ge(row_psum, 1)
            act.activation(RR[:, :], ps[0:B * TB, 0, 0:P], ACT.Copy).then_inc(row_copied, 1)

        @block.gpsimd
        def _(pool):
            def add_up(own, c, t):
                s, e = t % 4, ex(t)
                pool.wait_ge(exp_done, TB * c + t + 1)
                own.step(pool.tensor_tensor(SU[:, 0, s, :], e[:, 0, :], e[:, 1, :], ALU.add))
                own.step(pool.tensor_tensor(SU[:, 0, s, :], SU[:, 0, s, :], e[:, 2, :], ALU.add))
                pool.tensor_tensor(SU[:, 0, s, :], SU[:, 0, s, :], e[:, 3, :], ALU.add).then_inc(sum_done, 1)

            def chunk(c, first, last):
                own = Own(pool, pl, 1, c * (2 * TB) + (0 if first else 2))
                if first:
                    add_up(own, c, 0)
                for t in range(TB):
                    if t + 1 < TB or not last:
                        add_up(own, c, t + 1)
                    pool.wait_ge(inv_done, TB * c + t + 1)
                    pool.tensor_tensor(ex(t), ex(t), bc(SU[:, 1, t % 4, :].unsqueeze(1), [P, B, CW]), ALU.mult)\
                        .then_inc(disp_ready, 1)

            over_chunks(pool, chunk)

        @block.tensor
        def _(pe):
            prime(pe, y_psum)
            pe.wait_ge(loaded, 5 * 16)

            def logits(c, t):
                if not isinstance(c, int) or TB * c + t >= 2:
                    pe.wait_ge(shifted, TB * c + t - 1)
                for b in range(B):
                    at = b * N + (t % TB) * P
                    ins = pe.matmul(logits_of(t % 2)[:, b, :], m.XNT[:, at:at + P],
                                    PHI[:, bass.ds(c * CW + t // TB * CW, CW)], start=True, stop=True)
                ins.then_inc(l_psum, 1)

            def products(c, h):
                if h == 0:
                    pe.wait_ge(w_loaded, 16 * c + 16)
                    pe.wait_ge(y_ready, 2 * c + 1)
                for b in range(B):
                    for q in range(4):
                        n = 4 * h + q
                        ins = pe.matmul(ps[32 * q:32 * q + 32, 6 + h, b * D:(b + 1) * D],
                                        SL[:, b, n * NP_:(n + 1) * NP_], W[:, n, :], start=True, stop=True)
                ins.then_inc(y_psum, 1)

            def chunk(c, first, last):
                if first:
                    for t in range(AHEAD):
                        logits(c, t)
                for t in range(TB):
                    if t + AHEAD < TB or not last:
                        logits(c, t + AHEAD)
                    pe.wait_ge(disp_ready, TB * c + t + 1)
                    if t == 0 and not first:
                        pe.wait_ge(slots_ready, c + 1)
                    for b in range(B):
                        ins = pe.matmul(slots_bank[:, b, :], m.XN2[:, b * TB + t, :], ex(t)[:, b, :],
                                        start=t == 0 and b % 2 == 0, stop=t == TB - 1, skip_group_check=True)
                    ins.then_inc(slots_psum, 1)
                    if t in (1, 2) and not first:
                        products(c - 1, t - 1)
                if last:
                    pe.wait_ge(slots_ready, c + 1 + 1)
                    products(c, 0)
                    products(c, 1)

            over_chunks(pe, chunk)
            pe.wait_ge(row_ready, TB * CHUNKS)
            pe.wait_ge(y_ready, 2 * CHUNKS + 1)
            pe.transpose(ps[0:B * TB, 0, 0:P], RM[:, :, :].rearrange("p b t -> p (b t)"), m.ident[:, :])\
              .then_inc(row_psum, 1)
        part1.__exit__(None, None, None)

        MC = B * N // 512
        l2_psum, shifted2, exp2_done = sem("l2_psum"), sem("shifted2"), sem("exp2")
        acc_psum, out_ready, stored = sem("acc_psum"), sem("out_ready"), sem("stored")
        SH, CT = sb("sh", [P, 2, 512]), sb("ct", [P, 4, 512])
        DEN = sb("den", [P, 2, 4])
        block = ctx.enter_context(nc.Block())

        def acc(s, t):
            return ps[:, 4 + 2 * s + t // 2, (t % 2) * YW:(t % 2) * YW + YW]

        @block.sync
        def _(sp):
            with sp.Fori(0, MC) as c:
                sp.wait_ge(out_ready, c + 1 + 1)
                sp.dma_start(d.out[:, bass.ds(c * 4, 4), :], m.X[:, bass.ds(c * 4, 4), :]).then_inc(stored, 16)
            sp.wait_ge(stored, 16 * MC)

        @block.vector
        def _(v):
            prime(v, out_ready)
            with v.Fori(0, MC // 2) as cp:
                own = Own(v, vec, 8, cp + CHUNKS * 2)
                for s in range(2):
                    c = cp * 2 + s
                    for n in range(GROUPS):
                        v.wait_ge(l2_psum, c * GROUPS + n + 1)
                        if n >= 2:
                            v.wait_ge(exp2_done, c * GROUPS + n - 1)
                        v.tensor_tensor(SH[:, n % 2, :], ps[:, n % 4, :], RB[:, bass.ds(c * 512, 512)],
                                        ALU.subtract).then_inc(shifted2, 1)
                    v.wait_ge(acc_psum, (c + 1) * GROUPS)
                    for t in range(4):
                        own.mark(v.reciprocal(DEN[:, s, t:t + 1], acc(s, t)[:, D:D + 1]))
                    own.wait()
                    for t in range(4):
                        tile = m.X[:, bass.ds(c * 4 + t, 1), :].rearrange("p o d -> p (o d)")
                        ins = v.scalar_tensor_tensor(tile, acc(s, t)[:, 0:D], DEN[:, s, t:t + 1], tile,
                                                     ALU.mult, ALU.add)
                    ins.then_inc(out_ready, 1)
                own.end()

        @block.scalar
        def _(act):
            with act.Fori(0, MC) as c:
                for n in range(GROUPS):
                    act.wait_ge(shifted2, c * GROUPS + n + 1)
                    if n >= 4:
                        act.wait_ge(acc_psum, c * GROUPS + n - 3)
                    act.activation(CT[:, n % 4, :], SH[:, n % 2, :], ACT.Exp).then_inc(exp2_done, 1)

        @block.tensor
        def _(pe):
            with pe.Fori(0, MC // 2) as cp:
                for s in range(2):
                    c = cp * 2 + s

                    def logits2(n):
                        if n >= 4:
                            pe.wait_ge(shifted2, c * GROUPS + n - 3)
                        pe.matmul(ps[:, n % 4, :], PHI[:, n * P:(n + 1) * P], m.XNT[:, bass.ds(c * 512, 512)],
                                  start=True, stop=True).then_inc(l2_psum, 1)

                    for n in range(3):
                        logits2(n)
                    pe.wait_ge(out_ready, cp * 2 + 1)
                    for n in range(GROUPS):
                        pe.wait_ge(exp2_done, c * GROUPS + n + 1)
                        for t in range(4):
                            ins = pe.matmul(acc(s, t), CT[:, n % 4, t * P:(t + 1) * P],
                                            Y[:, n, bass.ds(cp, 1), :]
                                            .rearrange("p o e -> p (o e)"),
                                            start=n == 0 and t % 2 == 0, stop=n == GROUPS - 1, skip_group_check=True)
                        ins.then_inc(acc_psum, 1)
                        if n + 3 < GROUPS:
                            logits2(n + 3)


class Names:
    pass


def memory(nc, ctx):
    m = Names()

    def sb(name, shape, dt=fp32):
        return ctx.enter_context(nc.sbuf_tensor(name, shape, dt))

    m.X = sb("X", [P, TILES, D])
    m.ident = sb("ident", [P, P])
    m.mask_q = sb("mask_q", [P, 512], bf16)
    m.lower, m.half = sb("lower", [P, E, E]), sb("half", [P, TILES])
    m.Wqkv, m.Wr = sb("Wqkv", [P, 3 * D]), sb("Wr", [P, E])
    m.router_b, m.qk_scale = sb("router_b", [P, E]), sb("qk_scale", [P, 2 * H])
    m.XNT = sb("XNT", [P, B * N])
    m.QU, m.KU, m.VU = (sb(n, [P, U, TB, 32]) for n in ("QU", "KU", "VU"))
    m.LG, m.GT = sb("LG", [P, TILES, E]), sb("GT", [P, TILES, E])
    m.XN2 = m.KU[:, :, :, :].rearrange("p u t c -> p (u t c)").rearrange("p (a d) -> p a d", d=D)
    m.Wo, m.b2, m.b1 = sb("Wo", [P, D]), sb("b2", [E, D]), sb("b1", [P, E, HC])
    m.ps = ctx.enter_context(nc.psum_tensor("ps", [P, 8, 512], fp32))
    m.held = ctx.enter_context(nc.semaphore("held"))
    m.loaded = ctx.enter_context(nc.semaphore("loaded"))
    return m


def declare(nc, inputs):
    import numpy as np
    arr = {}
    d = Names()

    def give(name, a):
        arr["in_" + name] = np.ascontiguousarray(a)
        return nc.dram_tensor("in_" + name, a.shape, mybir.dt.from_np(a.dtype), kind="ExternalInput").ap()

    d.x = give("x", inputs["L0_attn_x"])
    d.wqkv = give("wqkv", np.concatenate([inputs["L0_attn_W" + c].T for c in "qkv"], axis=1))
    d.router_w = give("router_w", inputs["L0_ffn_router_w"])
    d.router_b = give("router_b", inputs["L0_ffn_router_b"])
    d.q_scale = give("q_scale", inputs["L0_attn_q_scale"])
    d.k_scale = give("k_scale", inputs["L0_attn_k_scale"])
    d.wo = give("wo", inputs["L0_attn_Wo"].T)
    d.w1, d.b1 = give("w1", inputs["L0_ffn_w1"]), give("b1", inputs["L0_ffn_b1"].reshape(E, HC, P).transpose(2, 0, 1))
    d.w2, d.b2 = give("w2", inputs["L0_ffn_w2"]), give("b2", inputs["L0_ffn_b2"])
    d.columns = give("columns", np.stack([inputs["L1_attn_" + name] for name in (
        "ln_g", "ln_b", "gamma_q", "beta_q", "gamma_k", "beta_k")], axis=1))
    d.w_in, d.b_out = give("w_in", inputs["L1_attn_W_in"]), give("b_out", inputs["L1_attn_b_out"])
    d.b_in = give("b_in", inputs["L1_attn_b_in"].reshape(5, P).T)
    d.b_v = give("b_v", inputs["L1_attn_b_in"][E1:2 * E1])
    d.w_out = give("w_out", inputs["L1_attn_W_out"])
    d.phi = give("phi", inputs["L1_ffn_phi"].reshape(D, SLOTS))
    d.w, d.b = give("w", inputs["L1_ffn_W"]), give("b", inputs["L1_ffn_b"])
    d.out = nc.dram_tensor("out", (B, N, D), fp32, kind="ExternalOutput").ap()\
        .rearrange("b (t p) d -> p (b t) d", p=P)
    return arr, d


def build(nc, d):
    with ExitStack() as ctx:
        m = memory(nc, ctx)
        setup(nc, m, d)
        project(nc, m)
        gates(nc, m)
        load_late(nc, m, d)
        attention(nc, m)
        mix_heads(nc, m)
        experts(nc, m, d)
        gated_attention(nc, m, d)
        soft_experts(nc, m, d)


def kernel(**inputs):
    import numpy as np
    import concourse.bacc as bacc
    from concourse.bass_utils import run_bass_kernel_spmd

    nc = bacc.Bacc("TRN2", target_bir_lowering=False, num_devices=1)
    arrays, d = declare(nc, {name: np.asarray(a) for name, a in inputs.items()})
    build(nc, d)
    return run_bass_kernel_spmd(nc, [arrays], core_ids=[0]).results[0]["out"]
```

```python
from contextlib import ExitStack

import concourse.bass as bass
from concourse import mybir

fp32 = mybir.dt.float32
f32r = mybir.dt.float32r
bf16 = mybir.dt.bfloat16
ALU = mybir.AluOpType
ACT = mybir.ActivationFunctionType
AX = mybir.AxisListType

P = 128
B, N, D = 4, 1024, 128
TB = N // P
TILES = B * TB
H, HD = 16, 8
HG = 4
G = H // HG
U = B * G
E, HID = 8, 512
HC = HID // P
NE, NP_ = 64, 32
SLOTS = NE * NP_
E1 = 256
EPS_LN, EPS_DIR = 1e-5, 1e-6
MASKED = -1e30


class Own:

    def __init__(self, eng, sem, per=0, turn=0):
        self.eng, self.sem, self.per, self.turn, self.n = eng, sem, per, turn, 0

    def mark(self, ins):
        self.n += 1
        ins.then_inc(self.sem, 1)
        return ins

    def wait(self):
        self.eng.wait_ge(self.sem, self.turn * self.per + self.n)

    def step(self, ins):
        self.mark(ins)
        self.wait()

    def end(self):
        assert self.n == self.per, self.n


def hold(eng, m):
    eng.sem_inc(m.held, 1)


def prime(eng, *semaphores):
    for s in semaphores:
        eng.sem_inc(s, 1)


def three(pe, out, w_high, w_low, high, low, start, stop):
    pe.matmul(out, w_high, high, start=start, stop=False)
    pe.matmul(out, w_high, low, start=False, stop=False)
    return pe.matmul(out, w_low, high, start=False, stop=stop)


def bc(ap, shape):
    return ap.to_broadcast(shape)


def setup(nc, m, d):
    with ExitStack() as ctx:
        zeroed = ctx.enter_context(nc.semaphore("zeroed"))
        block = ctx.enter_context(nc.Block())

        @block.sync
        def _(sp):
            x = d.x.rearrange("b (t p) d -> p (b t) d", p=P)
            sp.dma_start(m.X[:, 0:TB, :], x[:, 0:TB, :]).then_inc(m.loaded, 16)
            sp.dma_start(m.Wqkv[:, :], d.wqkv).then_inc(m.loaded, 16)
            sp.dma_start(m.Wr[:, :], d.router_w).then_inc(m.loaded, 16)
            sp.dma_start(m.router_b[:, :], d.router_b.partition_broadcast(P)).then_inc(m.loaded, 16)
            sp.dma_start(m.qk_scale[:, 0:H], d.q_scale.partition_broadcast(P)).then_inc(m.loaded, 16)
            sp.dma_start(m.qk_scale[:, H:2 * H], d.k_scale.partition_broadcast(P)).then_inc(m.loaded, 16)
            sp.dma_start(m.X[:, TB:TILES, :], x[:, TB:TILES, :]).then_inc(m.rest_loaded, 16)
            sp.wait_ge(m.loaded, 6 * 16)

        @block.gpsimd
        def _(pool):
            pool.memset(m.ident[:, :], 0.0).then_inc(zeroed, 1)
            pool.memset(m.mask_q[:, :], 0.0).then_inc(zeroed, 1)
            pool.memset(m.lower[:, :, :], 0.0).then_inc(zeroed, 1)
            pool.memset(m.half[:, :], -0.5).then_inc(zeroed, 1)
            pool.wait_ge(zeroed, 4)
            pool.affine_select(out=m.ident[:, :], in_=m.ident[:, :], compare_op=ALU.not_equal, fill=1.0, base=0,
                               pattern=[[-1, P]], channel_multiplier=1).then_inc(zeroed, 1)
            pool.affine_select(out=m.mask_q[:, 512 - P:512], in_=m.mask_q[:, 512 - P:512], compare_op=ALU.is_ge, fill=MASKED,
                               base=0, pattern=[[-1, P]], channel_multiplier=1).then_inc(zeroed, 1)
            pool.affine_select(out=m.lower[:, :, :], in_=m.lower[:, :, :], compare_op=ALU.is_ge, fill=1.0,
                               base=0, pattern=[[-1, E], [1, E]], channel_multiplier=0).then_inc(zeroed, 1)
            pool.wait_ge(zeroed, 7)


def project(nc, m):
    with ExitStack() as ctx:
        def sem(name):
            return ctx.enter_context(nc.semaphore("pj_" + name))

        def sb(name, shape, dt=fp32):
            return ctx.enter_context(nc.sbuf_tensor("pj_" + name, shape, dt))

        centred, squared, var_sum, rstd_ready = sem("centred"), sem("squared"), sem("var_sum"), sem("rstd")
        xn_ready, xt_psum, xt_ready = sem("xn_ready"), sem("xt_psum"), sem("xt_ready")
        copied, lg_taken = sem("copied"), sem("lg_taken")
        qkv_psum, silu_done, logits_psum = sem("qkv_psum"), sem("silu_done"), sem("logits_psum")
        qk_squared, n2_ready, r_ready = sem("qk_squared"), sem("n2_ready"), sem("r_ready")
        factors, k_scaled = sem("factors"), sem("k_scaled")
        vec, pl = sem("vec"), sem("pool")
        XC, SQ = sb("xc", [P, TILES, D]), sb("sq", [P, TB, D])
        XN, XT = sb("xn", [P, TB, D]), sb("xt", [P, N])
        ST, VAR = sb("st", [P, 3, TILES]), sb("var", [P, TB])
        SQK, SQ2 = sb("sqk", [P, TILES, 2 * D]), sb("sq2", [P, TB, 2 * D])
        N2, R, F = sb("n2", [P, TB, 2 * H]), sb("r", [P, TB, 2 * H]), sb("f", [P, TB, 2 * H])
        ps = m.ps
        block = ctx.enter_context(nc.Block())

        def of(tile, b):
            return tile[:, bass.ds(b * TB, TB), :]

        def st(k, b):
            return ST[:, k, bass.ds(b * TB, TB)]

        def steps(eng, step):
            with eng.Fori(0, B - 2) as b:
                step(b, 2)
            step(B - 2, 1)
            step(B - 1, 0)

        def scale(eng, b, s, dst):
            for g in range(G):
                ins = eng.tensor_tensor(
                    dst[:, bass.ds(b * G + g, 1), :, :].rearrange("p o t (j i) -> p (o t) j i", i=HD),
                    of(SQK, b)[:, :, s * D + g * 32:s * D + g * 32 + 32].rearrange("p t (j i) -> p t j i", i=HD),
                    bc(F[:, :, s * H + g * HG:s * H + g * HG + HG].unsqueeze(3), [P, TB, HG, HD]), ALU.mult)
            return ins

        @block.sync
        def _(sp):
            with sp.Fori(0, B) as b:
                sp.wait_ge(xt_ready, 2 * b + 2)
                hold(sp, m)
                sp.dma_start(m.XNT[:, bass.ds(b * N, N)], XT[:, :]).then_inc(copied, 16)
            sp.wait_ge(copied, 16 * B + 1)

        @block.vector
        def _(v):
            def centre(own, b):
                own.step(v.tensor_reduce(st(0, b), of(m.X, b), AX.X, ALU.add))
                own.step(v.tensor_scalar(st(1, b), st(0, b), -1.0 / D, None, ALU.mult))
                v.tensor_tensor(of(XC, b), of(m.X, b), bc(st(1, b).unsqueeze(2), [P, TB, D]), ALU.add)\
                 .then_inc(centred, 1)

            def variance(b):
                v.wait_ge(squared, b + 1)
                v.tensor_reduce(VAR[:, :], SQ[:, :, :], AX.X, ALU.add).then_inc(var_sum, 1)

            def normalised(b):
                v.wait_ge(rstd_ready, b + 1)
                if not isinstance(b, int) or b:
                    v.wait_ge(xt_psum, 2 * b)
                v.tensor_tensor(XN[:, :, :], of(XC, b), bc(st(2, b).unsqueeze(2), [P, TB, D]), ALU.mult)\
                 .then_inc(xn_ready, 1)

            def step(b, behind):
                own = Own(v, vec, 1, b * 6 + 4)
                if isinstance(b, int) and b == B - 1:
                    own = Own(v, vec, 1, b * 6 + 4 - 2)
                if behind >= 1:
                    normalised(b + 1)
                if behind == 2:
                    centre(own, b + 2)
                v.wait_ge(logits_psum, b + 1)
                v.tensor_tensor(of(m.LG, b), ps[:, 6, 0:TB * E].rearrange("p (t e) -> p t e", e=E),
                                bc(m.router_b[:, :].unsqueeze(1), [P, TB, E]), ALU.add).then_inc(lg_taken, 1)
                if behind == 2:
                    variance(b + 2)
                v.wait_ge(qk_squared, b + 1)
                v.tensor_reduce(N2[:, :, :], SQ2[:, :, :].rearrange("p t (h i) -> p t h i", i=HD), AX.X,
                                ALU.add).then_inc(n2_ready, 1)
                v.wait_ge(r_ready, b + 1)
                v.wait_ge(k_scaled, b + 1)
                own.step(v.tensor_scalar(F[:, :, :], R[:, :, :], EPS_DIR, None, ALU.add))
                own.step(v.reciprocal(N2[:, :, :], F[:, :, :]))
                own.step(v.tensor_tensor(F[:, :, :], R[:, :, :], N2[:, :, :], ALU.mult))
                v.tensor_tensor(F[:, :, :], F[:, :, :], bc(m.qk_scale[:, :].unsqueeze(1), [P, TB, 2 * H]),
                                ALU.mult).then_inc(factors, 1)
                v.wait_ge(factors, b + 1)
                own.mark(scale(v, b, 0, m.QU))

            prime(v, k_scaled)
            own = Own(v, vec)
            centre(own, 0)
            variance(0)
            v.wait_ge(m.rest_loaded, 16)
            centre(own, 1)
            normalised(0)
            variance(1)
            steps(v, step)

        @block.gpsimd
        def _(pool):
            def square(b):
                pool.wait_ge(centred, b + 1)
                hold(pool, m)
                pool.tensor_tensor(SQ[:, :, :], of(XC, b), of(XC, b), ALU.mult).then_inc(squared, 1)

            def deviation(b):
                pool.wait_ge(var_sum, b + 1)
                hold(pool, m)
                Own(pool, pl, 1, b).step(
                    pool.tensor_scalar(VAR[:, :], VAR[:, :], 1.0 / D, EPS_LN, ALU.mult, ALU.add))
                hold(pool, m)
                pool.tensor_tensor(st(2, b), VAR[:, :], m.half[:, 0:TB], ALU.pow).then_inc(rstd_ready, 1)

            def step(b, behind):
                if behind == 2:
                    square(b + 2)
                    deviation(b + 2)
                pool.wait_ge(factors, b + 1)
                hold(pool, m)
                scale(pool, b, 1, m.KU).then_inc(k_scaled, 1)

            for b in range(2):
                square(b)
                deviation(b)
            steps(pool, step)

        @block.scalar
        def _(act):
            prime(act, silu_done, copied)

            def turn(b):
                for f in range(2):
                    act.wait_ge(xt_psum, 2 * b + f + 1)
                    if f == 0:
                        act.wait_ge(copied, b * 16 + 1)
                        act.wait_ge(qkv_psum, TB * b + 1)
                    act.activation(XT[:, f * 512:f * 512 + 512], ps[:, f, :], ACT.Copy).then_inc(xt_ready, 1)

            def silu(b):
                for t in range(TB):
                    act.wait_ge(qkv_psum, TB * b + t + 1 + 1)
                    hold(act, m)
                    act.activation(SQK[:, bass.ds(b * TB + t, 1), :].rearrange("p o c -> p (o c)"),
                                   ps[:, 2 + t % 4, 0:2 * D], ACT.Silu)
                    act.activation(m.VU[:, bass.ds(b * G, G), t, :],
                                   ps[:, 2 + t % 4, 2 * D:3 * D].rearrange("p (g c) -> p g c", g=G),
                                   ACT.Silu).then_inc(silu_done, 1)

            def lengths(b):
                act.wait_ge(silu_done, TB * b + TB + 1)
                hold(act, m)
                act.activation(SQ2[:, :, :], of(SQK, b), ACT.Square).then_inc(qk_squared, 1)
                act.wait_ge(n2_ready, b + 1)
                act.activation(R[:, :, :], N2[:, :, :], ACT.Sqrt).then_inc(r_ready, 1)

            turn(0)
            with act.Fori(0, B - 1) as b:
                silu(b)
                turn(b + 1)
                lengths(b)
            silu(B - 1)
            lengths(B - 1)

        @block.tensor
        def _(pe):
            prime(pe, lg_taken, qkv_psum)
            with pe.Fori(0, B) as b:
                pe.wait_ge(xn_ready, b + 1)
                for t in range(TB):
                    ins = pe.transpose(ps[:, t // 4, (t % 4) * P:(t % 4 + 1) * P], XN[:, t, :], m.ident[:, :])
                    if t % 4 == 3:
                        ins.then_inc(xt_psum, 1)
                pe.wait_ge(xt_ready, 2 * b + 2)
                pe.wait_ge(lg_taken, b + 1)
                for t in range(TB):
                    last = pe.matmul(ps[:, 6, t * E:t * E + E], XT[:, t * P:(t + 1) * P], m.Wr[:, :],
                                     start=True, stop=True)
                last.then_inc(logits_psum, 1)
                for t in range(TB):
                    if t == 0:
                        pe.wait_ge(silu_done, TB * b + 1)
                    if t >= 4:
                        pe.wait_ge(silu_done, TB * b + t - 3 + 1)
                    pe.matmul(ps[:, 2 + t % 4, 0:3 * D], XT[:, t * P:(t + 1) * P], m.Wqkv[:, :],
                              start=True, stop=True).then_inc(qkv_psum, 1)


def gates(m, v, own, cmp_, rank, tie, mx, top, expd):
    full = [P, TILES, E, E]
    LG = m.LG[:, :, :]
    other, this = bc(LG.unsqueeze(2), full), bc(LG.unsqueeze(3), full)
    own.step(v.tensor_tensor(cmp_, other, this, ALU.is_gt))
    own.step(v.tensor_reduce(rank[:, :, :], cmp_, AX.X, ALU.add))
    own.step(v.tensor_tensor(cmp_, other, this, ALU.is_equal))
    own.step(v.tensor_tensor(cmp_, cmp_, bc(m.lower[:, :, :].unsqueeze(1), full), ALU.mult))
    own.step(v.tensor_reduce(tie[:, :, :], cmp_, AX.X, ALU.add))
    own.step(v.tensor_tensor(rank[:, :, :], rank[:, :, :], tie[:, :, :], ALU.add))
    own.step(v.tensor_scalar(rank[:, :, :], rank[:, :, :], 1.5, None, ALU.is_lt))
    own.step(v.tensor_reduce(mx[:, :], LG, AX.X, ALU.max))
    v.tensor_tensor(tie[:, :, :], LG, bc(mx[:, :].unsqueeze(2), [P, TILES, E]), ALU.subtract).then_inc(top, 1)
    v.wait_ge(expd, 1)
    own.step(v.tensor_tensor(tie[:, :, :], m.GT[:, :, :], rank[:, :, :], ALU.mult))
    own.step(v.tensor_reduce(mx[:, :], tie[:, :, :], AX.X, ALU.add))
    own.step(v.reciprocal(mx[:, :], mx[:, :]))
    v.tensor_tensor(m.GT[:, :, :], tie[:, :, :], bc(mx[:, :].unsqueeze(2), [P, TILES, E]), ALU.mult)


P2_UNITS = [(k, c) for half in (0, 1) for k in range(TB) for c in (2 * half, 2 * half + 1) if c >= k // 2]
P1_UNITS = ([(i, 0, j) for j in range(HG) for i in (0, 3, 1, 2)]
            + [(i, c, j) for i in range(4, TB) for j in range(HG) for c in (0, 1)])
N2U, N1U = len(P2_UNITS), len(P1_UNITS)
HALF2 = sum(c < 2 for _, c in P2_UNITS)
HALF1 = sum(i < 4 for i, _, _ in P1_UNITS)
DIAGONAL = [q for q, (k, c) in enumerate(P2_UNITS) if c == k // 2]
PV_LAG = 2
FREE_A = 1 + max(q for q, (k, _) in enumerate(P2_UNITS) if k < 4)
OB1, Q2B, OB0, Q2A, K0, K1, Q0, Q1 = range(8)
FILL_AT = {3: OB1, 4: Q2B, 9: OB0, 10: Q2A, 12: K0, 13: K1, 15: Q0, 17: Q1}
AT_FILL = {f: q for q, f in FILL_AT.items()}


def p1_upto(q):
    return N1U * (q + 1) // N2U


def p1_before_fill(q):
    return p1_upto(q) - 1


PRO_FILLS = 9


def attention(nc, m):
    with ExitStack() as ctx:
        def sem(name):
            return ctx.enter_context(nc.semaphore("at_" + name))

        def sb(name, shape, dt=fp32):
            return ctx.enter_context(nc.sbuf_tensor("at_" + name, shape, dt))

        k_staged, kq_staged, v_staged = sem("k_staged"), sem("kq_staged"), sem("v_staged")
        ktx_loaded = [sem("ktx_loaded_a"), sem("ktx_loaded_b")]
        filled, emptied = sem("filled"), sem("emptied")
        p1_psum, max_done, max_staged = sem("p1_psum"), sem("max_done"), sem("max_staged")
        masked = sem("masked_pt")
        s2_psum, exp_done, pv_done = sem("s2_psum"), sem("exp_done"), sem("pv_done")
        o_copied = sem("o_copied")
        vec, pl, zeroed = sem("vec"), sem("pool"), sem("zeroed")
        k_zeroed, ident_rounded = sem("k_zeroed"), sem("ident_rounded")
        KP, QP = sb("kp", [P, TB, HG, 32], f32r), sb("qp", [P, 2, TB, HG, 32], f32r)
        ident_r = sb("ident_r", [P, P], f32r)
        VW = sb("vw", [P, 2, TB, HG, 32])
        KT = sb("kt", [P, N], f32r)
        KTX = sb("ktx", [P, 2, HG, N], f32r)
        QT1, QT2 = sb("qt1", [P, 2, N], f32r), sb("qt2", [P, 2, N], f32r)
        PT = sb("pt", [P, 4, HG, 256])
        OT = sb("ot", [P, 512])
        MX, NM = sb("mx", [P, TB, 2, HG]), sb("nm", [P, TB, HG])
        DEN = sb("den", [P, 4, HG])
        gate_vec, top, gate_exp = sem("gate_vec"), sem("top"), sem("gate_exp")
        rank, tie, mx = sb("rank", [P, TILES, E]), sb("tie", [P, TILES, E]), sb("mx2", [P, TILES])
        MASKED_S = sb("masked", [P, 2, 512], bf16)
        ps = m.ps
        P2B = [ps[:, 2 * s:2 * s + 2, :].rearrange("p b (h n) -> p (b h) n", h=2) for s in range(2)]
        P1B = [ps[:, 4 + s, :] for s in range(2)]
        FIRST_BANKS = [ps[:, k, :] for k in (4, 5, 0, 1, 2, 3)]
        OB, TR = ps[:, 6, :], ps[:, 7, :]
        block = ctx.enter_context(nc.Block())

        def fills(u, at, left_out=0):
            return u * 8 + (at + PRO_FILLS - left_out)

        def steps(eng, step, before, after):
            before()
            step(0, 0)
            step(1, 1)
            with eng.Fori(0, (U - 4) // 2) as i:
                step(i * 2 + 2, 0)
                step(i * 2 + 3, 1)
            step(U - 2, 0)
            step(U - 1, 1)
            after()

        def is_(u, n):
            return isinstance(u, int) and u == n

        def has(u, d):
            return not isinstance(u, int) or u + d < U

        @block.sync
        def _(sp):
            def load(half, par):
                cols = slice(512 * half, 512 * half + 512)
                for j in range(HG):
                    sp.dma_start(KTX[32 * j:32 * j + 32, par, j, cols].bitcast(fp32),
                                 KT[32 * j:32 * j + 32, cols].bitcast(fp32)).then_inc(ktx_loaded[half], 16)

            def before():
                sp.wait_ge(zeroed, 3)
                for v in (0, 1):
                    for half in (0, 1):
                        sp.wait_ge(emptied, 4 * v + half + 1)
                        load(half, v)

            def step(u, par):
                if has(u, 2):
                    sp.wait_ge(emptied, fills(u, K0))
                    hold(sp, m)
                    sp.wait_ge(s2_psum, u * N2U + FREE_A)
                    hold(sp, m)
                    load(0, par)
                    sp.wait_ge(emptied, fills(u, K1))
                    hold(sp, m)
                    sp.wait_ge(s2_psum, u * N2U + N2U)
                    hold(sp, m)
                    load(1, par)

            steps(sp, step, before, lambda: sp.wait_ge(m.late_loaded, 9 * 16))

        @block.gpsimd
        def _(pool):
            def round_split(own, src, hi, hi2, lo):
                own.mark(pool.tensor_copy(hi, src))
                pool.tensor_copy(hi2, src)
                own.wait()
                hold(pool, m)
                return pool.tensor_tensor(lo, src, hi.bitcast(fp32), ALU.subtract)

            def unit_of(t, v):
                return t[:, bass.ds(v, 1), :, :].rearrange("p o t (j i) -> p (o t) j i", i=HD)

            def stage_kq(v, par, count):
                own = Own(pool, pl, 2, count)
                q = QP[:, par, :, :, :]
                round_split(own, unit_of(m.KU, v), KP[:, :, :, 0:8], KP[:, :, :, 8:16], KP[:, :, :, 16:24])\
                    .then_inc(k_staged, 1)
                round_split(own, unit_of(m.QU, v), q[:, :, :, 0:8], q[:, :, :, 16:24], q[:, :, :, 8:16])
                pool.memset(q[:, :, :, 24:26].bitcast(fp32), 0.0).then_inc(kq_staged, 1)

            def stage_v(v, par):
                pool.tensor_copy(VW[:, par, :, :, 0:8], unit_of(m.VU, v)).then_inc(v_staged, 1)

            def before():
                pool.memset(KP[:, :, :, :].bitcast(fp32), 0.0).then_inc(k_zeroed, 1)
                pool.wait_ge(k_zeroed, 1)
                pool.memset(KP[:, :, :, 24:26].bitcast(fp32), 1.0)
                pool.wait_ge(zeroed, 2)
                pool.memset(VW[:, :, :, :, 8:9], 1.0)
                stage_kq(0, 0, 0)
                stage_v(0, 0)
                pool.wait_ge(filled, 4)
                stage_kq(1, 1, 1)

            def mask(u, q):
                k, _ = P2_UNITS[q]
                pool.wait_ge(exp_done, u * N2U + q + 1)
                hold(pool, m)
                tile = PT[:, q % 4, :, (k % 2) * P:(k % 2 + 1) * P]
                pool.affine_select(out=tile, in_=tile, compare_op=ALU.is_ge, fill=0.0, base=0,
                                   pattern=[[0, HG], [1, P]], channel_multiplier=-1).then_inc(masked, 1)

            def step(u, par):
                for q in DIAGONAL:
                    if q == DIAGONAL[4]:
                        if has(u, 2):
                            pool.wait_ge(filled, fills(u, Q2B))
                            stage_kq(u + 2, par, u + 2)
                        if has(u, 1):
                            pool.wait_ge(pv_done, u * N2U + 1)
                            stage_v(u + 1, 1 - par)
                    mask(u, q)

            steps(pool, step, before, lambda: None)

        @block.scalar
        def _(act):
            def copy_out(dst, count):
                act.wait_ge(filled, count)
                act.activation(dst, TR, ACT.Copy).then_inc(emptied, 1)

            def before():
                act.activation(ident_r[:, :], m.ident[:, :], ACT.Copy).then_inc(ident_rounded, 1)
                for v in (0, 1):
                    if v == 1:
                        act.wait_ge(top, 1)
                        act.activation(m.GT[:, :, :], tie[:, :, :], ACT.Exp).then_inc(gate_exp, 1)
                    for f in range(2):
                        if v == 1:
                            act.wait_ge(ktx_loaded[f], HG * 16)
                        copy_out(KT[:, f * 512:f * 512 + 512], 4 * v + f + 1)
                    for f in range(2):
                        copy_out(QT1[:, v, f * 512:f * 512 + 512], 4 * v + f + 3)
                copy_out(QT2[:, 0, 0:512], 9)

            def copy_o(u, half):
                act.wait_ge(pv_done, u * N2U + (N2U if half else HALF2))
                act.activation(OT[:, :], OB, ACT.Copy).then_inc(o_copied, 1)

            def step(u, par):
                less = 4 if is_(u, U - 1) else 0
                for q, (k, c) in enumerate(P2_UNITS):
                    if q == PV_LAG and not is_(u, 0):
                        copy_o(u - 1, 1)
                    if q == HALF2 + PV_LAG:
                        copy_o(u, 0)
                    act.wait_ge(s2_psum, u * N2U + q + 1)
                    if q >= 4 or not is_(u, 0):
                        act.wait_ge(pv_done, u * N2U + (q - 3))
                    lo = 128 if k % 2 and c == k // 2 else 0
                    act.activation(PT[:, q % 4, :, lo:256] if lo else PT[:, q % 4, :, :],
                                   P2B[q % 2][:, :, lo:256] if lo else P2B[q % 2], ACT.Exp)\
                       .then_inc(exp_done, 1)
                    f = FILL_AT.get(q)
                    if f == Q2B:
                        copy_out(QT2[:, par, 512:1024], fills(u, Q2B, less))
                    if f == Q2A and has(u, 1):
                        copy_out(QT2[:, 1 - par, 0:512], fills(u, Q2A))
                    if f in (K0, K1) and has(u, 2):
                        copy_out(KT[:, (f - K0) * 512:(f - K0) * 512 + 512], fills(u, f))
                    if f in (Q0, Q1) and has(u, 2):
                        copy_out(QT1[:, par, (f - Q0) * 512:(f - Q0) * 512 + 512], fills(u, f))

            steps(act, step, before, lambda: copy_o(U - 1, 1))

        @block.vector
        def _(v):
            def reduce(un, n):
                i, c, j = P1_UNITS[n]
                w = min(512, (i + 1) * P - c * 512)
                scores = (FIRST_BANKS[n % 6] if is_(un, 0) else P1B[n % 2])[:, 0:w]
                if is_(un, 0) and n >= 2:
                    v.wait_ge(max_done, n - 1)
                v.wait_ge(p1_psum, un * N1U + n + 1)
                if c == i // 4:
                    hold(v, m)
                if c == i // 4:
                    v.tensor_tensor_reduce(out=MASKED_S[:, n % 2, 0:w], in0=scores, in1=m.mask_q[:, 512 - w:512],
                                           scale=1.0, scalar=-3e38, op0=ALU.add, op1=ALU.max,
                                           accum_out=MX[:, i, c, j:j + 1]).then_inc(max_done, 1)
                else:
                    v.tensor_reduce(MX[:, i, c, j:j + 1], scores, AX.X, ALU.max).then_inc(max_done, 1)

            def stage_max(own, un, par, half):
                rows = slice(4 * half, 4 * half + 4)
                v.wait_ge(max_done, un * N1U + (N1U if half else HALF1))
                src = MX[:, rows, 0, :]
                if half:
                    own.step(v.tensor_tensor(MX[:, rows, 0, :], src, MX[:, rows, 1, :], ALU.max))
                own.step(v.tensor_scalar(NM[:, rows, :], src, -1.0, None, ALU.mult))
                hi, lo = (QP[:, par, rows, :, c:c + 1].rearrange("p t j o -> p t (j o)") for c in (24, 25))
                own.step(v.tensor_scalar(hi, NM[:, rows, :], 1.0, None, ALU.mult))
                v.tensor_tensor(lo, NM[:, rows, :], hi.bitcast(fp32), ALU.subtract).then_inc(max_staged, 1)

            def divide(own, u, half, count):
                v.wait_ge(filled, count)
                t4 = TR.rearrange("p (t j c) -> p t j c", t=4, j=HG)
                own.step(v.reciprocal(DEN[:, :, :], t4[:, :, :, 8:9].rearrange("p t j o -> p t (j o)")))
                v.tensor_tensor(
                    m.QU[:, bass.ds(u, 1), 4 * half:4 * half + 4, :].rearrange("p o t (j i) -> p (o t) j i", i=HD),
                    t4[:, :, :, 0:8], bc(DEN[:, :, :].unsqueeze(3), [P, 4, HG, HD]), ALU.mult)\
                 .then_inc(emptied, 1)

            PER = 7

            def before():
                v.memset(QP[:, :, :, :, :].bitcast(fp32), 0.0).then_inc(zeroed, 1)
                v.memset(VW[:, :, :, :, :], 0.0).then_inc(zeroed, 1)
                v.memset(KTX[:, :, :, :].bitcast(fp32), 0.0).then_inc(zeroed, 1)
                gates(m, v, Own(v, gate_vec), PT[:, 0:2, :, :].rearrange("p a b c -> p (a b c)")
                      .rearrange("p (t e f) -> p t e f", e=E, f=E), rank, tie, mx, top, gate_exp)
                own = Own(v, vec)
                for n in range(N1U):
                    reduce(0, n)
                    if n == HALF1 - 1:
                        stage_max(own, 0, 0, 0)
                stage_max(own, 0, 0, 1)
                assert own.n == 5

            def step(u, par):
                less = 4 if is_(u, U - 1) else 0
                own = Own(v, vec, 1, u * PER + 5 - (0 if is_(u, 0) else 1))
                for n in range(N1U):
                    if n == p1_before_fill(AT_FILL[OB1]) and not is_(u, 0):
                        divide(own, u - 1, 1, fills(u, OB1, less))
                    if n == HALF1 and has(u, 1):
                        stage_max(own, u + 1, 1 - par, 0)
                    if n == p1_before_fill(AT_FILL[OB0]):
                        divide(own, u, 0, fills(u, OB0, less))
                    if has(u, 1):
                        reduce(u + 1, n)
                if has(u, 1):
                    stage_max(own, u + 1, 1 - par, 1)

            def after():
                own = Own(v, vec, 1, (U - 1) * PER + 5 - 1 + 2)
                divide(own, U - 1, 1, fills(U, OB1, 9))

            steps(v, step, before, after)

        @block.tensor
        def _(pe):
            def fill(what, in_of, count):
                if count > 1:
                    pe.wait_ge(emptied, count - 1)
                for t in range(4):
                    out, tile = TR[:, t * P:(t + 1) * P], in_of(t)
                    if what == "o":
                        ins = pe.transpose(out, tile, m.ident[:, :])
                    else:
                        ins = pe.transpose(out.bitcast(f32r), tile, ident_r[:, :])
                ins.then_inc(filled, 1)

            def staged(tile, half):
                return lambda t: tile[:, 4 * half + t, :, :].rearrange("p j c -> p (j c)")

            def pass1(un, par, n):
                i, c, j = P1_UNITS[n]
                w = max(256, min(512, (i + 1) * P - c * 512))
                banks = FIRST_BANKS if is_(un, 0) else P1B
                if not is_(un, 0) or n >= len(banks):
                    pe.wait_ge(max_done, un * N1U + (n - len(banks) + 1))
                pe.matmul(banks[n % len(banks)][:, 0:w], QT1[:, par, i * P:(i + 1) * P],
                          KTX[:, par, j, c * 512:c * 512 + w], start=True, stop=True).then_inc(p1_psum, 1)

            def scores2(u, par, q, pass1_steps):
                k, c = P2_UNITS[q]
                if not (is_(u, 0) and q < 2):
                    pe.wait_ge(exp_done, u * N2U + (q - 1))
                for j in range(HG):
                    if j == 2:
                        pass1_steps()
                    ins = pe.matmul(P2B[q % 2][:, j, :], KTX[:, par, j, k * P:(k + 1) * P],
                                    QT2[:, par, c * 256:c * 256 + 256], start=True, stop=True)
                ins.then_inc(s2_psum, 1)

            def values(u, par, q):
                k, c = P2_UNITS[q]
                if q in DIAGONAL:
                    pe.wait_ge(masked, u * len(DIAGONAL) + DIAGONAL.index(q) + 1)
                else:
                    pe.wait_ge(exp_done, u * N2U + q + 1)
                if q == 0:
                    pe.wait_ge(v_staged, u + 1)
                if q in (0, HALF2) and not (is_(u, 0) and q == 0):
                    pe.wait_ge(o_copied, u * 2 + (1 if q else 0))
                lo = 128 if k % 2 and c == k // 2 else 0
                at = (c % 2) * 256 + lo
                for j in range(HG):
                    ins = pe.matmul(OB[32 * j:32 * j + 32, at:at + 256 - lo], VW[:, par, k, j, :],
                                    PT[:, q % 4, j, lo:256], start=q in (0, HALF2),
                                    stop=q in (HALF2 - 1, N2U - 1), skip_group_check=True)
                ins.then_inc(pv_done, 1)

            def before():
                pe.wait_ge(ident_rounded, 1)
                for v in (0, 1):
                    pe.wait_ge(k_staged, v + 1)
                    for f in range(2):
                        fill("k", staged(KP, f), 4 * v + f + 1)
                    pe.wait_ge(kq_staged, v + 1)
                    for f in range(2):
                        fill("q", staged(QP[:, v, :, :, :], f), 4 * v + f + 3)
                pe.wait_ge(emptied, 4)
                for n in range(N1U):
                    if n in (0, HALF1):
                        pe.wait_ge(ktx_loaded[n // HALF1], HG * 16)
                    pass1(0, 0, n)
                    if n == HALF1 + 8:
                        pe.wait_ge(max_staged, 1)
                        fill("q2", staged(QP[:, 0, :, :, :], 0), 9)

            def step(u, par):
                less = 4 if is_(u, U - 1) else 0
                issued = 0

                def pass1_steps(upto):
                    nonlocal issued
                    while has(u, 1) and issued < upto:
                        if issued in (0, HALF1):
                            pe.wait_ge(ktx_loaded[issued // HALF1], (u + 2) * (HG * 16))
                            if not is_(u, 0):
                                pe.wait_ge(emptied, fills(u - 1, Q1 if issued else Q0))
                        pass1(u + 1, 1 - par, issued)
                        issued += 1

                for q in range(N2U):
                    if q == 0 and is_(u, 0):
                        pe.wait_ge(max_done, N1U)
                    if q == 0:
                        pe.wait_ge(emptied, 9 if is_(u, 0) else fills(u - 1, Q2A))
                    if q == HALF2:
                        pe.wait_ge(emptied, fills(u, Q2B, less))
                    scores2(u, par, q, lambda: pass1_steps(p1_upto(q) - 2))
                    pass1_steps(p1_before_fill(q))
                    f = FILL_AT.get(q)
                    if f == OB1 and not is_(u, 0):
                        pe.wait_ge(o_copied, u * 2)
                        fill("o", lambda t: OT[:, t * P:(t + 1) * P], fills(u, OB1, less))
                    if f == Q2B:
                        pe.wait_ge(max_staged, u * 2 + 2)
                        fill("q2", staged(QP[:, par, :, :, :], 1), fills(u, Q2B, less))
                    if f == OB0:
                        pe.wait_ge(o_copied, u * 2 + 1)
                        fill("o", lambda t: OT[:, t * P:(t + 1) * P], fills(u, OB0, less))
                    if f == Q2A and has(u, 1):
                        pe.wait_ge(max_staged, u * 2 + 3)
                        fill("q2", staged(QP[:, 1 - par, :, :, :], 0), fills(u, Q2A))
                    if f in (K0, K1, Q0, Q1) and has(u, 2):
                        if f == K0:
                            pe.wait_ge(kq_staged, u + 3)
                        tile = KP if f in (K0, K1) else QP[:, par, :, :, :]
                        fill("kq", staged(tile, f % 2), fills(u, f))
                    if q >= PV_LAG:
                        values(u, par, q - PV_LAG)
                    elif not is_(u, 0):
                        values(u - 1, 1 - par, N2U + q - PV_LAG)
                    pass1_steps(p1_upto(q))

            def after():
                for q in range(N2U - PV_LAG, N2U):
                    values(U - 1, 1, q)
                pe.wait_ge(o_copied, 2 * U)
                fill("o", lambda t: OT[:, t * P:(t + 1) * P], fills(U, OB1, 9))

            steps(pe, step, before, after)


def load_expert(sp, m, d, e, w):
    sp.dma_start(m.WR[:, w, 0:HID], d.w1[e, :, :]).then_inc(m.w_loaded[w], 16)
    sp.dma_start(m.WR[:, w, HID:2 * HID].rearrange("p (c d) -> p c d", d=D),
                 d.w2[e, :, :].rearrange("(c p) d -> p c d", p=P)).then_inc(m.w_loaded[w], 16)


def mix_heads(nc, m, d):
    with ExitStack() as ctx:
        def sem(name):
            return ctx.enter_context(nc.semaphore("mh_" + name))

        copied, gathered, turned, out_ready, added = (sem(n) for n in ("copied", "gathered", "turned", "out", "added"))
        stored, rounded = sem("stored"), sem("rounded")
        AW = ctx.enter_context(nc.sbuf_tensor("mh_aw", [P, 2, TB, G, 32], fp32))
        AT = ctx.enter_context(nc.sbuf_tensor("mh_at", [P, 2, N], fp32))
        GW = ctx.enter_context(nc.sbuf_tensor("mh_gw", [P, 2, TB, E], fp32))
        GTT = ctx.enter_context(nc.sbuf_tensor("mh_gt", [E, 2, N], fp32))
        ps = m.ps
        block = ctx.enter_context(nc.Block())

        @block.sync
        def _(sp):
            load_expert(sp, m, d, 0, 0)
            load_expert(sp, m, d, 1, 1)
            with sp.Fori(0, B // 2) as i:
                for s in range(2):
                    b = i * 2 + s
                    sp.wait_ge(turned, 4 * b + 4)
                    hold(sp, m)
                    sp.dma_start(m.gate_rows[:, bass.ds(b * N, N)], GTT[:, s, :]).then_inc(stored, 16)
            sp.wait_ge(stored, 16 * B + 1)

        @block.gpsimd
        def _(pool):
            for b in range(B):
                part = slice(b * N, b * N + N)
                pool.tensor_copy(m.XH[:, part], m.XNT[:, part]).then_inc(rounded, 1)
                pool.wait_ge(rounded, b + 1)
                pool.tensor_tensor(m.XL[:, part], m.XNT[:, part], m.XH[:, part].bitcast(fp32),
                                   ALU.subtract)

        def pairs(eng, step):
            with eng.Fori(0, B // 2 - 1) as i:
                step(i * 2, 0, True)
                step(i * 2 + 1, 1, True)
            step(B - 2, 0, True)
            step(B - 1, 1, False)

        @block.vector
        def _(v):
            def gather(b, s):
                v.tensor_copy(AW[:, s, :, :, :].rearrange("p t g c -> p g t c"), m.QU[:, bass.ds(b * G, G), :, :])
                v.tensor_copy(GW[:, s, :, :], m.GT[:, bass.ds(b * TB, TB), :]).then_inc(copied, 1)

            def step(b, s, more):
                if more:
                    v.wait_ge(gathered, 4 * b + 1)
                    gather(b + 1, 1 - s)
                for f in range(2):
                    v.wait_ge(out_ready, 2 * b + f + 1)
                    xs = m.X[:, bass.ds(b * TB + 4 * f, 4), :]
                    v.tensor_tensor(xs, xs, ps[:, 4 + f, :].rearrange("p (t d) -> p t d", t=4), ALU.add)\
                     .then_inc(added, 1)

            prime(v, added)
            gather(0, 0)
            pairs(v, step)
            v.wait_ge(m.w_rounded, 1)
            v.tensor_tensor(m.WL[:, 0, :], m.WR[:, 0, :], m.WH[:, 0, :].bitcast(fp32), ALU.subtract)\
             .then_inc(m.w_split, 1)

        @block.scalar
        def _(act):
            prime(act, stored)
            with act.Fori(0, B // 2) as i:
                for s in range(2):
                    b = i * 2 + s
                    for f in range(2):
                        act.wait_ge(gathered, 4 * b + f + 1 + 1)
                        act.activation(AT[:, s, f * 512:f * 512 + 512], ps[:, f, :], ACT.Copy).then_inc(turned, 1)
                    for f in range(2):
                        act.wait_ge(gathered, 4 * b + f + 3 + 1)
                        act.wait_ge(stored, 16 * b + 1)
                        act.activation(GTT[:, s, f * 512:f * 512 + 512], ps[0:E, 2 + f, :], ACT.Copy)\
                           .then_inc(turned, 1)
            act.wait_ge(m.w_loaded[0], 32)
            act.activation(m.WH[:, 0, :], m.WR[:, 0, :], ACT.Copy).then_inc(m.w_rounded, 1)

        @block.tensor
        def _(pe):
            def turn(b, s):
                pe.wait_ge(copied, b + 1)
                for t in range(TB):
                    ins = pe.transpose(ps[:, t // 4, (t % 4) * P:(t % 4 + 1) * P],
                                       AW[:, s, t, :, :].rearrange("p g c -> p (g c)"), m.ident[:, :])
                    if t % 4 == 3:
                        ins.then_inc(gathered, 1)
                for t in range(TB):
                    ins = pe.transpose(ps[0:E, 2 + t // 4, (t % 4) * P:(t % 4 + 1) * P], GW[:, s, t, :], m.ident[:, :])
                    if t % 4 == 3:
                        ins.then_inc(gathered, 1)

            def step(b, s, more):
                pe.wait_ge(turned, 4 * b + 4)
                if more:
                    turn(b + 1, 1 - s)
                for t in range(TB):
                    if t % 4 == 0:
                        pe.wait_ge(added, 2 * b + 1)
                    out = ps[:, 4 + t // 4, (t % 4) * P:(t % 4 + 1) * P]
                    pe.matmul(out, AT[:, s, t * P:(t + 1) * P], m.Wo[:, :], start=True, stop=False)
                    ins = pe.matmul(out, GTT[:, s, t * P:(t + 1) * P], m.b2[:, :], start=False, stop=True)
                    if t % 4 == 3:
                        ins.then_inc(out_ready, 1)

            prime(pe, gathered)
            turn(0, 0)
            pairs(pe, step)


def experts(nc, m, d):
    CH = B * N // 512
    ALL = E * CH
    with ExitStack() as ctx:
        def sem(name):
            return ctx.enter_context(nc.semaphore("ex_" + name))

        def sb(name, shape, dt=fp32):
            return ctx.enter_context(nc.sbuf_tensor("ex_" + name, shape, dt))

        gates_loaded, zeroed = [sem("gates%d" % j) for j in range(4)], sem("zeroed")
        w_loaded, w_rounded, w_split = m.w_loaded, m.w_rounded, m.w_split
        WR, WH, WL = m.WR, m.WH, m.WL
        h_psum, relu_done, hi_done, lo_done = (sem(n) for n in ("h_psum", "relu", "hi", "lo"))
        y_psum, gated, added = (sem(n) for n in ("y_psum", "gated", "added"))
        turned_psum, x_added = sem("turned_psum"), sem("x_added")
        HH, HL = sb("hh", [P, 2, HC, 512], f32r), sb("hl", [P, 2, HC, 512], f32r)
        YT, KF, VF = (t[:, :, :, :].rearrange("p u t c -> p (u t c)") for t in (m.QU, m.KU, m.VU))
        R = KF[:, 4 * HID:8 * HID].rearrange("p (h n) -> p h n", h=HC)
        GB = VF[:, 0:2048].rearrange("p (j n) -> p j n", j=4)
        T = VF[:, 2048:3072].rearrange("p (j n) -> p j n", j=2)
        ps = m.ps
        LO0, Y0, GATED0, ADDED0 = HC, 2, 4, CH
        block = ctx.enter_context(nc.Block())

        @block.sync
        def _(sp):
            def expert(e, w, more):
                if more:
                    sp.wait_ge(w_split, e + 1)
                    hold(sp, m)
                    load_expert(sp, m, d, e + 2, w)
                for c in range(CH):
                    n = e * CH + c
                    sp.wait_ge(gated, n - 3 + GATED0)
                    hold(sp, m)
                    sp.dma_start(GB[:, c % 4, :], m.gate_rows.rearrange("e t -> (e t)")[bass.ds(n * 512, 512)]
                                 .partition_broadcast(P)).then_inc(gates_loaded[c % 4], 16)

            with sp.Fori(0, E // 2 - 1) as ep:
                expert(ep * 2, 0, True)
                expert(ep * 2 + 1, 1, True)
            expert(E - 2, 0, False)
            expert(E - 1, 1, False)

        @block.scalar
        def _(act):
            def relu(e, n, hc):
                act.wait_ge(h_psum, n * HC + hc + 1)
                act.wait_ge(lo_done, n * HC + hc - HC + 1 + LO0)
                hold(act, m)
                act.activation(R[:, hc, :], ps[:, hc, :], ACT.Relu, bias=m.b1[:, bass.ds(e, 1), hc])\
                   .then_inc(relu_done, 1)

            def high(n, s, hc):
                act.wait_ge(relu_done, n * HC + hc + 1)
                if hc == 0:
                    act.wait_ge(y_psum, n - 1 + Y0)
                act.activation(HH[:, s, hc, :], R[:, hc, :], ACT.Copy).then_inc(hi_done, 1)

            with act.Fori(0, E) as e:
                with act.Fori(0, CH // 2) as cp:
                    for s in range(2):
                        n = e * CH + cp * 2 + s
                        relu(e, n, 0)
                        for hc in range(HC):
                            if hc + 1 < HC:
                                relu(e, n, hc + 1)
                            high(n, s, hc)

        @block.vector
        def _(v):
            def low(n, s):
                for hc in range(HC):
                    v.wait_ge(hi_done, n * HC + hc + 1)
                    v.tensor_tensor(HL[:, s, hc, :], R[:, hc, :], HH[:, s, hc, :].bitcast(fp32), ALU.subtract)\
                     .then_inc(lo_done, 1)

            def gate(n, i, c):
                v.wait_ge(y_psum, n + 1 + Y0)
                v.wait_ge(gates_loaded[c % 4], i * 16 + 16)
                v.wait_ge(added, n - 1 + ADDED0)
                v.tensor_tensor(T[:, c % 2, :], ps[:, 4 + c % 2, :], GB[:, c % 4, :], ALU.mult).then_inc(gated, 1)

            prime(v, *(Y0 * [y_psum] + LO0 * [lo_done] + GATED0 * [gated]))
            low(0, 0)
            with v.Fori(0, ALL // 4 - 1) as i:
                for c in range(4):
                    low(i * 4 + (c + 1), (c + 1) % 2)
                    gate(i * 4 + c, i, c)
            for c in range(4):
                if c < 3:
                    low(ALL - 4 + c + 1, (c + 1) % 2)
                gate(ALL - 4 + c, ALL // 4 - 1, c)
            for c in range(CH):
                v.wait_ge(turned_psum, c + 1)
                xs = m.X[:, 4 * c:4 * c + 4, :]
                v.tensor_tensor(xs, xs, ps[:, c % 4, :].rearrange("p (t d) -> p t d", t=4), ALU.add)\
                 .then_inc(x_added, 1)

        @block.gpsimd
        def _(pool):
            def split(e, w):
                pool.wait_ge(w_loaded[w], e // 2 * 32 + 32 if isinstance(e, int) else (e - w) * 16 + 32)
                hold(pool, m)
                if not isinstance(e, int) or e >= 2:
                    pool.wait_ge(y_psum, e * CH - CH + Y0)
                    hold(pool, m)
                pool.tensor_copy(WH[:, w, :], WR[:, w, :]).then_inc(w_rounded, 1)
                pool.wait_ge(w_rounded, e + 1)
                hold(pool, m)
                pool.tensor_tensor(WL[:, w, :], WR[:, w, :], WH[:, w, :].bitcast(fp32), ALU.subtract)\
                    .then_inc(w_split, 1)

            def expert(e, w, more):
                for c in range(CH):
                    n = e * CH + c
                    pool.wait_ge(gated, n + 1 + GATED0)
                    hold(pool, m)
                    pool.wait_ge(added, n - CH + 1 + ADDED0)
                    hold(pool, m)
                    chunk = YT[:, c * 512:c * 512 + 512]
                    pool.tensor_tensor(chunk, chunk, T[:, c % 2, :], ALU.add).then_inc(added, 1)
                    if more and c == 3:
                        split(e + 1, 1 - w)

            prime(pool, *(ADDED0 * [added]))
            pool.memset(YT, 0.0).then_inc(zeroed, 1)
            pool.wait_ge(zeroed, 1)
            with pool.Fori(0, E // 2 - 1) as ep:
                expert(ep * 2, 0, True)
                expert(ep * 2 + 1, 1, True)
            expert(E - 2, 0, True)
            expert(E - 1, 1, False)

        @block.tensor
        def _(pe):
            def hidden(n, w, c):
                high, low = (t[:, bass.ds(c * 512, 512)] for t in (m.XH, m.XL))
                for hc in range(HC):
                    if not isinstance(n, int) or n:
                        pe.wait_ge(relu_done, (n - 1) * HC + hc + 1)
                    at = slice(hc * P, hc * P + P)
                    three(pe, ps[:, hc, :], WH[:, w, at], WL[:, w, at], high, low, True, True).then_inc(h_psum, 1)

            def output(n, w, s):
                pe.wait_ge(gated, n - 1 + GATED0)
                for hc in range(HC):
                    pe.wait_ge(lo_done, n * HC + hc + 1 + LO0)
                    at = slice(HID + hc * D, HID + hc * D + D)
                    ins = three(pe, ps[:, 4 + s, :], WH[:, w, at], WL[:, w, at], HH[:, s, hc, :], HL[:, s, hc, :],
                                hc == 0, hc == HC - 1)
                ins.then_inc(y_psum, 1)

            def expert(e, w, more):
                with pe.Fori(0, CH // 2 - 1) as cp:
                    for s in range(2):
                        n = e * CH + cp * 2 + s
                        hidden(n + 1, w, cp * 2 + (s + 1))
                        output(n, w, s)
                hidden(e * CH + (CH - 1), w, CH - 1)
                output(e * CH + (CH - 2), w, 0)
                if more:
                    pe.wait_ge(w_split, e + 2)
                    hidden(e * CH + CH, 1 - w, 0)
                output(e * CH + (CH - 1), w, 1)

            pe.wait_ge(w_split, 1)
            hidden(0, 0, 0)
            with pe.Fori(0, E // 2 - 1) as ep:
                expert(ep * 2, 0, True)
                expert(ep * 2 + 1, 1, True)
            expert(E - 2, 0, True)
            expert(E - 1, 1, False)
            pe.wait_ge(relu_done, ALL * HC)
            for c in range(CH):
                pe.wait_ge(added, ALL - CH + c + 1 + ADDED0)
                if c >= 4:
                    pe.wait_ge(x_added, c - 3)
                for t in range(4):
                    at = (4 * c + t) * P
                    ins = pe.transpose(ps[:, c % 4, t * P:(t + 1) * P], YT[:, at:at + P], m.ident[:, :])
                ins.then_inc(turned_psum, 1)


def load_late(nc, m, d):
    with ExitStack() as ctx:
        block = ctx.enter_context(nc.Block())

        @block.sync
        def _(sp):
            for dst, src in ((m.Wo[:, :], d.wo), (m.b2[:, :], d.b2), (m.b1[:, :, :], d.b1), (m.WIN[:, :], d.w_in),
                             (m.BIN[:, :], d.b_in), (m.BV[:, :], d.b_v.partition_broadcast(P)),
                             (m.WOUT[:, :, :], d.w_out.rearrange("(c p) d -> p c d", p=P)),
                             (m.BOUT[:, :], d.b_out.partition_broadcast(P)), (m.COL[:, :], d.columns)):
                sp.dma_start(dst, src).then_inc(m.late_loaded, 16)


def gated_attention(nc, m, d):
    with ExitStack() as ctx:
        def sem(name):
            return ctx.enter_context(nc.semaphore("ga_" + name))

        def sb(name, shape, dt=fp32):
            return ctx.enter_context(nc.sbuf_tensor("ga_" + name, shape, dt))

        ps = m.ps
        centred, squared, var_sum, rstd = sem("centred"), sem("squared"), sem("var_sum"), sem("rstd")
        xn_ready, turned_psum, turned = sem("xn_ready"), sem("turned_psum"), sem("turned")
        xnn_ready, kept, residual = sem("xnn_ready"), sem("kept"), sem("residual")
        z_psum, z_ready, qk_ready = sem("z_psum"), sem("z_ready"), sem("qk_ready")
        qk_split = sem("qk_lo")
        u_psum, u_ready, v_psum, v_biased, v_ready = (sem(n) for n in ("u_psum", "u_ready", "v_psum", "v_biased", "v_ready"))
        s_psum, relu_done, a_ready, av_psum, o_ready = sem("s_psum"), sem("relu"), sem("a"), sem("av"), sem("o")
        out_psum, out_added = sem("out_psum"), sem("out_added")
        vec, pl = sem("vec"), sem("pool")
        XN, XNN = sb("xn", [P, TB, D]), sb("xnn", [P, TB, D])
        ST = sb("st", [P, 2, 4, TB])
        QF, VF = (t[:, :, :, :].rearrange("p u t c -> p (u t c)") for t in (m.QU, m.VU))
        XC, SQ = (QF[:, k * N:k * N + N].rearrange("p (t d) -> p t d", d=D) for k in (0, 1))
        Z, Q = QF[:, 2 * N:3 * N], QF[:, 3 * N:4 * N]
        K, XT = VF[:, 0:N], VF[:, N:2 * N]
        V = VF[:, 2 * N:4 * N].rearrange("p (t e) -> p t e", t=TB)
        UT, VB = sb("ut", [P, 2, N]), sb("vb", [P, 2, E1])
        QH, QL, KH, KL = (sb(n, [P, N], f32r) for n in ("qh", "ql", "kh", "kl"))
        VH, VL = sb("vh", [P, TB, E1], f32r), sb("vl", [P, TB, E1], f32r)
        RL, A = sb("rl", [P, 2, 512]), sb("a", [P, 4, 512])
        AH, AL = sb("ah", [P, 4, 512], f32r), sb("al", [P, 4, 512], f32r)
        qk_rounded, v_rounded, v_split, a_rounded, a_split = (
            sem(n) for n in ("qk_hi", "v_hi", "v_lo", "a_hi", "a_lo"))
        OG = sb("og", [P, 2, 512])
        NS = 2 * TB
        SB = 3
        OUT_BANK = (3, 4)
        block = ctx.enter_context(nc.Block())

        def steps(eng, before, step):
            before()
            with eng.Fori(0, B - 1) as b:
                step(b, True)
            step(B - 1, False)

        @block.sync
        def _(sp):
            sp.dma_start(m.PHI[:, :], d.phi).then_inc(m.phi_loaded, 16)

        @block.vector
        def _(v):
            def centre(b, k):
                own = Own(v, vec, 2, b * 2 + k)
                src = XN[:, :, :] if k else m.X[:, bass.ds(b * TB, TB), :]
                if k:
                    v.wait_ge(xn_ready, b + 1)
                own.step(v.tensor_reduce(ST[:, k, 0, :], src, AX.X, ALU.add))
                own.step(v.tensor_scalar(ST[:, k, 1, :], ST[:, k, 0, :], -1.0 / D, None, ALU.mult))
                v.tensor_tensor(XC[:, :, :], src, bc(ST[:, k, 1, :].unsqueeze(2), [P, TB, D]), ALU.add)\
                 .then_inc(centred, 1)

            def variance(b, k):
                v.wait_ge(squared, 2 * b + k + 1)
                v.tensor_reduce(ST[:, k, 2, :], SQ[:, :, :], AX.X, ALU.add).then_inc(var_sum, 1)

            def normalised(b, k):
                v.wait_ge(rstd, 2 * b + k + 1)
                if k == 0:
                    v.wait_ge(kept, b + 1)
                    v.wait_ge(turned_psum, 4 * b + 1)
                v.tensor_tensor((XNN if k else XN)[:, :, :], XC[:, :, :],
                                bc(ST[:, k, 3, :].unsqueeze(2), [P, TB, D]), ALU.mult)\
                 .then_inc(xnn_ready if k else xn_ready, 1)

            NORM = [(f, k) for k in (0, 1) for f in (centre, variance, normalised)]
            NORM_AT = dict(zip((1, 4, 7, 8, 12, 14), NORM))

            def add_out(b, c):
                v.wait_ge(out_psum, 2 * b + c + 1)
                v.wait_ge(residual, b + 1)
                xs = m.X[:, bass.ds(b * TB + 4 * c, 4), :]
                v.tensor_tensor(xs, xs, ps[:, OUT_BANK[c], :].rearrange("p (t d) -> p t d", t=4), ALU.add)\
                 .then_inc(out_added, 1)

            def affine(b):
                for f in range(2):
                    v.wait_ge(turned_psum, 4 * b + f + 3 + 1)
                    v.tensor_scalar(XT[:, f * 512:f * 512 + 512], ps[:, 2 + f, :], m.COL[:, 0:1], m.COL[:, 1:2],
                                    ALU.mult, ALU.add).then_inc(turned, 1)

            def before():
                prime(v, v_ready)
                for f, k in NORM:
                    f(0, k)
                affine(0)

            def step(b, more):
                v.wait_ge(z_ready, 2 * b + 2)
                v.tensor_scalar(Q, Z, m.COL[:, 2:3], m.COL[:, 3:4], ALU.mult, ALU.add).then_inc(qk_ready, 1)
                v.tensor_scalar(K, Z, m.COL[:, 4:5], m.COL[:, 5:6], ALU.mult, ALU.add).then_inc(qk_ready, 1)
                for k, (lo, whole, hi) in enumerate(((QL, Q, QH), (KL, K, KH))):
                    v.wait_ge(qk_rounded, 2 * b + k + 1)
                    v.tensor_tensor(lo[:, :], whole, hi[:, :].bitcast(fp32), ALU.subtract).then_inc(qk_split, 1)
                for t in range(TB):
                    v.wait_ge(v_psum, TB * b + t + 1)
                    if t >= 2:
                        v.wait_ge(v_ready, TB * b + t - 1 + 1)
                    v.tensor_tensor(VB[:, t % 2, :], ps[:, 4 + t % 2, 0:E1], m.BV[:, :], ALU.add)\
                     .then_inc(v_biased, 1)
                for n in range(NS + 1):
                    if n < NS:
                        v.wait_ge(relu_done, NS * b + n + 1)
                        v.tensor_tensor(A[:, n % 4, :], RL[:, n % 2, :], RL[:, n % 2, :], ALU.mult)\
                         .then_inc(a_ready, 1)
                    if n:
                        v.wait_ge(a_rounded, NS * b + n)
                        v.tensor_tensor(AL[:, (n - 1) % 4, :], A[:, (n - 1) % 4, :],
                                        AH[:, (n - 1) % 4, :].bitcast(fp32), ALU.subtract).then_inc(a_split, 1)
                    if n == TB + 1:
                        gate(b, 0)
                    if n == TB + 4:
                        add_out(b, 0)
                    if more and n in NORM_AT:
                        f, k = NORM_AT[n]
                        f(b + 1, k)
                gate(b, 1)
                if more:
                    affine(b + 1)
                add_out(b, 1)

            def gate(b, c):
                v.wait_ge(av_psum, NS * b + (c + 1) * TB)
                if c:
                    v.wait_ge(out_psum, 2 * b + 1)
                for e in range(2):
                    ins = v.tensor_tensor(OG[:, e, :], ps[:, 4 + 2 * c + e, :], UT[:, e, c * 512:c * 512 + 512],
                                          ALU.mult)
                ins.then_inc(o_ready, 1)

            steps(v, before, step)

        @block.gpsimd
        def _(pool):
            def norms(b):
                own = Own(pool, pl, 3, b)
                for k in range(2):
                    pool.wait_ge(centred, 2 * b + k + 1)
                    hold(pool, m)
                    pool.tensor_tensor(SQ[:, :, :], XC[:, :, :], XC[:, :, :], ALU.mult).then_inc(squared, 1)
                    pool.wait_ge(var_sum, 2 * b + k + 1)
                    hold(pool, m)
                    own.step(pool.tensor_scalar(ST[:, k, 2, :], ST[:, k, 2, :], 1.0 / D, EPS_LN, ALU.mult, ALU.add))
                    pool.tensor_tensor(ST[:, k, 3, :], ST[:, k, 2, :], m.half[:, 0:TB], ALU.pow).then_inc(rstd, 1)
                xb = m.X[:, bass.ds(b * TB, TB), :]
                pool.wait_ge(xnn_ready, b + 1)
                own.step(pool.tensor_tensor(xb, xb, XN[:, :, :], ALU.add))
                hold(pool, m)
                pool.tensor_tensor(xb, xb, bc(m.BOUT[:, :].unsqueeze(1), [P, TB, D]), ALU.add).then_inc(residual, 1)
                pool.tensor_copy(m.XN2[:, bass.ds(b * TB, TB), :], XN[:, :, :]).then_inc(kept, 1)
                own.end()

            def split_v(b):
                for t in range(TB):
                    pool.wait_ge(v_rounded, TB * b + t + 1)
                    pool.tensor_tensor(VL[:, t, :], V[:, t, :], VH[:, t, :].bitcast(fp32), ALU.subtract)\
                        .then_inc(v_split, 1)

            prime(pool, kept)
            norms(0)
            with pool.Fori(0, B - 1) as b:
                split_v(b)
                norms(b + 1)
            split_v(B - 1)

        @block.scalar
        def _(act):
            def keep(b):
                for f in range(2):
                    act.wait_ge(turned_psum, 4 * b + f + 1 + 1)
                    act.activation(m.XNT[:, bass.ds(b * N + f * 512, 512)], ps[:, f, :], ACT.Copy)\
                       .then_inc(turned, 1)

            def step(b, more):
                for f in range(2):
                    act.wait_ge(z_psum, 2 * b + f + 1)
                    act.activation(Z[:, f * 512:f * 512 + 512], ps[:, f, :], ACT.Silu, bias=m.BIN[:, 4:5])\
                       .then_inc(z_ready, 1)
                for k, (hi, whole) in enumerate(((QH, Q), (KH, K))):
                    act.wait_ge(qk_ready, 2 * b + k + 1)
                    act.activation(hi[:, :], whole, ACT.Copy).then_inc(qk_rounded, 1)
                for n in range(4):
                    act.wait_ge(u_psum, 4 * b + n + 1)
                    act.activation(UT[:, n // 2, (n % 2) * 512:(n % 2) * 512 + 512], ps[:, 2 + n % 2, :], ACT.Silu,
                                   bias=m.BIN[:, n // 2:n // 2 + 1]).then_inc(u_ready, 1)
                for t in range(TB + 1):
                    if t < TB:
                        act.wait_ge(v_biased, TB * b + t + 1)
                        act.activation(V[:, t, :], VB[:, t % 2, :], ACT.Silu).then_inc(v_ready, 1)
                    if t:
                        act.wait_ge(v_ready, TB * b + t + 1)
                        act.activation(VH[:, t - 1, :], V[:, t - 1, :], ACT.Copy).then_inc(v_rounded, 1)
                for n in range(NS + 1):
                    if n < NS:
                        act.wait_ge(s_psum, NS * b + n + 1)
                        if n >= 2:
                            act.wait_ge(a_ready, NS * b + n - 1)
                        act.activation(RL[:, n % 2, :], ps[:, n % SB, :], ACT.Relu, scale=1.0 / N)\
                           .then_inc(relu_done, 1)
                    if n:
                        act.wait_ge(a_ready, NS * b + n)
                        if n >= 5:
                            act.wait_ge(av_psum, NS * b + n - 4)
                        act.activation(AH[:, (n - 1) % 4, :], A[:, (n - 1) % 4, :], ACT.Copy).then_inc(a_rounded, 1)
                if more:
                    keep(b + 1)

            steps(act, lambda: keep(0), step)

        @block.tensor
        def _(pe):
            def turn(b):
                for k, (src, ready) in enumerate(((XN, xn_ready), (XNN, xnn_ready))):
                    pe.wait_ge(ready, b + 1)
                    for t in range(TB):
                        ins = pe.transpose(ps[:, 2 * k + t // 4, (t % 4) * P:(t % 4 + 1) * P], src[:, t, :],
                                           m.ident[:, :])
                        if t % 4 == 3:
                            ins.then_inc(turned_psum, 1)

            def output(b, c):
                pe.wait_ge(o_ready, 2 * b + c + 1)
                for t in range(4):
                    for e in range(2):
                        ins = pe.matmul(ps[:, OUT_BANK[c], t * P:(t + 1) * P], OG[:, e, t * P:(t + 1) * P],
                                        m.WOUT[:, e, :], start=e == 0, stop=e == 1)
                ins.then_inc(out_psum, 1)

            def before():
                prime(pe, turned_psum, out_added)
                turn(0)

            def step(b, more):
                pe.wait_ge(turned, 4 * b + 4)
                for f in range(2):
                    pe.matmul(ps[:, f, :], m.WIN[:, 4 * P:5 * P], XT[:, f * 512:f * 512 + 512],
                              start=True, stop=True).then_inc(z_psum, 1)
                for n in range(4):
                    if n >= 2:
                        pe.wait_ge(u_ready, 4 * b + n - 1)
                    pe.matmul(ps[:, 2 + n % 2, :], m.WIN[:, (n // 2) * P:(n // 2 + 1) * P],
                              XT[:, (n % 2) * 512:(n % 2) * 512 + 512], start=True, stop=True).then_inc(u_psum, 1)
                for t in range(TB):
                    if t == 0:
                        pe.wait_ge(out_added, 2 * b + 1)
                    if t >= 2:
                        pe.wait_ge(v_biased, TB * b + t - 1)
                    pe.matmul(ps[:, 4 + t % 2, 0:E1], XT[:, t * P:(t + 1) * P], m.WIN[:, E1:2 * E1],
                              start=True, stop=True).then_inc(v_psum, 1)
                pe.wait_ge(qk_split, 2 * b + 2)

                def scores(n):
                    if n == 0:
                        pe.wait_ge(u_ready, 4 * b + 4)
                    if n >= SB:
                        pe.wait_ge(relu_done, NS * b + n - SB + 1)
                    keys, queries = slice(n % TB * P, (n % TB + 1) * P), slice(n // TB * 512, n // TB * 512 + 512)
                    three(pe, ps[:, n % SB, :], KH[:, keys], KL[:, keys], QH[:, queries], QL[:, queries], True, True)\
                        .then_inc(s_psum, 1)

                for n in range(SB):
                    scores(n)
                for n in range(NS):
                    c, kk = n // TB, n % TB
                    if n + SB < NS:
                        scores(n + SB)
                    pe.wait_ge(a_split, NS * b + n + 1)
                    if c == 0:
                        pe.wait_ge(v_split, TB * b + kk + 1)
                    for e in range(2):
                        cols = slice(e * P, (e + 1) * P)
                        ins = three(pe, ps[:, 4 + 2 * c + e, :], VH[:, kk, cols], VL[:, kk, cols],
                                    AH[:, n % 4, :], AL[:, n % 4, :], kk == 0, kk == TB - 1)
                    ins.then_inc(av_psum, 1)
                    if n == TB + 1:
                        output(b, 0)
                if more:
                    pe.wait_ge(relu_done, NS * b + NS)
                    pe.wait_ge(out_added, 2 * b + 1 + 1)
                    turn(b + 1)
                output(b, 1)

            steps(pe, before, step)


CW = 256
CHUNKS = SLOTS // CW
EC = CW // NP_
GROUPS = SLOTS // P
AHEAD = 4
YW = D + 2


def soft_experts(nc, m, d):
    with ExitStack() as ctx:
        def sem(name):
            return ctx.enter_context(nc.semaphore("se_" + name))

        def sb(name, shape, dt=fp32):
            return ctx.enter_context(nc.sbuf_tensor("se_" + name, shape, dt))

        ps = m.ps
        loaded, w_loaded, filled = sem("loaded"), sem("w_loaded"), sem("filled")
        l_psum, shifted, exp_done, sum_done, inv_done = sem("l_psum"), sem("shifted"), sem("exp"), sem("sum"), sem("inv")
        disp_ready, slots_psum, slots_ready = sem("disp"), sem("slots_psum"), sem("slots_ready")
        y_psum, y_ready = sem("y_psum"), sem("y_ready")
        vec, pl, row_ready, row_psum = sem("vec"), sem("pool"), sem("row_ready"), sem("row_psum")
        row_copied, row_stored, row_spread = sem("row_copied"), sem("row_stored"), sem("row_spread")
        part1_tiles = ExitStack()

        def sb1(name, shape):
            return part1_tiles.enter_context(nc.sbuf_tensor("se_" + name, shape, fp32))

        PHI = m.PHI
        RM, RT = sb("rm", [P, B, TB]), sb("rt", [P, 2, B])
        RR = sb("rr", [B * TB, P])
        RB = sb("rb", [P, B * N])
        Y = sb("y", [P, GROUPS, B, YW])
        W = sb1("w", [P, EC, D])
        BIAS = sb1("bias", [P, GROUPS, D])
        M = sb1("m", [P, 2, CW])
        SU = sb1("su", [P, 2, 4, CW])
        SL = sb1("sl", [P, B, CW])
        row_dram = nc.dram_tensor("row_max", (B * TB, P), fp32).ap()

        def logits_of(s):
            return ps[:, 2 * s:2 * s + 2, :].rearrange("p k (h c) -> p (k h) c", h=2)

        EXH = [t[:, :, :, :].rearrange("p u t c -> p (u t c)").rearrange("p (s b c) -> p s b c", s=4, b=B)
               for t in (m.QU, m.VU)]

        def ex(t):
            return EXH[t % TB // 4][:, t % 4, :, :]

        slots_bank = ps[:, 4:6, :].rearrange("p k (h c) -> p (k h) c", h=2)

        def over_chunks(eng, chunk):
            chunk(0, True, False)
            with eng.Fori(0, CHUNKS - 2) as i:
                chunk(i + 1, False, False)
            chunk(CHUNKS - 1, False, True)

        part1 = nc.Block()
        block = part1.__enter__()

        @block.sync
        def _(sp):
            for q in range(4):
                sp.dma_start(BIAS[32 * q:32 * q + 32, :, :],
                             d.b.rearrange("(g q) e -> q g e", q=4)[q, :, :].partition_broadcast(32))\
                  .then_inc(loaded, 16)
            with sp.Fori(0, CHUNKS) as c:
                sp.wait_ge(y_psum, 2 * c + 1)
                sp.dma_start(W[:, :, :], d.w[bass.ds(c * EC, EC), :, :].rearrange("n d e -> d n e"))\
                  .then_inc(w_loaded, 16)

        @block.vector
        def _(v):
            prime(v, y_ready)
            v.memset(RM[:, :, :], -3.0e38)
            v.memset(Y[:, :, :, D:YW], 1.0).then_inc(filled, 1)
            v.wait_ge(filled, 1)

            def invert(c, t):
                v.wait_ge(sum_done, TB * c + t + 1)
                v.reciprocal(SU[:, 1, t % 4, :], SU[:, 0, t % 4, :]).then_inc(inv_done, 1)

            def add_bias(c, h):
                v.wait_ge(y_psum, 2 * c + h + 1 + 1)
                v.tensor_tensor(Y[:, bass.ds(2 * c + h, 1), :, 0:D].rearrange("p o b e -> p (o b) e"),
                                ps[:, 6 + h, :].rearrange("p (b e) -> p b e", b=B),
                                bc(BIAS[:, bass.ds(2 * c + h, 1), :], [P, B, D]), ALU.add).then_inc(y_ready, 1)

            def chunk(c, first, last):
                own = Own(v, vec, 2 * TB, c)
                for t in range(TB):
                    s = t % 2
                    v.wait_ge(l_psum, TB * c + t + 1)
                    L = logits_of(s)
                    own.mark(v.tensor_reduce(M[:, s, :], L.rearrange("p b c -> p c b"), AX.X, ALU.max))
                    own.mark(v.tensor_reduce(RT[:, s, :], L, AX.X, ALU.max))
                    if t >= 2 or not first:
                        invert(c, t - 2)
                    own.wait()
                    if not first:
                        v.wait_ge(slots_psum, TB * c + t - 7)
                    v.tensor_tensor(ex(t), L, bc(M[:, s, :].unsqueeze(1), [P, B, CW]), ALU.subtract)\
                     .then_inc(shifted, 1)
                    if not first:
                        v.wait_ge(row_ready, TB * c + t - 7)
                    v.tensor_tensor(RM[:, :, t], RM[:, :, t], RT[:, s, :], ALU.max).then_inc(row_ready, 1)
                    if t >= TB - 2 and not first:
                        add_bias(c - 1, t - (TB - 2))
                if first:
                    v.wait_ge(loaded, 4 * 16)
                if last:
                    invert(c, TB - 2)
                    invert(c, TB - 1)
                    add_bias(c, 0)
                    add_bias(c, 1)

            over_chunks(v, chunk)

        @block.scalar
        def _(act):
            prime(act, slots_ready)

            def copy_slots(c):
                act.wait_ge(slots_psum, TB * c + TB)
                act.activation(SL[:, :, :], slots_bank, ACT.Copy).then_inc(slots_ready, 1)

            def chunk(c, first, last):
                for t in range(TB):
                    if t == 3 and not first:
                        act.wait_ge(y_psum, 2 * c - 2 + 1)
                        copy_slots(c - 1)
                    act.wait_ge(shifted, TB * c + t + 1)
                    act.activation(ex(t), ex(t), ACT.Exp).then_inc(exp_done, 1)
                if last:
                    act.wait_ge(y_psum, 2 * c + 1)
                    copy_slots(c)

            over_chunks(act, chunk)
            act.wait_ge(row_psum, 1)
            act.activation(RR[:, :], ps[0:B * TB, 0, 0:P], ACT.Copy).then_inc(row_copied, 1)

        @block.gpsimd
        def _(pool):
            def add_up(own, c, t):
                s, e = t % 4, ex(t)
                pool.wait_ge(exp_done, TB * c + t + 1)
                own.step(pool.tensor_tensor(SU[:, 0, s, :], e[:, 0, :], e[:, 1, :], ALU.add))
                own.step(pool.tensor_tensor(SU[:, 0, s, :], SU[:, 0, s, :], e[:, 2, :], ALU.add))
                pool.tensor_tensor(SU[:, 0, s, :], SU[:, 0, s, :], e[:, 3, :], ALU.add).then_inc(sum_done, 1)

            def chunk(c, first, last):
                own = Own(pool, pl, 1, c * (2 * TB) + (0 if first else 2))
                if first:
                    add_up(own, c, 0)
                for t in range(TB):
                    if t + 1 < TB or not last:
                        add_up(own, c, t + 1)
                    pool.wait_ge(inv_done, TB * c + t + 1)
                    pool.tensor_tensor(ex(t), ex(t), bc(SU[:, 1, t % 4, :].unsqueeze(1), [P, B, CW]), ALU.mult)\
                        .then_inc(disp_ready, 1)

            over_chunks(pool, chunk)

        @block.tensor
        def _(pe):
            prime(pe, y_psum)
            pe.wait_ge(m.phi_loaded, 16)

            def logits(c, t):
                if not isinstance(c, int) or TB * c + t >= 2:
                    pe.wait_ge(shifted, TB * c + t - 1)
                for b in range(B):
                    at = b * N + (t % TB) * P
                    ins = pe.matmul(logits_of(t % 2)[:, b, :], m.XNT[:, at:at + P],
                                    PHI[:, bass.ds(c * CW + t // TB * CW, CW)], start=True, stop=True)
                ins.then_inc(l_psum, 1)

            def products(c, h):
                if h == 0:
                    pe.wait_ge(w_loaded, 16 * c + 16)
                    pe.wait_ge(y_ready, 2 * c + 1)
                for b in range(B):
                    for q in range(4):
                        n = 4 * h + q
                        ins = pe.matmul(ps[32 * q:32 * q + 32, 6 + h, b * D:(b + 1) * D],
                                        SL[:, b, n * NP_:(n + 1) * NP_], W[:, n, :], start=True, stop=True)
                ins.then_inc(y_psum, 1)

            def chunk(c, first, last):
                if first:
                    for t in range(AHEAD):
                        logits(c, t)
                for t in range(TB):
                    if t + AHEAD < TB or not last:
                        logits(c, t + AHEAD)
                    pe.wait_ge(disp_ready, TB * c + t + 1)
                    if t == 0 and not first:
                        pe.wait_ge(slots_ready, c + 1)
                    for b in range(B):
                        ins = pe.matmul(slots_bank[:, b, :], m.XN2[:, b * TB + t, :], ex(t)[:, b, :],
                                        start=t == 0 and b % 2 == 0, stop=t == TB - 1, skip_group_check=True)
                    ins.then_inc(slots_psum, 1)
                    if t in (1, 2) and not first:
                        products(c - 1, t - 1)
                if last:
                    pe.wait_ge(slots_ready, c + 1 + 1)
                    products(c, 0)
                    products(c, 1)

            over_chunks(pe, chunk)
            pe.wait_ge(row_ready, TB * CHUNKS)
            pe.wait_ge(y_ready, 2 * CHUNKS + 1)
            pe.transpose(ps[0:B * TB, 0, 0:P], RM[:, :, :].rearrange("p b t -> p (b t)"), m.ident[:, :])\
              .then_inc(row_psum, 1)
        part1.__exit__(None, None, None)
        part1_tiles.close()

        MC = B * N // 512
        l2_psum, shifted2, exp2_done = sem("l2_psum"), sem("shifted2"), sem("exp2")
        acc_psum, out_ready, stored = sem("acc_psum"), sem("out_ready"), sem("stored")
        SH, CT = sb("sh", [P, 2, 512]), sb("ct", [P, 4, 512])
        DEN = sb("den", [P, 2, 4])
        PH, PL = sb("ph", [P, SLOTS], f32r), sb("pl", [P, SLOTS], f32r)
        XH, XL = sb("xh", [P, 2, 512], f32r), sb("xl", [P, 2, 512], f32r)
        phi_rounded, phi_split, x_rounded, x_split = (sem(n) for n in ("phi_hi", "phi_lo", "x_hi", "x_lo"))
        block = ctx.enter_context(nc.Block())

        def acc(s, t):
            return ps[:, 4 + 2 * s + t // 2, (t % 2) * YW:(t % 2) * YW + YW]

        @block.sync
        def _(sp):
            sp.wait_ge(row_copied, 1)
            sp.dma_start(row_dram, RR[:, :]).then_inc(row_stored, 16)
            sp.wait_ge(row_stored, 16)
            sp.dma_start(RB[:, :], row_dram.rearrange("a p -> (a p)").partition_broadcast(P)).then_inc(row_spread, 16)
            with sp.Fori(0, MC) as c:
                sp.wait_ge(out_ready, c + 1 + 1)
                sp.dma_start(d.out[:, bass.ds(c * 4, 4), :], m.X[:, bass.ds(c * 4, 4), :]).then_inc(stored, 16)
            sp.wait_ge(stored, 16 * MC)

        @block.vector
        def _(v):
            prime(v, out_ready)
            for k in range(4):
                v.wait_ge(phi_rounded, k + 1)
                part = slice(k * 512, k * 512 + 512)
                v.tensor_tensor(PL[:, part], PHI[:, part], PH[:, part].bitcast(fp32), ALU.subtract)\
                 .then_inc(phi_split, 1)
            v.wait_ge(row_spread, 16)
            with v.Fori(0, MC // 2) as cp:
                own = Own(v, vec, 8, cp + CHUNKS * 2)
                for s in range(2):
                    c = cp * 2 + s
                    for n in range(GROUPS):
                        v.wait_ge(l2_psum, c * GROUPS + n + 1)
                        if n >= 2:
                            v.wait_ge(exp2_done, c * GROUPS + n - 1)
                        v.tensor_tensor(SH[:, n % 2, :], ps[:, n % 4, :], RB[:, bass.ds(c * 512, 512)],
                                        ALU.subtract).then_inc(shifted2, 1)
                    v.wait_ge(acc_psum, (c + 1) * GROUPS)
                    for t in range(4):
                        own.mark(v.reciprocal(DEN[:, s, t:t + 1], acc(s, t)[:, D:D + 1]))
                    own.wait()
                    for t in range(4):
                        tile = m.X[:, bass.ds(c * 4 + t, 1), :].rearrange("p o d -> p (o d)")
                        ins = v.scalar_tensor_tensor(tile, acc(s, t)[:, 0:D], DEN[:, s, t:t + 1], tile,
                                                     ALU.mult, ALU.add)
                    ins.then_inc(out_ready, 1)
                own.end()

        @block.gpsimd
        def _(pool):
            def split(c, s):
                tokens = m.XNT[:, bass.ds(c * 512, 512)]
                pool.tensor_copy(XH[:, s, :], tokens).then_inc(x_rounded, 1)
                pool.wait_ge(x_rounded, c + 1)
                hold(pool, m)
                pool.tensor_tensor(XL[:, s, :], tokens, XH[:, s, :].bitcast(fp32), ALU.subtract).then_inc(x_split, 1)

            split(0, 0)
            split(1, 1)
            with pool.Fori(0, MC // 2 - 1) as cp:
                for s in range(2):
                    pool.wait_ge(l2_psum, (cp * 2 + s + 1) * GROUPS)
                    hold(pool, m)
                    split(cp * 2 + s + 2, s)

        @block.scalar
        def _(act):
            for k in range(4):
                part = slice(k * 512, k * 512 + 512)
                act.activation(PH[:, part], PHI[:, part], ACT.Copy).then_inc(phi_rounded, 1)
            with act.Fori(0, MC) as c:
                for n in range(GROUPS):
                    act.wait_ge(shifted2, c * GROUPS + n + 1)
                    if n >= 4:
                        act.wait_ge(acc_psum, c * GROUPS + n - 3)
                    act.activation(CT[:, n % 4, :], SH[:, n % 2, :], ACT.Exp).then_inc(exp2_done, 1)

        @block.tensor
        def _(pe):
            pe.wait_ge(phi_split, 4)
            with pe.Fori(0, MC // 2) as cp:
                for s in range(2):
                    c = cp * 2 + s

                    def logits2(n):
                        if n >= 4:
                            pe.wait_ge(shifted2, c * GROUPS + n - 3)
                        at, out = slice(n * P, (n + 1) * P), ps[:, n % 4, :]
                        three(pe, out, PH[:, at], PL[:, at], XH[:, s, :], XL[:, s, :], True, True)\
                            .then_inc(l2_psum, 1)

                    pe.wait_ge(x_split, c + 1)
                    for n in range(3):
                        logits2(n)
                    pe.wait_ge(out_ready, cp * 2 + 1)
                    for n in range(GROUPS):
                        pe.wait_ge(exp2_done, c * GROUPS + n + 1)
                        for t in range(4):
                            ins = pe.matmul(acc(s, t), CT[:, n % 4, t * P:(t + 1) * P],
                                            Y[:, n, bass.ds(cp, 1), :]
                                            .rearrange("p o e -> p (o e)"),
                                            start=n == 0 and t % 2 == 0, stop=n == GROUPS - 1, skip_group_check=True)
                        ins.then_inc(acc_psum, 1)
                        if n + 3 < GROUPS:
                            logits2(n + 3)


class Names:
    pass


def memory(nc, ctx):
    m = Names()

    def sb(name, shape, dt=fp32):
        return ctx.enter_context(nc.sbuf_tensor(name, shape, dt))

    m.X = sb("X", [P, TILES, D])
    m.ident = sb("ident", [P, P])
    m.mask_q = sb("mask_q", [P, 512], bf16)
    m.lower, m.half = sb("lower", [P, E, E]), sb("half", [P, TILES])
    m.Wqkv, m.Wr = sb("Wqkv", [P, 3 * D]), sb("Wr", [P, E])
    m.router_b, m.qk_scale = sb("router_b", [P, E]), sb("qk_scale", [P, 2 * H])
    m.XNT = sb("XNT", [P, B * N])
    m.QU, m.KU, m.VU = (sb(n, [P, U, TB, 32]) for n in ("QU", "KU", "VU"))
    m.LG, m.GT = sb("LG", [P, TILES, E]), sb("GT", [P, TILES, E])
    m.XN2 = m.KU[:, :, :, :].rearrange("p u t c -> p (u t c)").rearrange("p (a d) -> p a d", d=D)
    m.gate_rows = nc.dram_tensor("gate_rows", (E, B * N), fp32).ap()
    m.Wo, m.b2, m.b1 = sb("Wo", [P, D]), sb("b2", [E, D]), sb("b1", [P, E, HC])
    m.WIN, m.BIN, m.BV = sb("win", [P, 5 * P]), sb("bin", [P, 5]), sb("bv", [P, E1])
    m.WOUT, m.BOUT, m.COL = sb("wout", [P, 2, D]), sb("bout", [P, D]), sb("col", [P, 6])
    m.late_loaded = ctx.enter_context(nc.semaphore("late_loaded"))
    m.ps = ctx.enter_context(nc.psum_tensor("ps", [P, 8, 512], fp32))
    m.held = ctx.enter_context(nc.semaphore("held"))
    m.rest_loaded = ctx.enter_context(nc.semaphore("rest_loaded"))
    m.loaded = ctx.enter_context(nc.semaphore("loaded"))
    return m


def declare(nc, inputs):
    import numpy as np
    arr = {}
    d = Names()

    def give(name, a):
        arr["in_" + name] = np.ascontiguousarray(a)
        return nc.dram_tensor("in_" + name, a.shape, mybir.dt.from_np(a.dtype), kind="ExternalInput").ap()

    d.x = give("x", inputs["L0_attn_x"])
    d.wqkv = give("wqkv", np.concatenate([inputs["L0_attn_W" + c].T for c in "qkv"], axis=1))
    d.router_w = give("router_w", inputs["L0_ffn_router_w"])
    d.router_b = give("router_b", inputs["L0_ffn_router_b"])
    d.q_scale = give("q_scale", inputs["L0_attn_q_scale"])
    d.k_scale = give("k_scale", inputs["L0_attn_k_scale"])
    d.wo = give("wo", inputs["L0_attn_Wo"].T)
    d.w1, d.b1 = give("w1", inputs["L0_ffn_w1"]), give("b1", inputs["L0_ffn_b1"].reshape(E, HC, P).transpose(2, 0, 1))
    d.w2, d.b2 = give("w2", inputs["L0_ffn_w2"]), give("b2", inputs["L0_ffn_b2"])
    d.columns = give("columns", np.stack([inputs["L1_attn_" + name] for name in (
        "ln_g", "ln_b", "gamma_q", "beta_q", "gamma_k", "beta_k")], axis=1))
    d.w_in, d.b_out = give("w_in", inputs["L1_attn_W_in"]), give("b_out", inputs["L1_attn_b_out"])
    d.b_in = give("b_in", inputs["L1_attn_b_in"].reshape(5, P).T)
    d.b_v = give("b_v", inputs["L1_attn_b_in"][E1:2 * E1])
    d.w_out = give("w_out", inputs["L1_attn_W_out"])
    d.phi = give("phi", inputs["L1_ffn_phi"].reshape(D, SLOTS))
    d.w, d.b = give("w", inputs["L1_ffn_W"]), give("b", inputs["L1_ffn_b"])
    d.out = nc.dram_tensor("out", (B, N, D), fp32, kind="ExternalOutput").ap()\
        .rearrange("b (t p) d -> p (b t) d", p=P)
    return arr, d


def parts(nc, m, d):
    setup(nc, m, d)
    project(nc, m)
    load_late(nc, m, d)
    attention(nc, m)
    with ExitStack() as part:
        m.XH, m.XL = (part.enter_context(nc.sbuf_tensor(name, [P, B * N], f32r)) for name in ("XH", "XL"))
        m.WR = m.KU[:, :, :, :].rearrange("p u t c -> p (u t c)")[:, 0:4 * HID].rearrange("p (w c) -> p w c", w=2)
        m.WH, m.WL = (part.enter_context(nc.sbuf_tensor(name, [P, 2, 2 * HID], f32r)) for name in ("WH", "WL"))
        m.w_loaded = [part.enter_context(nc.semaphore("w_loaded%d" % w)) for w in range(2)]
        m.w_rounded, m.w_split = (part.enter_context(nc.semaphore(name)) for name in ("w_rounded", "w_split"))
        mix_heads(nc, m, d)
        experts(nc, m, d)
    with ExitStack() as part:
        m.PHI = part.enter_context(nc.sbuf_tensor("PHI", [P, SLOTS], fp32))
        m.phi_loaded = part.enter_context(nc.semaphore("phi_loaded"))
        gated_attention(nc, m, d)
        soft_experts(nc, m, d)


def build(nc, d):
    with ExitStack() as ctx:
        parts(nc, memory(nc, ctx), d)


def kernel(**inputs):
    import numpy as np
    import concourse.bacc as bacc
    from concourse.bass_utils import run_bass_kernel_spmd

    nc = bacc.Bacc("TRN2", target_bir_lowering=False, num_devices=1)
    arrays, d = declare(nc, {name: np.asarray(a) for name, a in inputs.items()})
    build(nc, d)
    return run_bass_kernel_spmd(nc, [arrays], core_ids=[0]).results[0]["out"]
```
